# Optimizing a Trainium2 kernel written in Bass

```python
import numpy as np
import jax
import jax.numpy as jnp

def _softmax(x, axis=-1):
    return jax.nn.softmax(x, axis=axis)

def _gelu(x):
    return jax.nn.gelu(x, approximate=True)

def _silu(x):
    return jax.nn.silu(x)

def _sigmoid(x):
    return jax.nn.sigmoid(x)

def _layernorm(x, axis=-1, eps=1e-05):
    m = jnp.mean(x, axis=axis, keepdims=True)
    v = jnp.var(x, axis=axis, keepdims=True)
    return (x - m) / jnp.sqrt(v + eps)

def _scatter_add(tgt, idx, src, axis=0):
    return tgt.at[idx].add(src)

def _segment_sum(src, seg, n):
    return jax.ops.segment_sum(src, seg, n)
kernel_name = 'mk_macaron_d2_jaxref_r8_c3f962'

def setup_inputs(seed: int=0):
    np.random.seed(seed)
    _w = jnp.asarray

    def _L0_attn_setup():
        import jax, jax.numpy as jnp
        import numpy as np
        C_CONST = 8.0
        EPS = 1e-06
        K = 4

        def rmsnorm(x, w):
            var = jnp.mean(x * x, axis=-1, keepdims=True)
            return x * jax.lax.rsqrt(var + EPS) * w

        def causal_depthwise_conv(x, conv_w, conv_b):
            B, S, D = x.shape
            xp = jnp.pad(x, ((0, 0), (K - 1, 0), (0, 0)))
            out = conv_b
            for k in range(K):
                out = out + conv_w[k] * xp[:, k:k + S, :]
            return out

        def rg_lru(x, Wi, Wa, lam):
            r = jax.nn.sigmoid(jnp.einsum('bsd,de->bse', x, Wa))
            i = jax.nn.sigmoid(jnp.einsum('bsd,de->bse', x, Wi))
            log_a = -C_CONST * jax.nn.softplus(lam) * r
            a = jnp.exp(log_a)
            b = jnp.sqrt(jnp.maximum(1.0 - a * a, 1e-12)) * (i * x)

            def comb(e1, e2):
                a1, b1 = e1
                a2, b2 = e2
                return (a1 * a2, a2 * b1 + b2)
            _, h = jax.lax.associative_scan(comb, (a, b), axis=1)
            return h
        key = jax.random.key(seed)
        ks = jax.random.split(key, 16)
        B, S, D, H = (4, 256, 128, 512)
        s = 0.02
        return {'x': jax.random.normal(ks[0], (B, S, D), jnp.float32), 'norm1_w': jnp.ones((D,), jnp.float32), 'Wx': jax.random.normal(ks[1], (D, D), jnp.float32) * s, 'Wy': jax.random.normal(ks[2], (D, D), jnp.float32) * s, 'conv_w': jax.random.normal(ks[3], (K, D), jnp.float32) * s, 'conv_b': jnp.zeros((D,), jnp.float32), 'Wi': jax.random.normal(ks[4], (D, D), jnp.float32) * s, 'Wa': jax.random.normal(ks[5], (D, D), jnp.float32) * s, 'lam': jax.random.normal(ks[6], (D,), jnp.float32) * 0.5, 'Wo': jax.random.normal(ks[7], (D, D), jnp.float32) * s, 'norm2_w': jnp.ones((D,), jnp.float32), 'Wg': jax.random.normal(ks[8], (D, H), jnp.float32) * s, 'Wu': jax.random.normal(ks[9], (D, H), jnp.float32) * s, 'Wd': jax.random.normal(ks[10], (H, D), jnp.float32) * s}
    _L0_attn_in = _L0_attn_setup()

    def _L0_ffn_setup():
        import jax, jax.numpy as jnp
        import numpy as np
        B, S, IN, OUT = (4, 1024, 128, 128)
        EPS = 1e-06

        def _xla_quantized_matmul(x2d, weight_q, weight_scale):
            amax = jnp.max(jnp.abs(x2d), axis=-1, keepdims=True)
            x_scale = jnp.maximum(amax, EPS) / 127.0
            x_q = jnp.clip(jnp.round(x2d / x_scale), -128, 127).astype(jnp.int8)
            acc = jax.lax.dot_general(x_q, weight_q, (((1,), (1,)), ((), ())), preferred_element_type=jnp.int32)
            return acc.astype(jnp.float32) * x_scale * weight_scale[None, :]
        key = jax.random.key(seed)
        k1, k2, k3, k4 = jax.random.split(key, 4)
        x = jax.random.normal(k1, (B, S, IN), dtype=jnp.float32)
        weight_q = jax.random.randint(k2, (OUT, IN), -128, 128, dtype=jnp.int32).astype(jnp.int8)
        weight_scale = jax.random.uniform(k3, (OUT,), dtype=jnp.float32, minval=0.001, maxval=0.01)
        bias = jax.random.normal(k4, (OUT,), dtype=jnp.float32) * 0.01
        return {'x': x, 'weight_q': weight_q, 'weight_scale': weight_scale, 'bias': bias}
    _L0_ffn_in = _L0_ffn_setup()

    def _L1_attn_setup():
        import jax, jax.numpy as jnp
        import numpy as np
        B, T, H = (8, 256, 128)
        K, V, O = (128, 128, 128)

        def _reference_tuple_inner(hidden_state, Wq, bq, Wk, bk, Wv, bv, Wg, bg, Wo, bo):
            q = hidden_state @ Wq + bq
            k = jax.nn.sigmoid(hidden_state @ Wk + bk)
            g = jax.nn.sigmoid(hidden_state @ Wg + bg)
            v = hidden_state @ Wv + bv
            Bn = hidden_state.shape[0]
            Kd, Vd = (Wk.shape[1], Wv.shape[1])

            def step(state, xs):
                qi, ki, vi, gi = xs
                state = state * gi[:, :, None] + ki[:, :, None] * vi[:, None, :]
                oi = jnp.einsum('bk,bkv->bv', qi, state)
                return (state, oi)
            init = jnp.zeros((Bn, Kd, Vd), hidden_state.dtype)
            xs = (jnp.swapaxes(q, 0, 1), jnp.swapaxes(k, 0, 1), jnp.swapaxes(v, 0, 1), jnp.swapaxes(g, 0, 1))
            state, outs = jax.lax.scan(step, init, xs)
            out = jnp.swapaxes(outs, 0, 1) @ Wo + bo
            return (out, state)
        key = jax.random.key(seed)
        ks = jax.random.split(key, 12)
        s = 0.02
        return {'hidden_state': jax.random.normal(ks[0], (B, T, H), jnp.float32), 'Wq': jax.random.normal(ks[1], (H, H), jnp.float32) * s, 'bq': jax.random.normal(ks[2], (H,), jnp.float32) * s, 'Wk': jax.random.normal(ks[3], (H, K), jnp.float32) * s, 'bk': jax.random.normal(ks[4], (K,), jnp.float32) * s, 'Wv': jax.random.normal(ks[5], (H, V), jnp.float32) * s, 'bv': jax.random.normal(ks[6], (V,), jnp.float32) * s, 'Wg': jax.random.normal(ks[7], (H, K), jnp.float32) * s, 'bg': jax.random.normal(ks[8], (K,), jnp.float32) * s, 'Wo': jax.random.normal(ks[9], (V, O), jnp.float32) * s, 'bo': jax.random.normal(ks[10], (O,), jnp.float32) * s}
    _L1_attn_in = _L1_attn_setup()

    def _L1_ffn_setup():
        import jax, jax.numpy as jnp
        import numpy as np
        B, S, H, I, E_ROUTED, TOP_K = (8, 256, 128, 256, 8, 2)

        def _expert(x, Wg, Wu, Wd):
            return jax.nn.silu(x @ Wg.T) * (x @ Wu.T) @ Wd.T
        key = jax.random.key(seed)
        ks = jax.random.split(key, 9)
        s = 0.02
        return {'x': jax.random.normal(ks[0], (B, S, H), dtype=jnp.float32), 'Wg_s': jax.random.normal(ks[1], (I, H), dtype=jnp.float32) * s, 'Wu_s': jax.random.normal(ks[2], (I, H), dtype=jnp.float32) * s, 'Wd_s': jax.random.normal(ks[3], (H, I), dtype=jnp.float32) * s, 'Wg': jax.random.normal(ks[4], (E_ROUTED, I, H), dtype=jnp.float32) * s, 'Wu': jax.random.normal(ks[5], (E_ROUTED, I, H), dtype=jnp.float32) * s, 'Wd': jax.random.normal(ks[6], (E_ROUTED, H, I), dtype=jnp.float32) * s, 'Wr': jax.random.normal(ks[7], (E_ROUTED, H), dtype=jnp.float32) * s, 'rb': jnp.zeros((E_ROUTED,), dtype=jnp.float32)}
    _L1_ffn_in = _L1_ffn_setup()
    _d = {'L0_attn_x': _L0_attn_in['x'], 'L0_attn_norm1_w': _L0_attn_in['norm1_w'], 'L0_attn_Wx': _L0_attn_in['Wx'], 'L0_attn_Wy': _L0_attn_in['Wy'], 'L0_attn_conv_w': _L0_attn_in['conv_w'], 'L0_attn_conv_b': _L0_attn_in['conv_b'], 'L0_attn_Wi': _L0_attn_in['Wi'], 'L0_attn_Wa': _L0_attn_in['Wa'], 'L0_attn_lam': _L0_attn_in['lam'], 'L0_attn_Wo': _L0_attn_in['Wo'], 'L0_attn_norm2_w': _L0_attn_in['norm2_w'], 'L0_attn_Wg': _L0_attn_in['Wg'], 'L0_attn_Wu': _L0_attn_in['Wu'], 'L0_attn_Wd': _L0_attn_in['Wd'], 'L0_ffn_weight_q': _L0_ffn_in['weight_q'], 'L0_ffn_weight_scale': _L0_ffn_in['weight_scale'], 'L0_ffn_bias': _L0_ffn_in['bias'], 'L1_attn_Wq': _L1_attn_in['Wq'], 'L1_attn_bq': _L1_attn_in['bq'], 'L1_attn_Wk': _L1_attn_in['Wk'], 'L1_attn_bk': _L1_attn_in['bk'], 'L1_attn_Wv': _L1_attn_in['Wv'], 'L1_attn_bv': _L1_attn_in['bv'], 'L1_attn_Wg': _L1_attn_in['Wg'], 'L1_attn_bg': _L1_attn_in['bg'], 'L1_attn_Wo': _L1_attn_in['Wo'], 'L1_attn_bo': _L1_attn_in['bo'], 'L1_ffn_Wg_s': _L1_ffn_in['Wg_s'], 'L1_ffn_Wu_s': _L1_ffn_in['Wu_s'], 'L1_ffn_Wd_s': _L1_ffn_in['Wd_s'], 'L1_ffn_Wg': _L1_ffn_in['Wg'], 'L1_ffn_Wu': _L1_ffn_in['Wu'], 'L1_ffn_Wd': _L1_ffn_in['Wd'], 'L1_ffn_Wr': _L1_ffn_in['Wr'], 'L1_ffn_rb': _L1_ffn_in['rb']}
    _x0 = _d['L0_attn_x']
    _d['L0_attn_x'] = jax.random.normal(jax.random.fold_in(jax.random.key(seed), 1), (16, 256, 128), dtype=_x0.dtype)
    del _x0
    return _d

def reference(L0_attn_x, L0_attn_norm1_w, L0_attn_Wx, L0_attn_Wy, L0_attn_conv_w, L0_attn_conv_b, L0_attn_Wi, L0_attn_Wa, L0_attn_lam, L0_attn_Wo, L0_attn_norm2_w, L0_attn_Wg, L0_attn_Wu, L0_attn_Wd, L0_ffn_weight_q, L0_ffn_weight_scale, L0_ffn_bias, L1_attn_Wq, L1_attn_bq, L1_attn_Wk, L1_attn_bk, L1_attn_Wv, L1_attn_bv, L1_attn_Wg, L1_attn_bg, L1_attn_Wo, L1_attn_bo, L1_ffn_Wg_s, L1_ffn_Wu_s, L1_ffn_Wd_s, L1_ffn_Wg, L1_ffn_Wu, L1_ffn_Wd, L1_ffn_Wr, L1_ffn_rb):

    def _L0_attn_ref(x, norm1_w, Wx, Wy, conv_w, conv_b, Wi, Wa, lam, Wo, norm2_w, Wg, Wu, Wd):
        import jax, jax.numpy as jnp
        import numpy as np
        C_CONST = 8.0
        EPS = 1e-06
        K = 4

        def rmsnorm(x, w):
            var = jnp.mean(x * x, axis=-1, keepdims=True)
            return x * jax.lax.rsqrt(var + EPS) * w

        def causal_depthwise_conv(x, conv_w, conv_b):
            B, S, D = x.shape
            xp = jnp.pad(x, ((0, 0), (K - 1, 0), (0, 0)))
            out = conv_b
            for k in range(K):
                out = out + conv_w[k] * xp[:, k:k + S, :]
            return out

        def rg_lru(x, Wi, Wa, lam):
            r = jax.nn.sigmoid(jnp.einsum('bsd,de->bse', x, Wa))
            i = jax.nn.sigmoid(jnp.einsum('bsd,de->bse', x, Wi))
            log_a = -C_CONST * jax.nn.softplus(lam) * r
            a = jnp.exp(log_a)
            b = jnp.sqrt(jnp.maximum(1.0 - a * a, 1e-12)) * (i * x)

            def comb(e1, e2):
                a1, b1 = e1
                a2, b2 = e2
                return (a1 * a2, a2 * b1 + b2)
            _, h = jax.lax.associative_scan(comb, (a, b), axis=1)
            return h
        t = rmsnorm(x, norm1_w)
        xb = jnp.einsum('bsd,de->bse', t, Wx)
        xb = causal_depthwise_conv(xb, conv_w, conv_b)
        h = rg_lru(xb, Wi, Wa, lam)
        yb = jax.nn.gelu(jnp.einsum('bsd,de->bse', t, Wy))
        mix = jnp.einsum('bsd,de->bse', h * yb, Wo)
        h1 = x + mix
        u = rmsnorm(h1, norm2_w)
        ffn = jnp.einsum('bsh,hd->bsd', jax.nn.gelu(jnp.einsum('bsd,dh->bsh', u, Wg)) * jnp.einsum('bsd,dh->bsh', u, Wu), Wd)
        return h1 + ffn

    def _L0_ffn_ref(x, weight_q, weight_scale, bias):
        import jax, jax.numpy as jnp
        import numpy as np
        B, S, IN, OUT = (4, 1024, 128, 128)
        EPS = 1e-06

        def _xla_quantized_matmul(x2d, weight_q, weight_scale):
            amax = jnp.max(jnp.abs(x2d), axis=-1, keepdims=True)
            x_scale = jnp.maximum(amax, EPS) / 127.0
            x_q = jnp.clip(jnp.round(x2d / x_scale), -128, 127).astype(jnp.int8)
            acc = jax.lax.dot_general(x_q, weight_q, (((1,), (1,)), ((), ())), preferred_element_type=jnp.int32)
            return acc.astype(jnp.float32) * x_scale * weight_scale[None, :]
        orig_shape = x.shape
        x2d = x.reshape(-1, orig_shape[-1])
        out = _xla_quantized_matmul(x2d, weight_q, weight_scale)
        out = out.reshape(*orig_shape[:-1], out.shape[-1])
        out = out + bias
        return out

    def _L1_attn_ref(hidden_state, Wq, bq, Wk, bk, Wv, bv, Wg, bg, Wo, bo):
        import jax, jax.numpy as jnp
        import numpy as np
        B, T, H = (8, 256, 128)
        K, V, O = (128, 128, 128)

        def _reference_tuple_inner(hidden_state, Wq, bq, Wk, bk, Wv, bv, Wg, bg, Wo, bo):
            q = hidden_state @ Wq + bq
            k = jax.nn.sigmoid(hidden_state @ Wk + bk)
            g = jax.nn.sigmoid(hidden_state @ Wg + bg)
            v = hidden_state @ Wv + bv
            Bn = hidden_state.shape[0]
            Kd, Vd = (Wk.shape[1], Wv.shape[1])

            def step(state, xs):
                qi, ki, vi, gi = xs
                state = state * gi[:, :, None] + ki[:, :, None] * vi[:, None, :]
                oi = jnp.einsum('bk,bkv->bv', qi, state)
                return (state, oi)
            init = jnp.zeros((Bn, Kd, Vd), hidden_state.dtype)
            xs = (jnp.swapaxes(q, 0, 1), jnp.swapaxes(k, 0, 1), jnp.swapaxes(v, 0, 1), jnp.swapaxes(g, 0, 1))
            state, outs = jax.lax.scan(step, init, xs)
            out = jnp.swapaxes(outs, 0, 1) @ Wo + bo
            return (out, state)
        return _reference_tuple_inner(hidden_state, Wq, bq, Wk, bk, Wv, bv, Wg, bg, Wo, bo)[0]

    def _L1_ffn_ref(x, Wg_s, Wu_s, Wd_s, Wg, Wu, Wd, Wr, rb):
        import jax, jax.numpy as jnp
        import numpy as np
        B, S, H, I, E_ROUTED, TOP_K = (8, 256, 128, 256, 8, 2)

        def _expert(x, Wg, Wu, Wd):
            return jax.nn.silu(x @ Wg.T) * (x @ Wu.T) @ Wd.T
        shared = _expert(x, Wg_s, Wu_s, Wd_s)
        logits = jnp.einsum('bsh,eh->bse', x, Wr) + rb
        probs = jax.nn.sigmoid(logits)
        scores, idx = jax.lax.top_k(probs, TOP_K)
        cw = (jax.nn.one_hot(idx, E_ROUTED, dtype=x.dtype) * scores[..., None]).sum(-2)
        out = shared
        for e in range(E_ROUTED):
            out = out + cw[..., e:e + 1] * _expert(x, Wg[e], Wu[e], Wd[e])
        return out
    x = L0_attn_x
    x = x + 0.5 * _L0_ffn_ref(_layernorm(x, axis=-1), L0_ffn_weight_q, L0_ffn_weight_scale, L0_ffn_bias)
    x = x + _L0_attn_ref(_layernorm(x, axis=-1), L0_attn_norm1_w, L0_attn_Wx, L0_attn_Wy, L0_attn_conv_w, L0_attn_conv_b, L0_attn_Wi, L0_attn_Wa, L0_attn_lam, L0_attn_Wo, L0_attn_norm2_w, L0_attn_Wg, L0_attn_Wu, L0_attn_Wd)
    x = x + 0.5 * _L0_ffn_ref(_layernorm(x, axis=-1), L0_ffn_weight_q, L0_ffn_weight_scale, L0_ffn_bias)
    x = x + 0.5 * _L1_ffn_ref(_layernorm(x, axis=-1), L1_ffn_Wg_s, L1_ffn_Wu_s, L1_ffn_Wd_s, L1_ffn_Wg, L1_ffn_Wu, L1_ffn_Wd, L1_ffn_Wr, L1_ffn_rb)
    x = x + _L1_attn_ref(_layernorm(x, axis=-1), L1_attn_Wq, L1_attn_bq, L1_attn_Wk, L1_attn_bk, L1_attn_Wv, L1_attn_bv, L1_attn_Wg, L1_attn_bg, L1_attn_Wo, L1_attn_bo)
    x = x + 0.5 * _L1_ffn_ref(_layernorm(x, axis=-1), L1_ffn_Wg_s, L1_ffn_Wu_s, L1_ffn_Wd_s, L1_ffn_Wg, L1_ffn_Wu, L1_ffn_Wd, L1_ffn_Wr, L1_ffn_rb)
    return x

_drawn_inputs = setup_inputs


def setup_inputs(seed=0):
    import zlib

    import numpy as np

    out = dict(_drawn_inputs(seed))
    spreads = {'L0_attn_norm1_w': (1.0, 0.6),
     'L0_attn_conv_b': (0.0, 0.8),
     'L0_attn_norm2_w': (1.0, 0.6),
     'L1_ffn_rb': (0.0, 0.8)}
    factors = {'L0_attn_Wx': 8.0,
     'L0_attn_Wy': 8.0,
     'L0_attn_conv_w': 8.0,
     'L0_attn_Wi': 8.0,
     'L0_attn_Wa': 8.0,
     'L0_attn_lam': 8.0,
     'L0_attn_Wo': 8.0,
     'L0_attn_Wg': 8.0,
     'L0_attn_Wu': 8.0,
     'L0_attn_Wd': 8.0,
     'L0_ffn_bias': 8.0,
     'L1_attn_Wq': 4.012,
     'L1_attn_bq': 8.0,
     'L1_attn_Wk': 8.0,
     'L1_attn_bk': 8.0,
     'L1_attn_Wv': 4.148,
     'L1_attn_bv': 8.0,
     'L1_attn_Wg': 8.0,
     'L1_attn_bg': 8.0,
     'L1_attn_Wo': 4.111,
     'L1_attn_bo': 30.663,
     'L1_ffn_Wg_s': 8.0,
     'L1_ffn_Wu_s': 8.0,
     'L1_ffn_Wd_s': 8.0,
     'L1_ffn_Wg': 8.0,
     'L1_ffn_Wu': 8.0,
     'L1_ffn_Wd': 8.0,
     'L1_ffn_Wr': 8.0}
    for name, (base, spread) in spreads.items():
        noise = np.random.default_rng([zlib.crc32(name.encode()), seed]).standard_normal(out[name].shape)
        drawn = base * np.exp(spread * noise) if base else spread * noise
        out[name] = jnp.asarray(drawn.astype(out[name].dtype))
    for name, factor in factors.items():
        out[name] = (out[name] * factor).astype(out[name].dtype)
    return out
```

```python
from contextlib import ExitStack

import concourse.bass as bass
from concourse import mybir

ALU = mybir.AluOpType
ACT = mybir.ActivationFunctionType
AX = mybir.AxisListType
F32 = mybir.dt.float32
BF16 = mybir.dt.bfloat16
I32 = mybir.dt.int32

P = 128
B, S, D = 16, 256, 128
TOKENS = B * S
GROUP = 512
TILES = GROUP // P
GROUPS = TOKENS // GROUP
PAIRS = GROUPS // 2
SEQS = GROUP // S
HID = 512
HJ = HID // P
TAPS = 4
PAD = TAPS - 1
E_ROUTED, E_ALL, INNER = 8, 9, 256
IJ = INNER // P
LEVELS = 7
LN_EPS, RMS_EPS, Q_EPS = 1e-5, 1e-6, 1e-6
MAGIC = 1.5 * 2.0 ** 23
C_CONST = 8.0

N1W, CW0, CB, LAM, N2W, BQ, BK, BG = 0, 1, 5, 6, 7, 8, 9, 10
NCOLS = 11
R_WS, R_QB, R_BV, R_BO, R_RB = 0, P, 2 * P, 3 * P, 4 * P
NROWS = 4 * P + E_ROUTED


def macaron_kernel(nc, x_in, wq64, cols_in, rows_in, l0_sq, l0_gu, l0_dn, l1_sq, moe_gu, moe_dn, moe_r,
                   ident_in, masks_in, lower_in, out):
    with ExitStack() as ctx:
        def sb(name, shape, dt=F32):
            return ctx.enter_context(nc.sbuf_tensor(name, shape, dt))

        def sem(name):
            return ctx.enter_context(nc.semaphore(name))

        x = sb("x", [P, PAIRS, 2, GROUP])
        xt_all = sb("xt_all", [P, PAIRS, 2, GROUP])
        cw = sb("cw", [P, PAIRS, 2, TILES * E_ALL])
        wq_int = sb("wq_int", [P, P, 2], I32)
        wq = sb("wq", [P, P], BF16)
        cols = sb("cols", [P, NCOLS])
        rows = sb("rows", [P, NROWS])
        w_sq = sb("w_sq", [P, 5, P])
        w_gu = sb("w_gu", [P, 2, HID])
        w_dn = sb("w_dn", [P, HJ, P])
        a_sq = sb("a_sq", [P, 5, P])
        e_gu = sb("e_gu", [P, E_ALL, 2, INNER])
        e_dn = sb("e_dn", [P, E_ALL, IJ, P])
        w_r = sb("w_r", [P, E_ROUTED])
        ident = sb("ident", [P, P])
        ident_bf = sb("ident_bf", [P, P], BF16)
        masks = sb("masks", [P, (LEVELS - 1) * 256 + GROUP], I32)
        lower = sb("lower", [P, E_ROUTED, E_ROUTED])
        neg_half = sb("neg_half", [P, TILES])
        ln_eps = sb("ln_eps", [P, TILES])
        rms_eps = sb("rms_eps", [P, TILES])
        wx_n = sb("wx_n", [P, 2, P])
        wgu_n = sb("wgu_n", [P, 2, HID])
        half_ws = sb("half_ws", [P, TILES, P])
        half_qb = sb("half_qb", [P, TILES, P])
        sp = sb("sp", [P, 4])
        decay = sb("decay", [P, 1])

        def two(name, shape, dt=F32):
            return [sb(f"{name}{h}", shape, dt) for h in range(2)]

        stats = two("stats", [P, TILES, 6])
        msum = two("msum", [P, TILES])
        mdif = two("mdif", [P, TILES])
        m2 = two("m2", [P, TILES])
        mean = two("mean", [P, TILES])
        var = two("var", [P, TILES])
        ve = two("ve", [P, TILES])
        rstd = two("rstd", [P, TILES])
        xn = two("xn", [P, TILES, P])
        xt = two("xt", [P, GROUP])
        amax = two("amax", [P, TILES])
        qs = two("qs", [P, TILES])
        qinv = two("qinv", [P, TILES])
        qt = two("qt", [P, TILES, P])
        qi = two("qi", [P, TILES, P], BF16)
        qit = two("qit", [P, GROUP], BF16)
        r2 = two("r2", [P, TILES])
        tt = two("tt", [P, TILES, P])
        xp = two("xp", [P, SEQS, PAD + S])
        xc = two("xc", [P, SEQS, S])
        bufA = two("bufA", [P, GROUP])
        bufB = two("bufB", [P, GROUP])
        bufC = two("bufC", [P, GROUP])
        bufD = two("bufD", [P, GROUP])
        bufE = two("bufE", [P, GROUP])
        h1 = two("h1", [P, TILES, P])
        ss = two("ss", [P, TILES])
        gate = two("gate", [P, HJ, GROUP])
        hid = two("hid", [P, HJ, GROUP])
        at = two("at", [P, GROUP])
        across = two("across", [P, SEQS, P])
        tseg = two("tseg", [P, GROUP])
        tseg2 = two("tseg2", [P, GROUP // 2])
        probs = two("probs", [P, TILES, E_ROUTED])
        gt = two("gt", [P, TILES, E_ROUTED, E_ROUTED])
        eq = two("eq", [P, TILES, E_ROUTED, E_ROUTED])
        rank = two("rank", [P, TILES, E_ROUTED])
        sg = two("sg", [P, GROUP])
        eh = [[sb(f"eh{a}{j}", [P, GROUP]) for j in range(IJ)] for a in range(2)]

        bank = [ctx.enter_context(nc.psum_tensor(f"bank{i}", [P, GROUP], F32)) for i in range(8)]

        def pb(h, k):
            return bank[4 * h + k]

        s_load = sem("s_load")
        s_load2 = sem("s_load2")
        s_act_sp = sem("s_act_sp")
        s_const = sem("s_const")
        s_pool_const = sem("s_pool_const")
        s_act_const = sem("s_act_const")
        s_stats = sem("s_stats")
        s_mom = sem("s_mom"); s_mean = sem("s_mean")
        s_mv = sem("s_mv")
        s_ve = sem("s_ve")
        s_rstd = sem("s_rstd")
        s_xn = sem("s_xn")
        s_x = sem("s_x")
        s_xtr = sem("s_xtr")
        s_xt = sem("s_xt")
        s_amax = sem("s_amax"); s_qs = sem("s_qs"); s_qinv = sem("s_qinv"); s_qmul = sem("s_qmul")
        s_qclip = sem("s_qclip"); s_qi = sem("s_qi"); s_qtr = sem("s_qtr"); s_qit = sem("s_qit")
        s_qy = sem("s_qy"); s_qz = sem("s_qz"); s_qxb = sem("s_qxb")
        s_xb = sem("s_xb"); s_xp = sem("s_xp"); s_r2a = sem("s_r2a"); s_r2b = sem("s_r2b"); s_r2 = sem("s_r2")
        s_t = sem("s_t"); s_ttr = sem("s_ttr"); s_tx = sem("s_tx")
        s_conv = sem("s_conv"); s_y = sem("s_y"); s_gates = sem("s_gates"); s_sig = sem("s_sig")
        s_a = sem("s_a"); s_a2 = sem("s_a2"); s_om = sem("s_om"); s_sq = sem("s_sq"); s_ix = sem("s_ix")
        s_b = sem("s_b"); s_scan = sem("s_scan"); s_yb = sem("s_yb"); s_hy = sem("s_hy")
        s_mix = sem("s_mix"); s_h1 = sem("s_h1"); s_ss = sem("s_ss"); s_s2a = sem("s_s2a"); s_s2 = sem("s_s2")
        s_u = sem("s_u"); s_utr = sem("s_utr"); s_ut = sem("s_ut"); s_fg = sem("s_fg"); s_fu = sem("s_fu")
        s_gelu = sem("s_gelu"); s_hid = sem("s_hid"); s_ffn = sem("s_ffn"); s_xh = sem("s_xh")
        s_qkg = sem("s_qkg"); s_v = sem("s_v"); s_qk = sem("s_qk"); s_vb = sem("s_vb")
        s_q0 = sem("s_q0"); s_lvl = sem("s_lvl"); s_upd = sem("s_upd")
        s_pred = sem("s_pred"); s_cross = sem("s_cross"); s_cc = sem("s_cc"); s_o = sem("s_o")
        s_oc = sem("s_oc"); s_op = sem("s_op"); s_xbo = sem("s_xbo"); s_dg = sem("s_dg")
        s_xta = sem("s_xta"); s_rl = sem("s_rl"); s_rlb = sem("s_rlb"); s_pr = sem("s_pr"); s_cmp = sem("s_cmp")
        s_cml = sem("s_cml"); s_cms = sem("s_cms"); s_rank = sem("s_rank"); s_rk2 = sem("s_rk2")
        s_cw = sem("s_cw")
        s_eg = sem("s_eg"); s_eu = sem("s_eu")
        s_silu = sem("s_silu"); s_eh = sem("s_eh"); s_ed = sem("s_ed"); s_acc = sem("s_acc")
        s_out = sem("s_out")

        LOADS = 14

        def xg(i, h):
            return x[:, i, h, :].rearrange("p (t d) -> p t d", t=TILES)

        def seqs(buf):
            return buf[:, :].rearrange("p (b s) -> p b s", b=SEQS)

        def n(i, h, ph=0):
            return 2 * i + (h + 1 + GROUPS * ph)

        def tile_mm(pe, ps, lhs, rhs, w=P):
            for t in range(TILES):
                m = pe.matmul(ps[:, t * w:(t + 1) * w], lhs[:, t * P:(t + 1) * P], rhs, start=True, stop=True)
            return m

        def transposes(pe, ps, src, idn):
            for t in range(TILES):
                m = pe.transpose(ps[:, t * P:(t + 1) * P], src[:, t, :], idn)
            return m

        def ln_vector(dve, i, ph):
            for h in range(2):
                if ph:
                    dve.wait_ge(s_x, n(i, h, ph - 1))
                for t in range(TILES):
                    m = dve.bn_stats(stats[h][:, t, :], xg(i, h)[:, t, :])
                m.then_inc(s_stats, 1)
            for h in range(2):
                dve.wait_ge(s_stats, n(i, h, ph))
                dve.tensor_tensor(msum[h][:, :], stats[h][:, :, 1], stats[h][:, :, 4], ALU.add)
                dve.tensor_tensor(mdif[h][:, :], stats[h][:, :, 1], stats[h][:, :, 4], ALU.subtract)
                dve.tensor_tensor(m2[h][:, :], stats[h][:, :, 2], stats[h][:, :, 5], ALU.add).then_inc(s_mom, 1)
            for h in range(2):
                dve.wait_ge(s_mom, n(i, h, ph))
                dve.tensor_scalar(mean[h][:, :], msum[h][:, :], 0.5, None, ALU.mult)
                dve.scalar_tensor_tensor(out=mdif[h][:, :], in0=mdif[h][:, :], scalar=0.25, in1=mdif[h][:, :],
                                         op0=ALU.mult, op1=ALU.mult).then_inc(s_mean, 1)
            for h in range(2):
                dve.wait_ge(s_mean, n(i, h, ph))
                dve.scalar_tensor_tensor(out=var[h][:, :], in0=m2[h][:, :], scalar=1.0 / D, in1=mdif[h][:, :],
                                         op0=ALU.mult, op1=ALU.add).then_inc(s_mv, 1)
            for h in range(2):
                dve.wait_ge(s_rstd, n(i, h, ph))
                for t in range(TILES):
                    m = dve.tensor_scalar(xn[h][:, t, :], xg(i, h)[:, t, :], mean[h][:, t:t + 1],
                                          rstd[h][:, t:t + 1], ALU.subtract, ALU.mult)
                m.then_inc(s_xn, 1)

        def ln_gpsimd(pool, i, ph):
            for h in range(2):
                pool.wait_ge(s_mv, n(i, h, ph))
                pool.tensor_tensor(ve[h][:, :], var[h][:, :], ln_eps[:, :], ALU.add).then_inc(s_ve, 1)
                pool.wait_ge(s_ve, n(i, h, ph))
                pool.tensor_tensor(rstd[h][:, :], ve[h][:, :], neg_half[:, :], ALU.pow).then_inc(s_rstd, 1)

        def xt_tensor(pe, i, ph, k):
            for h in range(2):
                pe.wait_ge(s_xn, n(i, h, ph))
                transposes(pe, pb(h, 0), xn[h], ident[:, :]).then_inc(s_xtr, 1)

        def xt_scalar(act, i, k):
            for h in range(2):
                act.wait_ge(s_xtr, n(i, h, k))
                act.activation(xt[h][:, :], pb(h, 0)[:, :], ACT.Copy).then_inc(s_xt, 1)

        block = ctx.enter_context(nc.Block())

        @block.sync
        def _(sp_):
            for g in range(PAIRS):
                sp_.dma_start(x[:, g, :, :], x_in[:, g, :, :]).then_inc(s_load, 16)
            for dst, src in ((cols, cols_in), (rows, rows_in), (ident, ident_in),
                             (masks, masks_in)):
                sp_.dma_start(dst[:, :], src).then_inc(s_load, 16)
            sp_.dma_start(wq_int[:, :, :], wq64.bitcast(I32).rearrange("p (n w) -> p n w", w=2)).then_inc(s_load, 16)
            sp_.dma_start(lower[:, :, :], lower_in).then_inc(s_load, 16)
            sp_.dma_start(w_sq[:, :, :], l0_sq).then_inc(s_load, 16)
            sp_.dma_start(w_gu[:, :, :], l0_gu).then_inc(s_load, 16)
            sp_.dma_start(w_dn[:, :, :], l0_dn).then_inc(s_load, 16)
            sp_.dma_start(w_r[:, :], moe_r).then_inc(s_load, 16)
            sp_.dma_start(a_sq[:, :, :], l1_sq).then_inc(s_load2, 16)
            sp_.dma_start(e_gu[:, :, :, :], moe_gu).then_inc(s_load2, 16)
            sp_.dma_start(e_dn[:, :, :, :], moe_dn).then_inc(s_load2, 16)
            sp_.wait_ge(s_x, GROUPS * 6)
            sp_.dma_start(out, x[:, :, :, :]).then_inc(s_out, 16)
            sp_.wait_ge(s_out, 16)

        def quant_vector(dve, i, p, ph):
            ln_vector(dve, i, ph)
            for h in range(2):
                dve.wait_ge(s_xn, n(i, h, ph))
                dve.tensor_reduce(amax[h][:, :], xn[h][:, :, :], AX.X, ALU.max,
                                  apply_absolute_value=True).then_inc(s_amax, 1)
            for h in range(2):
                dve.wait_ge(s_amax, n(i, h, p))
                dve.tensor_scalar(qs[h][:, :], amax[h][:, :], Q_EPS, 1.0 / 127.0, ALU.max, ALU.mult).then_inc(s_qs, 1)
            for h in range(2):
                dve.wait_ge(s_qs, n(i, h, p))
                dve.reciprocal(qinv[h][:, :], qs[h][:, :]).then_inc(s_qinv, 1)
            for h in range(2):
                dve.wait_ge(s_qinv, n(i, h, p))
                for t in range(TILES):
                    m = dve.tensor_scalar(qt[h][:, t, :], xn[h][:, t, :], qinv[h][:, t:t + 1], MAGIC,
                                          ALU.mult, ALU.add)
                m.then_inc(s_qmul, 1)
            for h in range(2):
                dve.wait_ge(s_qmul, n(i, h, p))
                dve.tensor_scalar(qt[h][:, :, :], qt[h][:, :, :], MAGIC - 128.0, MAGIC + 127.0,
                                  ALU.max, ALU.min).then_inc(s_qclip, 1)
            for h in range(2):
                dve.wait_ge(s_qclip, n(i, h, p))
                dve.tensor_scalar(qi[h][:, :, :], qt[h][:, :, :], -MAGIC, None, ALU.add).then_inc(s_qi, 1)
            for h in range(2):
                dve.wait_ge(s_qy, n(i, h, p))
                dve.wait_ge(s_qxb, n(i, h, p))
                for t in range(TILES):
                    m = dve.scalar_tensor_tensor(out=qt[h][:, t, :], in0=pb(h, 1)[:, t * P:(t + 1) * P],
                                                 scalar=qs[h][:, t:t + 1], in1=half_ws[:, t, :],
                                                 op0=ALU.mult, op1=ALU.mult)
                m.then_inc(s_qz, 1)
            for h in range(2):
                dve.wait_ge(s_qz, n(i, h, p))
                dve.tensor_tensor(xg(i, h), xg(i, h), qt[h][:, :, :], ALU.add).then_inc(s_x, 1)

        def quant_gpsimd(pool, i, p, ph):
            ln_gpsimd(pool, i, ph)
            for h in range(2):
                pool.wait_ge(s_xn, n(i, h, ph))
                pool.tensor_tensor(xg(i, h), xg(i, h), half_qb[:, :, :], ALU.add).then_inc(s_qxb, 1)

        def quant_tensor(pe, i, p):
            for h in range(2):
                pe.wait_ge(s_qi, n(i, h, p))
                transposes(pe, pb(h, 0)[:, 0:GROUP // 2].bitcast(BF16), qi[h], ident_bf[:, :]).then_inc(s_qtr, 1)
            for h in range(2):
                pe.wait_ge(s_qit, n(i, h, p))
                tile_mm(pe, pb(h, 1), qit[h], wq[:, :]).then_inc(s_qy, 1)

        def quant_scalar(act, i, p):
            for h in range(2):
                act.wait_ge(s_qtr, n(i, h, p))
                act.activation(qit[h][:, :], pb(h, 0)[:, 0:GROUP // 2].bitcast(BF16), ACT.Copy).then_inc(s_qit, 1)

        def l0_vector(dve, i, ph):
            ln_vector(dve, i, ph)
            for h in range(2):
                dve.wait_ge(s_r2, n(i, h))
                dve.wait_ge(s_xn, n(i, h, ph))
                for t in range(TILES):
                    m = dve.tensor_scalar(tt[h][:, t, :], xn[h][:, t, :], r2[h][:, t:t + 1], None, ALU.mult)
                m.then_inc(s_t, 1)
            for k in range(PAD):
                for h in range(2):
                    dve.wait_ge(s_xp, n(i, h))
                    if k:
                        dve.wait_ge(s_conv, i * (2 * PAD) + (2 * (k - 1) + h + 1))
                    dve.scalar_tensor_tensor(out=xc[h][:, :, :], in0=xp[h][:, :, k:k + S],
                                             scalar=cols[:, CW0 + k:CW0 + k + 1], in1=xc[h][:, :, :],
                                             op0=ALU.mult, op1=ALU.add).then_inc(s_conv, 1)
            for h in range(2):
                dve.wait_ge(s_a, n(i, h))
                dve.scalar_tensor_tensor(out=bufD[h][:, :], in0=bufA[h][:, :], scalar=-1.0, in1=bufA[h][:, :],
                                         op0=ALU.mult, op1=ALU.mult).then_inc(s_a2, 1)
            for h in range(2):
                dve.wait_ge(s_a2, n(i, h))
                dve.tensor_scalar(bufD[h][:, :], bufD[h][:, :], 1.0, 1e-12, ALU.add, ALU.max).then_inc(s_om, 1)
            for h in range(2):
                dve.wait_ge(s_b, n(i, h))
                for b in range(SEQS):
                    m = dve.tensor_tensor_scan(bufE[h][:, b * S:(b + 1) * S], bufA[h][:, b * S:(b + 1) * S],
                                               bufB[h][:, b * S:(b + 1) * S], 0.0, ALU.mult, ALU.add)
                m.then_inc(s_scan, 1)
            for h in range(2):
                dve.wait_ge(s_scan, n(i, h))
                dve.wait_ge(s_yb, n(i, h))
                dve.tensor_tensor(bufE[h][:, :], bufE[h][:, :], bufC[h][:, :], ALU.mult).then_inc(s_hy, 1)
            for h in range(2):
                dve.wait_ge(s_mix, n(i, h))
                dve.tensor_tensor(h1[h][:, :, :], xn[h][:, :, :],
                                  pb(h, 1)[:, :].rearrange("p (t d) -> p t d", t=TILES), ALU.add).then_inc(s_h1, 1)
            for h in range(2):
                dve.wait_ge(s_s2, n(i, h))
                for t in range(TILES):
                    m = dve.tensor_scalar(tt[h][:, t, :], h1[h][:, t, :], r2[h][:, t:t + 1], None, ALU.mult)
                m.then_inc(s_u, 1)
            for j in range(HJ):
                for h in range(2):
                    dve.wait_ge(s_gelu, i * (2 * HJ) + (2 * j + h + 1))
                    dve.wait_ge(s_fu, i * (2 * HJ) + (2 * j + h + 1))
                    dve.tensor_tensor(hid[h][:, j, :], gate[h][:, j, :], pb(h, 1 + 2 * (j % 2))[:, :],
                                      ALU.mult).then_inc(s_hid, 1)
            for h in range(2):
                dve.wait_ge(s_ffn, n(i, h))
                dve.wait_ge(s_xh, n(i, h))
                dve.tensor_tensor(x[:, i, h, :], x[:, i, h, :], pb(h, 0)[:, :], ALU.add).then_inc(s_x, 1)

        def l0_gpsimd(pool, i, ph):
            ln_gpsimd(pool, i, ph)
            for h in range(2):
                pool.wait_ge(s_rstd, n(i, h, ph))
                pool.tensor_tensor(r2[h][:, :], rstd[h][:, :], rstd[h][:, :], ALU.mult).then_inc(s_r2a, 1)
                pool.wait_ge(s_r2a, n(i, h))
                pool.tensor_tensor(r2[h][:, :], r2[h][:, :], var[h][:, :], ALU.mult).then_inc(s_r2b, 1)
                pool.wait_ge(s_r2b, 2 * (2 * i) + (2 * h + 1))
                pool.tensor_tensor(r2[h][:, :], r2[h][:, :], rms_eps[:, :], ALU.add).then_inc(s_r2b, 1)
                pool.wait_ge(s_r2b, 2 * (2 * i) + (2 * h + 2))
                pool.tensor_tensor(r2[h][:, :], r2[h][:, :], neg_half[:, :], ALU.pow).then_inc(s_r2, 1)
            for h in range(2):
                pool.wait_ge(s_sig, n(i, h))
                pool.tensor_tensor(bufB[h][:, :].rearrange("p (b s) -> p b s", b=SEQS),
                                   seqs(bufB[h]), xc[h][:, :, :], ALU.mult).then_inc(s_ix, 1)
            for h in range(2):
                pool.wait_ge(s_sq, n(i, h))
                pool.wait_ge(s_ix, n(i, h))
                pool.tensor_tensor(bufB[h][:, :], bufD[h][:, :], bufB[h][:, :], ALU.mult).then_inc(s_b, 1)
            for h in range(2):
                pool.wait_ge(s_ss, n(i, h))
                pool.tensor_tensor(ss[h][:, :], ss[h][:, :], rms_eps[:, :], ALU.add).then_inc(s_s2a, 1)
                pool.wait_ge(s_s2a, n(i, h))
                pool.tensor_tensor(r2[h][:, :], ss[h][:, :], neg_half[:, :], ALU.pow).then_inc(s_s2, 1)
            for h in range(2):
                pool.wait_ge(s_h1, n(i, h))
                pool.tensor_tensor(xg(i, h), xg(i, h), h1[h][:, :, :], ALU.add).then_inc(s_xh, 1)

        def l0_tensor(pe, i):
            for h in range(2):
                pe.wait_ge(s_t, n(i, h))
                transposes(pe, pb(h, 0), tt[h], ident[:, :]).then_inc(s_ttr, 1)
            for h in range(2):
                pe.wait_ge(s_tx, n(i, h))
                pe.matmul(pb(h, 1)[:, :], wx_n[:, 0, :], xt[h][:, :], start=True, stop=True).then_inc(s_xb, 1)
            for h in range(2):
                pe.matmul(pb(h, 2)[:, :], wx_n[:, 1, :], xt[h][:, :], start=True, stop=True).then_inc(s_y, 1)
            for h in range(2):
                pe.wait_ge(s_conv, i * (2 * PAD) + (2 * (PAD - 1) + h + 1))
                pe.matmul(pb(h, 3)[:, :], w_sq[:, 3, :], xc[h][:, :, :], start=True, stop=True)
                pe.matmul(pb(h, 0)[:, :], w_sq[:, 2, :], xc[h][:, :, :], start=True, stop=True).then_inc(s_gates, 1)
            for h in range(2):
                pe.wait_ge(s_hy, n(i, h))
                tile_mm(pe, pb(h, 1), bufE[h], w_sq[:, 4, :]).then_inc(s_mix, 1)
            for h in range(2):
                pe.wait_ge(s_u, n(i, h))
                transposes(pe, pb(h, 3), tt[h], ident[:, :]).then_inc(s_utr, 1)
            for j in range(HJ):
                for h in range(2):
                    pe.wait_ge(s_ut, n(i, h))
                    if j >= 2:
                        pe.wait_ge(s_gelu, i * (2 * HJ) + (2 * (j - 2) + h + 1))
                        pe.wait_ge(s_hid, i * (2 * HJ) + (2 * (j - 2) + h + 1))
                    pe.matmul(pb(h, 2 * (j % 2))[:, :], wgu_n[:, 0, j * P:(j + 1) * P], xt[h][:, :],
                              start=True, stop=True).then_inc(s_fg, 1)
                    pe.matmul(pb(h, 1 + 2 * (j % 2))[:, :], wgu_n[:, 1, j * P:(j + 1) * P], xt[h][:, :],
                              start=True, stop=True).then_inc(s_fu, 1)
            for h in range(2):
                pe.wait_ge(s_hid, i * (2 * HJ) + (2 * (HJ - 1) + h + 1))
                for t in range(TILES):
                    for j in range(HJ):
                        m = pe.matmul(pb(h, 0)[:, t * P:(t + 1) * P], hid[h][:, j, t * P:(t + 1) * P],
                                      w_dn[:, j, :], start=(j == 0), stop=(j == HJ - 1))
                m.then_inc(s_ffn, 1)

        def l0_scalar(act, i):
            for h in range(2):
                act.wait_ge(s_ttr, n(i, h))
                act.activation(xt[h][:, :], pb(h, 0)[:, :], ACT.Copy).then_inc(s_tx, 1)
            for h in range(2):
                act.wait_ge(s_xb, n(i, h))
                act.activation(xp[h][:, :, PAD:], seqs(pb(h, 1)), ACT.Copy)
                act.activation(xc[h][:, :, :], seqs(pb(h, 1)), ACT.Identity, scale=cols[:, CW0 + PAD:CW0 + PAD + 1],
                               bias=cols[:, CB:CB + 1]).then_inc(s_xp, 1)
            for h in range(2):
                act.wait_ge(s_gates, n(i, h))
                act.activation(bufA[h][:, :], pb(h, 3)[:, :], ACT.Sigmoid)
                act.activation(bufB[h][:, :], pb(h, 0)[:, :], ACT.Sigmoid).then_inc(s_sig, 1)
            for h in range(2):
                act.wait_ge(s_sig, n(i, h))
                act.activation(bufA[h][:, :], bufA[h][:, :], ACT.Exp, scale=decay[:, 0:1]).then_inc(s_a, 1)
            for h in range(2):
                act.wait_ge(s_om, n(i, h))
                act.activation(bufD[h][:, :], bufD[h][:, :], ACT.Sqrt).then_inc(s_sq, 1)
            for h in range(2):
                act.wait_ge(s_y, n(i, h))
                act.activation(bufC[h][:, :], pb(h, 2)[:, :], ACT.Gelu_apprx_tanh).then_inc(s_yb, 1)
            for h in range(2):
                act.wait_ge(s_h1, n(i, h))
                for t in range(TILES):
                    m = act.activation(bufD[h][:, t * P:(t + 1) * P], h1[h][:, t, :], ACT.Square, scale=float(D) ** -0.5,
                                       accum_out=ss[h][:, t:t + 1])
                m.then_inc(s_ss, 1)
            for h in range(2):
                act.wait_ge(s_utr, n(i, h))
                act.activation(xt[h][:, :], pb(h, 3)[:, :], ACT.Copy).then_inc(s_ut, 1)
            for j in range(HJ):
                for h in range(2):
                    act.wait_ge(s_fg, i * (2 * HJ) + (2 * j + h + 1))
                    act.activation(gate[h][:, j, :], pb(h, 2 * (j % 2))[:, :], ACT.Gelu_apprx_tanh).then_inc(s_gelu, 1)

        def route_vector(dve, i, p, ph):
            ln_vector(dve, i, ph)
            for h in range(2):
                dve.wait_ge(s_rl, n(i, h, p))
                dve.tensor_tensor(probs[h][:, :, :], pb(h, 1)[:, 0:TILES * E_ROUTED].rearrange("p (t e) -> p t e", t=TILES),
                                  rows[:, None, R_RB:R_RB + E_ROUTED].to_broadcast([P, TILES, E_ROUTED]),
                                  ALU.add).then_inc(s_rlb, 1)
            for h in range(2):
                dve.wait_ge(s_pr, n(i, h, p))
                pj = probs[h][:, :, None, :].to_broadcast([P, TILES, E_ROUTED, E_ROUTED])
                pe_ = probs[h][:, :, :, None].to_broadcast([P, TILES, E_ROUTED, E_ROUTED])
                dve.tensor_tensor(gt[h][:, :, :, :], pj, pe_, ALU.is_gt)
                dve.tensor_tensor(eq[h][:, :, :, :], pj, pe_, ALU.is_equal).then_inc(s_cmp, 1)
            for h in range(2):
                dve.wait_ge(s_cmp, n(i, h, p))
                dve.tensor_tensor(eq[h][:, :, :, :], eq[h][:, :, :, :],
                                  lower[:, None, :, :].to_broadcast([P, TILES, E_ROUTED, E_ROUTED]),
                                  ALU.mult).then_inc(s_cml, 1)
            for h in range(2):
                dve.wait_ge(s_cml, n(i, h, p))
                dve.tensor_tensor(gt[h][:, :, :, :], gt[h][:, :, :, :], eq[h][:, :, :, :], ALU.add).then_inc(s_cms, 1)
            for h in range(2):
                dve.wait_ge(s_cms, n(i, h, p))
                dve.tensor_reduce(rank[h][:, :, :], gt[h][:, :, :, :], AX.X, ALU.add).then_inc(s_rank, 1)
            for h in range(2):
                dve.wait_ge(s_rank, n(i, h, p))
                dve.tensor_scalar(rank[h][:, :, :], rank[h][:, :, :], 2.0, 0.5, ALU.is_lt, ALU.mult).then_inc(s_rk2, 1)
            for h in range(2):
                dve.wait_ge(s_rk2, n(i, h, p))
                cwg = cw[:, i, h, :].rearrange("p (t e) -> p t e", t=TILES)
                dve.tensor_tensor(cwg[:, :, 1:], rank[h][:, :, :], probs[h][:, :, :], ALU.mult).then_inc(s_cw, 1)

        def route_gpsimd(pool, i, p, ph):
            ln_gpsimd(pool, i, ph)
            for h in range(2):
                pool.wait_ge(s_xt, n(i, h, [0, 2][p]))
                pool.tensor_copy(xt_all[:, i, h, :], xt[h][:, :]).then_inc(s_xta, 1)

        def route_tensor(pe, i, p, ph):
            xt_tensor(pe, i, ph, [0, 2][p])
            for h in range(2):
                pe.wait_ge(s_xt, n(i, h, [0, 2][p]))
                tile_mm(pe, pb(h, 1), xt[h], w_r[:, :], E_ROUTED).then_inc(s_rl, 1)

        def route_scalar(act, i, p):
            xt_scalar(act, i, [0, 2][p])
            for h in range(2):
                act.wait_ge(s_rlb, n(i, h, p))
                act.activation(probs[h][:, :, :], probs[h][:, :, :], ACT.Sigmoid).then_inc(s_pr, 1)

        STEPS = 2 * E_ALL
        G_BANK, U_BANK, Y_BANK = (0, 1), (2, 3), (4, 5)

        def unit(i, p, st, j):
            return i * (STEPS * IJ) + (st * IJ + j + p * PAIRS * STEPS * IJ)

        def step_no(i, p, st):
            return i * STEPS + (st + p * PAIRS * STEPS)

        def moe_tensor(pe, i, p):
            def up(st):
                h, e = divmod(st, E_ALL)
                for j in range(IJ):
                    pe.wait_ge(s_silu, unit(i, p, st, j) + 1)
                    pe.matmul(bank[G_BANK[j]][:, :], e_gu[:, e, 0, j * P:(j + 1) * P], xt_all[:, i, h, :],
                              start=True, stop=True).then_inc(s_eg, 1)
                    pe.wait_ge(s_eh, unit(i, p, st, j) + 1)
                    pe.matmul(bank[U_BANK[j]][:, :], e_gu[:, e, 1, j * P:(j + 1) * P], xt_all[:, i, h, :],
                              start=True, stop=True).then_inc(s_eu, 1)

            def down(st):
                e = st % E_ALL
                pe.wait_ge(s_eh, unit(i, p, st, IJ - 1) + 3)
                pe.wait_ge(s_acc, step_no(i, p, st) + 1)
                y = bank[Y_BANK[st % 2]]
                for t in range(TILES):
                    for j in range(IJ):
                        m = pe.matmul(y[:, t * P:(t + 1) * P], eh[st % 2][j][:, t * P:(t + 1) * P], e_dn[:, e, j, :],
                                      start=(j == 0), stop=(j == IJ - 1))
                m.then_inc(s_ed, 1)

            up(0)
            for st in range(1, STEPS):
                up(st)
                down(st - 1)
            down(STEPS - 1)

        def moe_scalar(act, i, p):
            for st in range(STEPS):
                for j in range(IJ):
                    act.wait_ge(s_eg, unit(i, p, st, j) + 1)
                    act.wait_ge(s_eh, unit(i, p, st, j) + 1)
                    act.activation(sg[j][:, :], bank[G_BANK[j]][:, :], ACT.Silu).then_inc(s_silu, 1)

        def moe_vector(dve, i, p):
            def hidden(st):
                for j in range(IJ):
                    dve.wait_ge(s_silu, unit(i, p, st, j) + 3)
                    dve.wait_ge(s_eu, unit(i, p, st, j) + 1)
                    if st >= 2:
                        dve.wait_ge(s_ed, step_no(i, p, st - 2) + 1)
                    dve.tensor_tensor(eh[st % 2][j][:, :], sg[j][:, :], bank[U_BANK[j]][:, :], ALU.mult).then_inc(s_eh, 1)

            def add(st):
                h, e = divmod(st, E_ALL)
                dve.wait_ge(s_ed, step_no(i, p, st) + 1)
                dve.wait_ge(s_acc, step_no(i, p, st) + 2)
                for t in range(TILES):
                    m = dve.scalar_tensor_tensor(out=xg(i, h)[:, t, :], in0=bank[Y_BANK[st % 2]][:, t * P:(t + 1) * P],
                                                 scalar=cw[:, i, h, t * E_ALL + e:t * E_ALL + e + 1],
                                                 in1=xg(i, h)[:, t, :], op0=ALU.mult, op1=ALU.add)
                m.then_inc(s_acc, 1)
                if e == E_ALL - 1:
                    dve.wait_ge(s_acc, step_no(i, p, st) + 3)
                    dve.sem_inc(s_x, 1)

            hidden(0)
            for st in range(1, STEPS):
                hidden(st)
                add(st - 1)
            add(STEPS - 1)

        COPIES = LEVELS + 1

        def halves(buf, w):
            return buf[:, :].rearrange("p (b two r) -> p b two r", two=2, r=w)

        def gla_vector(dve, i, ph):
            ln_vector(dve, i, ph)
            for h in range(2):
                dve.wait_ge(s_v, n(i, h))
                dve.tensor_tensor(hid[h][:, 0, :].rearrange("p (t d) -> p t d", t=TILES),
                                  pb(h, 0)[:, :].rearrange("p (t d) -> p t d", t=TILES),
                                  rows[:, None, R_BV:R_BV + P].to_broadcast([P, TILES, P]), ALU.add).then_inc(s_vb, 1)
            for h in range(2):
                dve.wait_ge(s_qk, n(i, h))
                dve.tensor_tensor(bufA[h][:, :], bufD[h][:, :], tseg[h][:, :], ALU.mult).then_inc(s_q0, 1)
            for lv in range(LEVELS):
                w = 1 << lv
                for h in range(2):
                    dve.wait_ge(s_lvl, i * (2 * LEVELS) + (2 * lv + h + 1))
                    if lv:
                        dve.wait_ge(s_upd, i * (2 * LEVELS) + (2 * (lv - 1) + h + 1))
                        dve.wait_ge(s_pred, i * (2 * COPIES) + (2 * (lv - 1) + h + 1))
                    else:
                        dve.wait_ge(s_dg, n(i, h))
                    cur, nxt = (tseg[h], tseg2[h]) if lv % 2 == 0 else (tseg2[h], tseg[h])
                    seg = cur[:, 0:GROUP // w].rearrange("p (b two) -> p b two", two=2)
                    nb = GROUP // (2 * w)
                    dve.tensor_tensor(halves(bufA[h], w)[:, :, 1, :], halves(bufA[h], w)[:, :, 1, :],
                                      seg[:, :, 0:1].to_broadcast([P, nb, w]), ALU.mult)
                    m = dve.tensor_tensor(halves(bufB[h], w)[:, :, 0, :], halves(bufB[h], w)[:, :, 0, :],
                                          seg[:, :, 1:2].to_broadcast([P, nb, w]), ALU.mult)
                    if lv < LEVELS - 1:
                        m = dve.tensor_tensor(nxt[:, 0:nb], seg[:, :, 0], seg[:, :, 1], ALU.mult)
                    m.then_inc(s_upd, 1)
                    if lv == 0:
                        m = dve.copy_predicated(at[h][:, :], masks[:, (LEVELS - 1) * 256:], pb(h, 3)[:, :])
                    else:
                        m = dve.copy_predicated(
                            halves(at[h], w // 2)[:, :, 1, :],
                            masks[:, (lv - 1) * 256:lv * 256].rearrange("p (b r) -> p b r", r=w // 2),
                            pb(h, 1 + (lv - 1) % 3)[:, 0:256].rearrange("p (b r) -> p b r", r=w // 2))
                    m.then_inc(s_pred, 1)
            for h in range(2):
                dve.wait_ge(s_pred, i * (2 * COPIES) + (2 * (LEVELS - 1) + h + 1))
                dve.tensor_copy(halves(at[h], P // 2)[0:P // 2, :, 1, :],
                                pb(h, 1 + (LEVELS - 1) % 3)[0:P // 2, 0:256].rearrange("p (c r) -> p c r", c=TILES)
                                ).then_inc(s_pred, 1)
            for h in range(2):
                dve.wait_ge(s_op, n(i, h))
                dve.wait_ge(s_xbo, n(i, h))
                dve.tensor_tensor(x[:, i, h, :], x[:, i, h, :], pb(h, 2)[:, :], ALU.add).then_inc(s_x, 1)

        def gla_gpsimd(pool, i, ph):
            ln_gpsimd(pool, i, ph)
            for h in range(2):
                pool.wait_ge(s_xn, n(i, h, ph))
                pool.tensor_tensor(xg(i, h), xg(i, h), rows[:, None, R_BO:R_BO + P].to_broadcast([P, TILES, P]),
                                   ALU.add).then_inc(s_xbo, 1)

        def gla_tensor(pe, i, ph):
            xt_tensor(pe, i, ph, 1)
            for h in range(2):
                pe.wait_ge(s_xt, n(i, h, 1))
                pe.matmul(pb(h, 1)[:, :], a_sq[:, 0, :], xt[h][:, :], start=True, stop=True)
                pe.matmul(pb(h, 2)[:, :], a_sq[:, 1, :], xt[h][:, :], start=True, stop=True)
                pe.matmul(pb(h, 3)[:, :], a_sq[:, 3, :], xt[h][:, :], start=True, stop=True).then_inc(s_qkg, 1)
                tile_mm(pe, pb(h, 0), xt[h], a_sq[:, 2, :]).then_inc(s_v, 1)
            for h in range(2):
                pe.wait_ge(s_qk, n(i, h))
                for c in range(TILES):
                    m = pe.matmul(pb(h, 3)[:, c * P:(c + 1) * P], bufB[h][:, c * P:(c + 1) * P],
                                  bufD[h][:, c * P:(c + 1) * P], start=True, stop=True)
                m.then_inc(s_dg, 1)
            for lv in range(LEVELS):
                w = 1 << lv
                for h in range(2):
                    if lv:
                        pe.wait_ge(s_upd, i * (2 * LEVELS) + (2 * (lv - 1) + h + 1))
                    else:
                        pe.wait_ge(s_q0, n(i, h))
                    qv = bufA[h][:, :].rearrange("p (c b two r) -> p c b two r", c=TILES, two=2, r=w)
                    for c in range(TILES):
                        m = pe.matmul(pb(h, 1 + lv % 3)[:, c * 64:(c + 1) * 64], bufB[h][:, c * P:(c + 1) * P],
                                      qv[:, c, :, 1, :], start=True, stop=True)
                    m.then_inc(s_lvl, 1)
            for h in range(2):
                pe.wait_ge(s_upd, i * (2 * LEVELS) + (2 * (LEVELS - 1) + h + 1))
                pe.wait_ge(s_vb, n(i, h))
                for b in range(SEQS):
                    m = pe.matmul(pb(h, 0)[:, b * P:(b + 1) * P], bufB[h][:, 2 * b * P:(2 * b + 1) * P],
                                  bufA[h][:, (2 * b + 1) * P:(2 * b + 2) * P], start=True, stop=True)
                m.then_inc(s_cross, 1)
            for h in range(2):
                pe.wait_ge(s_cc, n(i, h))
                pe.wait_ge(s_pred, i * (2 * COPIES) + (2 * (COPIES - 1) + h + 1))
                v = hid[h][:, 0, :]
                for b in range(SEQS):
                    c0, c1 = 2 * b * P, (2 * b + 1) * P
                    pe.matmul(pb(h, 1)[:, c0:c0 + P], v[:, c0:c0 + P], at[h][:, c0:c0 + P], start=True, stop=True)
                    pe.matmul(pb(h, 1)[:, c1:c1 + P], v[:, c0:c0 + P], across[h][:, b, :], start=True, stop=False)
                    m = pe.matmul(pb(h, 1)[:, c1:c1 + P], v[:, c1:c1 + P], at[h][:, c1:c1 + P], start=False, stop=True)
                m.then_inc(s_o, 1)
            for h in range(2):
                pe.wait_ge(s_oc, n(i, h))
                tile_mm(pe, pb(h, 2), bufE[h], a_sq[:, 4, :]).then_inc(s_op, 1)

        def gla_scalar(act, i):
            xt_scalar(act, i, 1)
            for h in range(2):
                act.wait_ge(s_qkg, n(i, h))
                act.activation(bufD[h][:, :], pb(h, 1)[:, :], ACT.Identity, bias=cols[:, BQ:BQ + 1])
                act.activation(bufB[h][:, :], pb(h, 2)[:, :], ACT.Sigmoid, bias=cols[:, BK:BK + 1])
                act.activation(tseg[h][:, :], pb(h, 3)[:, :], ACT.Sigmoid, bias=cols[:, BG:BG + 1]).then_inc(s_qk, 1)
            for h in range(2):
                act.wait_ge(s_cross, n(i, h))
                act.activation(across[h][:, :, :], pb(h, 0)[:, 0:SEQS * P].rearrange("p (b c) -> p b c", b=SEQS),
                               ACT.Copy).then_inc(s_cc, 1)
            for h in range(2):
                act.wait_ge(s_o, n(i, h))
                act.activation(bufE[h][:, :], pb(h, 1)[:, :], ACT.Copy).then_inc(s_oc, 1)

        @block.vector
        def _(dve):
            dve.sem_inc(s_eh, 2)
            dve.sem_inc(s_acc, 2)
            for h in range(2):
                dve.memset(at[h][:, :], 0.0)
                dve.memset(xp[h][:, :, 0:PAD], 0.0)
            dve.wait_ge(s_load, 16 * LOADS)
            dve.tensor_copy(wq[:, :], wq_int[:, :, 0])
            dve.tensor_copy(ident_bf[:, :], ident[:, :])
            for t in range(TILES):
                dve.tensor_scalar(half_ws[:, t, :], rows[:, R_WS:R_WS + P], 0.5, None, ALU.mult)
                dve.tensor_scalar(half_qb[:, t, :], rows[:, R_QB:R_QB + P], 0.5, None, ALU.mult)
            dve.tensor_scalar(wx_n[:, :, :], w_sq[:, 0:2, :], cols[:, N1W:N1W + 1], None, ALU.mult)
            dve.tensor_scalar(wgu_n[:, :, :], w_gu[:, :, :], cols[:, N2W:N2W + 1], None, ALU.mult).then_inc(s_const, 1)
            dve.wait_ge(s_act_const, 1)
            dve.tensor_scalar(sp[:, 3:4], cols[:, LAM:LAM + 1], 0.0, sp[:, 2:3], ALU.max, ALU.add).then_inc(s_const, 1)
            dve.wait_ge(s_const, 2)
            dve.tensor_scalar(decay[:, :], sp[:, 3:4], -C_CONST, None, ALU.mult).then_inc(s_const, 1)
            with dve.Fori(0, PAIRS) as i:
                quant_vector(dve, i, 0, 0)
            with dve.Fori(0, PAIRS) as i:
                l0_vector(dve, i, 1)
            with dve.Fori(0, PAIRS) as i:
                quant_vector(dve, i, 1, 2)
            with dve.Fori(0, PAIRS) as i:
                route_vector(dve, i, 0, 3)
            with dve.Fori(0, PAIRS) as i:
                moe_vector(dve, i, 0)
            with dve.Fori(0, PAIRS) as i:
                gla_vector(dve, i, 4)
            with dve.Fori(0, PAIRS) as i:
                route_vector(dve, i, 1, 5)
            with dve.Fori(0, PAIRS) as i:
                moe_vector(dve, i, 1)

        @block.gpsimd
        def _(pool):
            pool.memset(cw[:, :, :, :], 0.5)
            pool.memset(ln_eps[:, :], LN_EPS)
            pool.memset(rms_eps[:, :], RMS_EPS)
            pool.memset(neg_half[:, :], -0.5).then_inc(s_pool_const, 1)
            pool.wait_ge(s_pool_const, 1)
            pool.wait_ge(s_const, 1)
            with pool.Fori(0, PAIRS) as i:
                quant_gpsimd(pool, i, 0, 0)
            with pool.Fori(0, PAIRS) as i:
                l0_gpsimd(pool, i, 1)
            with pool.Fori(0, PAIRS) as i:
                quant_gpsimd(pool, i, 1, 2)
            with pool.Fori(0, PAIRS) as i:
                route_gpsimd(pool, i, 0, 3)
            with pool.Fori(0, PAIRS) as i:
                gla_gpsimd(pool, i, 4)
            with pool.Fori(0, PAIRS) as i:
                route_gpsimd(pool, i, 1, 5)

        @block.tensor
        def _(pe):
            pe.wait_ge(s_const, 1)
            with pe.Fori(0, PAIRS) as i:
                quant_tensor(pe, i, 0)
            with pe.Fori(0, PAIRS) as i:
                l0_tensor(pe, i)
            with pe.Fori(0, PAIRS) as i:
                quant_tensor(pe, i, 1)
            pe.wait_ge(s_load2, 48)
            with pe.Fori(0, PAIRS) as i:
                route_tensor(pe, i, 0, 3)
            pe.wait_ge(s_cw, GROUPS)
            pe.wait_ge(s_xta, GROUPS)
            with pe.Fori(0, PAIRS) as i:
                moe_tensor(pe, i, 0)
            with pe.Fori(0, PAIRS) as i:
                gla_tensor(pe, i, 4)
            with pe.Fori(0, PAIRS) as i:
                route_tensor(pe, i, 1, 5)
            pe.wait_ge(s_cw, 2 * GROUPS)
            pe.wait_ge(s_xta, 2 * GROUPS)
            with pe.Fori(0, PAIRS) as i:
                moe_tensor(pe, i, 1)

        @block.scalar
        def _(act):
            act.sem_inc(s_silu, 2)
            act.wait_ge(s_load, 16 * LOADS)
            act.activation(sp[:, 0:1], cols[:, LAM:LAM + 1], ACT.Abs).then_inc(s_act_sp, 1)
            act.wait_ge(s_act_sp, 1)
            act.activation(sp[:, 1:2], sp[:, 0:1], ACT.Exp, scale=-1.0).then_inc(s_act_sp, 1)
            act.wait_ge(s_act_sp, 2)
            act.activation(sp[:, 2:3], sp[:, 1:2], ACT.Ln, bias=1.0).then_inc(s_act_const, 1)
            act.wait_ge(s_const, 3)
            with act.Fori(0, PAIRS) as i:
                quant_scalar(act, i, 0)
            with act.Fori(0, PAIRS) as i:
                l0_scalar(act, i)
            with act.Fori(0, PAIRS) as i:
                quant_scalar(act, i, 1)
            with act.Fori(0, PAIRS) as i:
                route_scalar(act, i, 0)
            with act.Fori(0, PAIRS) as i:
                moe_scalar(act, i, 0)
            with act.Fori(0, PAIRS) as i:
                gla_scalar(act, i)
            with act.Fori(0, PAIRS) as i:
                route_scalar(act, i, 1)
            with act.Fori(0, PAIRS) as i:
                moe_scalar(act, i, 1)


def kernel(**inputs):
    import numpy as np
    import concourse.bacc as bacc
    from concourse.bass_utils import run_bass_kernel_spmd as run

    v = {k: np.asarray(a) for k, a in inputs.items()}
    c = np.ascontiguousarray

    def across(*vectors):
        return c(np.broadcast_to(np.concatenate(vectors)[None, :], (P, sum(len(a) for a in vectors))))

    def tokens(a):
        return a.reshape(PAIRS, 2, TILES, P, D).transpose(3, 0, 1, 2, 4).reshape(P, PAIRS, 2, GROUP)

    gate_up = np.stack([np.concatenate([v["L1_ffn_Wg_s"][None], v["L1_ffn_Wg"]]),
                        np.concatenate([v["L1_ffn_Wu_s"][None], v["L1_ffn_Wu"]])], axis=1)
    down = np.concatenate([v["L1_ffn_Wd_s"][None], v["L1_ffn_Wd"]])

    row = np.arange(P)[:, None]
    levels = []
    for lv in range(LEVELS - 1):
        w = 1 << lv
        col = np.arange(64)[None, :] // w
        levels.append(np.tile((row // w == 2 * col), (1, TILES)))
    levels.append(np.tile(row == np.arange(P)[None, :], (1, TILES)))
    masks = np.concatenate(levels, axis=1).astype(np.int32)
    lower = np.tile((np.arange(E_ROUTED)[None, :] < np.arange(E_ROUTED)[:, None])[None], (P, 1, 1)).astype(np.float32)

    arrays = {
        "x_in": tokens(v["L0_attn_x"].reshape(TOKENS, D)),
        "wq64": v["L0_ffn_weight_q"].T.astype(np.int64),
        "cols_in": np.stack([v["L0_attn_norm1_w"], *v["L0_attn_conv_w"], v["L0_attn_conv_b"], v["L0_attn_lam"],
                             v["L0_attn_norm2_w"], v["L1_attn_bq"], v["L1_attn_bk"], v["L1_attn_bg"]], axis=1),
        "rows_in": across(v["L0_ffn_weight_scale"], v["L0_ffn_bias"], v["L1_attn_bv"], v["L1_attn_bo"], v["L1_ffn_rb"]),
        "l0_sq": np.stack([v["L0_attn_" + k] for k in ("Wx", "Wy", "Wi", "Wa", "Wo")], axis=1),
        "l0_gu": np.stack([v["L0_attn_Wg"], v["L0_attn_Wu"]], axis=1),
        "l0_dn": v["L0_attn_Wd"].reshape(HJ, P, D).transpose(1, 0, 2),
        "l1_sq": np.stack([v["L1_attn_" + k] for k in ("Wq", "Wk", "Wv", "Wg", "Wo")], axis=1),
        "moe_gu": gate_up.transpose(3, 0, 1, 2),
        "moe_dn": down.transpose(2, 0, 1).reshape(IJ, P, E_ALL, D).transpose(1, 2, 0, 3),
        "moe_r": v["L1_ffn_Wr"].T,
        "ident_in": np.eye(P, dtype=np.float32),
        "masks_in": masks,
        "lower_in": lower,
    }
    nc = bacc.Bacc("TRN2", target_bir_lowering=False, num_devices=1)
    args, feed = [], {}
    for name, a in arrays.items():
        feed[name] = c(a)
        args.append(nc.dram_tensor(name, a.shape, mybir.dt.from_np(a.dtype), kind="ExternalInput").ap())
    args.append(nc.dram_tensor("out", (P, PAIRS, 2, GROUP), F32, kind="ExternalOutput").ap())
    macaron_kernel(nc, *args)
    r = run(nc, [feed], core_ids=[0])
    got = r.results[0]["out"]
    return c(got.reshape(P, PAIRS, 2, TILES, D).transpose(1, 2, 3, 0, 4).reshape(B, S, D))
```

```python
from contextlib import ExitStack

import concourse.bass as bass
from concourse import mybir

ALU = mybir.AluOpType
ACT = mybir.ActivationFunctionType
AX = mybir.AxisListType
F32 = mybir.dt.float32
BF16 = mybir.dt.bfloat16
I32 = mybir.dt.int32
U8 = mybir.dt.uint8

P = 128
B, S, D = 16, 256, 128
TOKENS = B * S
GROUP = 512
TILES = GROUP // P
GROUPS = TOKENS // GROUP
PAIRS = GROUPS // 2
SEQS = GROUP // S
HID = 512
HJ = HID // P
TAPS = 4
PAD = TAPS - 1
E_ROUTED, E_ALL, INNER = 8, 9, 256
IJ = INNER // P
SHARED = E_ROUTED
TOP_K = 2
NT = TOP_K * TOKENS // P + E_ROUTED
REGION = TOKENS + P
BLK = 8
OUT_RING = 4
NB = NT // BLK
ROW = D + 1
LEVELS = 7
LN_EPS, RMS_EPS, Q_EPS = 1e-5, 1e-6, 1e-6
MAGIC = 1.5 * 2.0 ** 23
C_CONST = 8.0

N1W, CW0, CB, LAM, N2W, BQ, BK, BG = 0, 1, 5, 6, 7, 8, 9, 10
NCOLS = 11
R_WS, R_QB, R_BV, R_BO, R_RB = 0, P, 2 * P, 3 * P, 4 * P
NROWS = 4 * P + E_ROUTED
K_ID, K_BEFORE, K_LOWER, K_REGION, K_PAD, K_J, K_J128 = 0, P, 2 * P, 2 * P + 64, 2 * P + 72, 2 * P + 80, 2 * P + 80 + NT
K_TOKEN = K_J128 + NT
K_AWAY = K_TOKEN + TOKENS // P
NCONST = K_AWAY + 2 * E_ROUTED


def macaron_kernel(nc, x_in, wq64, cols_in, rows_in, l0_sq, l0_gu, l0_dn, l1_sq, moe_gu, moe_dn, moe_r,
                   consts_in, masks_in, rows_by_expert, rows_done, out):
    with ExitStack() as ctx:
        def sb(name, shape, dt=F32):
            return ctx.enter_context(nc.sbuf_tensor(name, shape, dt))

        def sem(name):
            return ctx.enter_context(nc.semaphore(name))

        ctx.enter_context(nc.allow_low_precision(reason="whole numbers below 2^24"))

        x = sb("x", [P, PAIRS, 2, GROUP])
        score = sb("score", [P, PAIRS, 2, TOP_K * TILES])
        carry = [sb(f"carry{h}", [P, E_ROUTED]) for h in range(2)]
        cnt = sb("cnt", [P, E_ROUTED])
        tl = sb("tl", [P, 4, E_ROUTED])
        tiles_e = sb("tiles_e", [P, E_ROUTED])
        cum = sb("cum", [P, E_ROUTED])
        padidx = sb("padidx", [P, E_ROUTED], I32)
        cmp = sb("cmp", [P, NT, E_ROUTED])
        cmpt = sb("cmpt", [P, NT, E_ROUTED])
        etabf = sb("etabf", [P, NT])
        stab = sb("stab", [P, NT])
        rtabf = sb("rtabf", [P, NT])
        etab = sb("etab", [P, NB, BLK], I32)
        rtab = sb("rtab", [P, NB, BLK], I32)
        zero_col = sb("zero_col", [P, 1])
        scratch2 = [sb(f"scratch2{h}", [P, 1]) for h in range(2)]
        ones8 = sb("ones8", [P, E_ROUTED])
        ones_bf = sb("ones_bf", [P, P], BF16)
        before_bf = sb("before_bf", [P, P], BF16)
        wq_int = sb("wq_int", [P, P, 2], I32)
        wq = sb("wq", [P, P], BF16)
        cols = sb("cols", [P, NCOLS])
        rows = sb("rows", [P, NROWS])
        w_sq = sb("w_sq", [P, 5, P])
        w_gu = sb("w_gu", [P, 2, HID])
        w_dn = sb("w_dn", [P, HJ, P])
        a_sq = sb("a_sq", [P, 5, P])
        e_gu = sb("e_gu", [P, E_ALL, 2, INNER])
        e_dn = sb("e_dn", [P, E_ALL, IJ, P])
        w_r = sb("w_r", [P, E_ROUTED])
        consts = sb("consts", [P, NCONST])
        ident = consts[:, K_ID:K_ID + P]
        ident_bf = sb("ident_bf", [P, P], BF16)
        masks = sb("masks", [P, (LEVELS - 1) * 256 + GROUP], U8)
        lower = consts[:, K_LOWER:K_LOWER + 64].rearrange("p (e j) -> p e j", e=E_ROUTED)
        region = consts[:, K_REGION:K_REGION + E_ROUTED]
        neg_half = sb("neg_half", [P, TILES])
        rms_eps = sb("rms_eps", [P, TILES])
        wx_n = sb("wx_n", [P, 2, P])
        wgu_n = sb("wgu_n", [P, 2, HID])
        half_ws = sb("half_ws", [P, TILES, P])
        half_qb = sb("half_qb", [P, TILES, P])
        sp = sb("sp", [P, 4])
        decay = sb("decay", [P, 1])

        def two(name, shape, dt=F32):
            return [sb(f"{name}{h}", shape, dt) for h in range(2)]

        stats = two("stats", [P, 2, TILES, 6])
        msum = two("msum", [P, 2, TILES])
        mdif = two("mdif", [P, 2, TILES])
        m2 = two("m2", [P, 2, TILES])
        mean = two("mean", [P, 2, TILES])
        var = two("var", [P, 2, TILES])
        ve = two("ve", [P, 2, TILES])
        rstd = two("rstd", [P, 2, TILES])
        xn = two("xn", [P, TILES, ROW])
        xt = two("xt", [P, GROUP])
        amax = two("amax", [P, TILES])
        qs = two("qs", [P, TILES])
        qinv = two("qinv", [P, TILES])
        qt = two("qt", [P, TILES, P])
        qi = two("qi", [P, TILES, P], BF16)
        qit = two("qit", [P, GROUP], BF16)
        r2 = sb("r2", [P, 2, TILES])
        ms = sb("ms", [P, 2, TILES])
        tt = two("tt", [P, TILES, P])
        xp = two("xp", [P, SEQS, PAD + S])
        xc = two("xc", [P, SEQS, S])
        bufA = two("bufA", [P, GROUP])
        bufB = two("bufB", [P, GROUP])
        bufC = two("bufC", [P, GROUP])
        bufD = two("bufD", [P, GROUP])
        bufE = two("bufE", [P, GROUP])
        h1 = two("h1", [P, TILES, P])
        ss = two("ss", [P, TILES])
        gate = two("gate", [P, HJ, GROUP])
        hid = two("hid", [P, HJ, GROUP])
        masks_wide = hid[0][:, :, :].rearrange("p j c -> p (j c)").bitcast(I32)
        at = two("at", [P, GROUP])
        across = two("across", [P, SEQS, P])
        tseg = two("tseg", [P, GROUP])
        tseg2 = two("tseg2", [P, GROUP // 2])
        probs = two("probs", [P, TILES, E_ROUTED])
        gt = [h1[h][:, 0:2, :].rearrange("p a (b e j) -> p (a b) e j", b=2, e=E_ROUTED) for h in range(2)]
        eq = [h1[h][:, 2:4, :].rearrange("p a (b e j) -> p (a b) e j", b=2, e=E_ROUTED) for h in range(2)]
        gxt = [xc[h][:, :, :].rearrange("p b s -> p (b s)") for h in range(2)]
        rank = two("rank", [P, TILES, E_ROUTED])
        chosen = two("chosen", [P, TILES, E_ROUTED], BF16)
        slot = two("slot", [P, TILES, E_ROUTED])
        slotf = two("slotf", [P, TOP_K, TILES, E_ROUTED])
        scoref = two("scoref", [P, TOP_K, TILES, E_ROUTED])
        sidx = two("sidx", [P, TOP_K * TILES], I32)
        first2 = two("first2", [P, TOP_K, TILES, E_ROUTED])
        xn2 = two("xn2", [P, TILES, ROW])
        got = two("got", [P, TOP_K * TILES, P])
        qxn = [got[h][:, 0:TILES, :] for h in range(2)]
        ut = [got[h][:, TILES:, :].rearrange("p t d -> p (t d)") for h in range(2)]
        tin = [sb(f"tin{k}", [P, ROW]) for k in range(BLK)]
        tdst = [sb(f"tdst{k}", [P, 1], I32) for k in range(BLK)]
        tout = [sb(f"tout{k}", [P, P]) for k in range(OUT_RING)]
        tint = two("tint", [P, P])
        tsil = two("tsil", [P, INNER])
        thid = two("thid", [P, INNER])
        thidt = two("thidt", [P, IJ, P])

        bank = [ctx.enter_context(nc.psum_tensor(f"bank{i}", [P, GROUP], F32)) for i in range(8)]

        def pb(h, k):
            return bank[4 * h + k]

        def gb(h, k):
            return bank[4 * h + k]

        def rb(h, k):
            return bank[4 * h + 2 + k]

        s_first = sem("s_first")
        s_load = sem("s_load")
        s_load2 = sem("s_load2")
        s_act_sp = sem("s_act_sp")
        s_const = sem("s_const")
        s_pool_const = sem("s_pool_const")
        s_act_const = sem("s_act_const")
        s_stats = [sem(f"s_stats{u}") for u in range(2)]
        s_mom = [sem(f"s_mom{u}") for u in range(2)]; s_mean = [sem(f"s_mean{u}") for u in range(2)]
        s_mv = [sem(f"s_mv{u}") for u in range(2)]
        s_ve = [sem(f"s_ve{u}") for u in range(2)]
        s_rstd = [sem(f"s_rstd{u}") for u in range(2)]
        s_xn = [sem(f"s_xn{u}") for u in range(2)]
        s_xq = sem("s_xq"); s_xl = sem("s_xl"); s_x = sem("s_x")
        s_xtr = [sem(f"s_xtr{u}") for u in range(2)]
        s_xt = [sem(f"s_xt{u}") for u in range(2)]
        s_root = [sem(f"s_root{u}") for u in range(2)]
        s_amax = sem("s_amax"); s_qs = sem("s_qs"); s_qinv = sem("s_qinv"); s_qmul = sem("s_qmul")
        s_qclip = sem("s_qclip"); s_qi = sem("s_qi"); s_qtr = sem("s_qtr"); s_qit = sem("s_qit")
        s_qy = sem("s_qy"); s_qz = sem("s_qz"); s_qxb = sem("s_qxb")
        s_xb = sem("s_xb"); s_xp = sem("s_xp"); s_ms = sem("s_ms"); s_r2 = sem("s_r2")
        s_t = sem("s_t"); s_ttr = sem("s_ttr"); s_tx = sem("s_tx")
        s_conv = sem("s_conv"); s_y = sem("s_y"); s_gates = sem("s_gates"); s_sig = sem("s_sig")
        s_a = sem("s_a"); s_a2 = sem("s_a2"); s_om = sem("s_om"); s_sq = sem("s_sq"); s_ix = sem("s_ix")
        s_b = sem("s_b"); s_scan = sem("s_scan"); s_yb = sem("s_yb"); s_hy = sem("s_hy")
        s_mix = sem("s_mix"); s_h1 = sem("s_h1"); s_ss = sem("s_ss"); s_s2a = sem("s_s2a"); s_s2 = sem("s_s2")
        s_u = sem("s_u"); s_utr = sem("s_utr"); s_ut = sem("s_ut"); s_fg = sem("s_fg"); s_fu = sem("s_fu")
        s_gelu = sem("s_gelu"); s_hid = sem("s_hid"); s_ffn = sem("s_ffn"); s_xh = sem("s_xh")
        s_qkp = sem("s_qkp"); s_qkc = sem("s_qkc"); s_gp = sem("s_gp"); s_v = sem("s_v"); s_qk = sem("s_qk"); s_vb = sem("s_vb")
        s_q0 = sem("s_q0"); s_lvl = sem("s_lvl"); s_upd = sem("s_upd")
        s_pred = sem("s_pred"); s_cross = sem("s_cross"); s_cc = sem("s_cc"); s_o = sem("s_o")
        s_oc = sem("s_oc"); s_op = sem("s_op"); s_xbo = sem("s_xbo"); s_dg = sem("s_dg")
        s_rl = sem("s_rl"); s_rlb = sem("s_rlb"); s_pr = sem("s_pr"); s_cmp = sem("s_cmp")
        s_cml = sem("s_cml"); s_cms = sem("s_cms"); s_rank = sem("s_rank"); s_first2 = sem("s_first2")
        s_pref = sem("s_pref"); s_slot = sem("s_slot"); s_prod = sem("s_prod"); s_idx = sem("s_idx")
        s_ids = sem("s_ids"); s_xn2 = sem("s_xn2"); s_carry = sem("s_carry")
        s_scat = [sem(f"s_scat{h}") for h in range(2)]
        s_tab = sem("s_tab")
        s_zero = sem("s_zero"); s_padding = sem("s_padding"); s_zfill = sem("s_zfill"); s_pad = sem("s_pad")
        s_sg = sem("s_sg"); s_su = sem("s_su"); s_silu = sem("s_silu"); s_sh = sem("s_sh"); s_sd = sem("s_sd")
        s_xsh = sem("s_xsh")
        s_add0 = sem("s_add0"); s_add1 = sem("s_add1")
        s_got = [sem(f"s_got{h}") for h in range(2)]
        s_in = [sem(f"s_in{k}") for k in range(BLK)]
        s_st = [sem(f"s_st{k}") for k in range(OUT_RING)]
        s_tt = sem("s_tt"); s_ttc = sem("s_ttc"); s_tgu = sem("s_tgu"); s_tsil = sem("s_tsil")
        s_thid = sem("s_thid"); s_tht = sem("s_tht"); s_thc = sem("s_thc"); s_tdn = sem("s_tdn")
        s_tyc = sem("s_tyc"); s_tdst = sem("s_tdst")
        s_out = sem("s_out")

        FIRST, LOADS = 5, 8
        SCAT = 16 * TOP_K * TILES
        XL_AHEAD = 2

        def xg(i, h):
            return x[:, i, h, :].rearrange("p (t d) -> p t d", t=TILES)

        def seqs(buf):
            return buf[:, :].rearrange("p (b s) -> p b s", b=SEQS)

        def n(i, h, ph=0):
            return 2 * i + (h + 1 + GROUPS * ph)

        def body(i, ph=0):
            return i + (1 + PAIRS * ph)

        def tile_mm(pe, ps, lhs, rhs, w=P):
            for t in range(TILES):
                m = pe.matmul(ps[:, t * w:(t + 1) * w], lhs[:, t * P:(t + 1) * P], rhs, start=True, stop=True)
            return m

        def transposes(pe, ps, src, idn):
            for t in range(TILES):
                m = pe.transpose(ps[:, t * P:(t + 1) * P], src[:, t, 0:P], idn)
            return m

        def ln_stats(dve, i, u, ph):
            for h in range(2):
                for t in range(TILES):
                    m = dve.bn_stats(stats[u][:, h, t, :], xg(i, h)[:, t, :])
            m.then_inc(s_stats[u], 1)
            dve.wait_ge(s_stats[u], body(i, ph))
            dve.tensor_tensor(msum[u][:, :, :], stats[u][:, :, :, 1], stats[u][:, :, :, 4], ALU.add)
            dve.tensor_tensor(mdif[u][:, :, :], stats[u][:, :, :, 1], stats[u][:, :, :, 4], ALU.subtract)
            dve.tensor_tensor(m2[u][:, :, :], stats[u][:, :, :, 2], stats[u][:, :, :, 5], ALU.add).then_inc(s_mom[u], 1)
            dve.wait_ge(s_mom[u], body(i, ph))
            dve.tensor_scalar(mean[u][:, :, :], msum[u][:, :, :], 0.5, None, ALU.mult)
            dve.scalar_tensor_tensor(out=mdif[u][:, :, :], in0=mdif[u][:, :, :], scalar=0.25, in1=mdif[u][:, :, :],
                                     op0=ALU.mult, op1=ALU.mult).then_inc(s_mean[u], 1)
            dve.wait_ge(s_mean[u], body(i, ph))
            dve.scalar_tensor_tensor(out=var[u][:, :, :], in0=m2[u][:, :, :], scalar=1.0 / D, in1=mdif[u][:, :, :],
                                     op0=ALU.mult, op1=ALU.add).then_inc(s_mv[u], 1)
            dve.wait_ge(s_mv[u], body(i, ph))
            dve.tensor_scalar(ve[u][:, :, :], var[u][:, :, :], LN_EPS, None, ALU.add).then_inc(s_ve[u], 1)

        def ln_gpsimd(pool, i, u, ph):
            pool.wait_ge(s_ve[u], body(i, ph))
            for h in range(2):
                pool.tensor_tensor(rstd[u][:, h, :], ve[u][:, h, :], neg_half[:, :], ALU.pow).then_inc(s_rstd[u], 1)

        def ln_root_scalar(act, i, u, ph):
            act.wait_ge(s_ve[u], body(i, ph))
            act.activation(ve[u][:, :, :], ve[u][:, :, :], ACT.Sqrt).then_inc(s_root[u], 1)

        def ln_root_vector(dve, i, u, ph):
            dve.wait_ge(s_root[u], body(i) if u else i)
            for h in range(2):
                dve.reciprocal(rstd[u][:, h, :], ve[u][:, h, :]).then_inc(s_rstd[u], 1)

        def ln_apply(dve, i, u, ph, dst):
            for h in range(2):
                dve.wait_ge(s_rstd[u], n(i, h, ph))
                for t in range(TILES):
                    m = dve.tensor_scalar(dst[h][:, t, 0:D], xg(i, h)[:, t, :], mean[u][:, h, t:t + 1],
                                          rstd[u][:, h, t:t + 1], ALU.subtract, ALU.mult)
                m.then_inc(s_xn[u], 1)

        def xt_tensor(pe, i, u, ph, src, k, banks):
            for h in range(2):
                pe.wait_ge(s_xn[u], n(i, h, ph))
                transposes(pe, banks(h), src[h], ident).then_inc(s_xtr[u], 1)

        def xt_scalar(act, i, u, k, dst, banks):
            for h in range(2):
                act.wait_ge(s_xtr[u], n(i, h, k))
                act.activation(dst[h], banks(h)[:, :], ACT.Copy).then_inc(s_xt[u], 1)

        block = ctx.enter_context(nc.Block())

        def quant_ln_vector(dve, i, p):
            if p:
                dve.wait_ge(s_xl, (2 if isinstance(i, int) and i == 0 else GROUPS) + XL_AHEAD)
            ln_stats(dve, i, 0, p)

        def quant_apply_vector(dve, i, p):
            ln_apply(dve, i, 0, p, qxn)

        def quant_max_vector(dve, i, p):
            for h in range(2):
                dve.wait_ge(s_xn[0], n(i, h, p))
                dve.tensor_reduce(amax[h][:, :], qxn[h], AX.X, ALU.max, apply_absolute_value=True).then_inc(s_amax, 1)

        def quant_round_vector(dve, i, p):
            for h in range(2):
                dve.wait_ge(s_amax, n(i, h, p))
                dve.tensor_scalar(qs[h][:, :], amax[h][:, :], Q_EPS, 1.0 / 127.0, ALU.max, ALU.mult).then_inc(s_qs, 1)
            for h in range(2):
                dve.wait_ge(s_qs, n(i, h, p))
                dve.reciprocal(qinv[h][:, :], qs[h][:, :]).then_inc(s_qinv, 1)
            for h in range(2):
                dve.wait_ge(s_qinv, n(i, h, p))
                for t in range(TILES):
                    m = dve.tensor_scalar(qt[h][:, t, :], qxn[h][:, t, :], qinv[h][:, t:t + 1], MAGIC,
                                          ALU.mult, ALU.add)
                m.then_inc(s_qmul, 1)

        def quant_clip_vector(dve, i, p):
            for h in range(2):
                dve.wait_ge(s_qmul, n(i, h, p))
                dve.tensor_scalar(qt[h][:, :, :], qt[h][:, :, :], MAGIC - 128.0, MAGIC + 127.0,
                                  ALU.max, ALU.min).then_inc(s_qclip, 1)
            for h in range(2):
                dve.wait_ge(s_qclip, n(i, h, p))
                dve.tensor_scalar(qi[h][:, :, :], qt[h][:, :, :], -MAGIC, None, ALU.add).then_inc(s_qi, 1)

        def quant_add_vector(dve, i, p):
            for h in range(2):
                dve.wait_ge(s_qy, n(i, h, p))
                dve.wait_ge(s_qxb, n(i, h, p))
                for t in range(TILES):
                    m = dve.scalar_tensor_tensor(out=qt[h][:, t, :], in0=pb(h, 0)[:, t * P:(t + 1) * P],
                                                 scalar=qs[h][:, t:t + 1], in1=half_ws[:, t, :],
                                                 op0=ALU.mult, op1=ALU.mult)
                m.then_inc(s_qz, 1)
            for h in range(2):
                dve.wait_ge(s_qz, n(i, h, p))
                dve.tensor_tensor(xg(i, h), xg(i, h), qt[h][:, :, :], ALU.add).then_inc(s_xq, 1)

        def quant_gpsimd(pool, i, p):
            for h in range(2):
                pool.wait_ge(s_xn[0], n(i, h, p))
                pool.tensor_tensor(xg(i, h), xg(i, h), half_qb[:, :, :], ALU.add).then_inc(s_qxb, 1)

        def quant_tensor(pe, i, p):
            for h in range(2):
                pe.wait_ge(s_qi, n(i, h, p))
                transposes(pe, pb(h, 0)[:, 0:GROUP // 2].bitcast(BF16), qi[h], ident_bf[:, :]).then_inc(s_qtr, 1)
            for h in range(2):
                pe.wait_ge(s_qit, n(i, h, p))
                tile_mm(pe, pb(h, 0), qit[h], wq[:, :]).then_inc(s_qy, 1)

        def quant_scalar(act, i, p):
            for h in range(2):
                act.wait_ge(s_qtr, n(i, h, p))
                act.activation(qit[h][:, :], pb(h, 0)[:, 0:GROUP // 2].bitcast(BF16), ACT.Copy).then_inc(s_qit, 1)

        def front_ln_vector(dve, i):
            dve.wait_ge(s_xq, n(i, 1))
            dve.memset(scratch2[0][:, :], 0.0)
            ln_stats(dve, i, 1, 0)

        def front_norm_vector(dve, i):
            dve.wait_ge(s_rstd[1], n(i, 1))
            dve.tensor_tensor(ms[:, :, :], rstd[1][:, :, :], rstd[1][:, :, :], ALU.mult).then_inc(s_ms, 1)
            dve.wait_ge(s_ms, 3 * i + 1)
            dve.tensor_tensor(ms[:, :, :], ms[:, :, :], var[1][:, :, :], ALU.mult).then_inc(s_ms, 1)
            dve.wait_ge(s_ms, 3 * i + 2)
            dve.tensor_scalar(ms[:, :, :], ms[:, :, :], RMS_EPS, None, ALU.add).then_inc(s_ms, 1)
            ln_apply(dve, i, 1, 0, xn)

        def front_conv_vector(dve, i):
            for k in range(PAD):
                for h in range(2):
                    dve.wait_ge(s_xp, n(i, h))
                    if k:
                        dve.wait_ge(s_conv, i * (2 * PAD) + (2 * (k - 1) + h + 1))
                    dve.scalar_tensor_tensor(out=xc[h][:, :, :], in0=xp[h][:, :, k:k + S],
                                             scalar=cols[:, CW0 + k:CW0 + k + 1], in1=xc[h][:, :, :],
                                             op0=ALU.mult, op1=ALU.add).then_inc(s_conv, 1)

        def front_decay_vector(dve, i):
            for h in range(2):
                dve.wait_ge(s_a, n(i, h))
                dve.scalar_tensor_tensor(out=bufD[h][:, :], in0=bufA[h][:, :], scalar=-1.0, in1=bufA[h][:, :],
                                         op0=ALU.mult, op1=ALU.mult).then_inc(s_a2, 1)
            for h in range(2):
                dve.wait_ge(s_a2, n(i, h))
                dve.tensor_scalar(bufD[h][:, :], bufD[h][:, :], 1.0, 1e-12, ALU.add, ALU.max).then_inc(s_om, 1)

        def front_scan_vector(dve, i):
            for h in range(2):
                dve.wait_ge(s_b, n(i, h))
                for b in range(SEQS):
                    m = dve.tensor_tensor_scan(bufE[h][:, b * S:(b + 1) * S], bufA[h][:, b * S:(b + 1) * S],
                                               bufB[h][:, b * S:(b + 1) * S], 0.0, ALU.mult, ALU.add)
                m.then_inc(s_scan, 1)

        def front_gated_vector(dve, i):
            for h in range(2):
                dve.wait_ge(s_scan, n(i, h))
                dve.wait_ge(s_yb, n(i, h))
                dve.tensor_tensor(bufE[h][:, :], bufE[h][:, :], bufC[h][:, :], ALU.mult).then_inc(s_hy, 1)

        def front_mixed_vector(dve, i):
            for h in range(2):
                dve.wait_ge(s_mix, n(i, h))
                dve.tensor_tensor(h1[h][:, :, :], xn[h][:, :, 0:D],
                                  pb(h, 1)[:, :].rearrange("p (t d) -> p t d", t=TILES), ALU.add).then_inc(s_h1, 1)

        def ffn_hidden_vector(dve, i, j):
            for h in range(2):
                dve.wait_ge(s_gelu, i * (2 * HJ) + (2 * j + h + 1))
                dve.wait_ge(s_fu, i * (2 * HJ) + (2 * j + h + 1))
                dve.tensor_tensor(hid[h][:, j, :], gate[h][:, j, :], pb(h, 3)[:, :], ALU.mult).then_inc(s_hid, 1)

        def ffn_add_vector(dve, i):
            for h in range(2):
                dve.wait_ge(s_ffn, n(i, h))
                dve.wait_ge(s_xh, n(i, h))
                dve.tensor_tensor(x[:, i, h, :], x[:, i, h, :], pb(h, 2)[:, :], ALU.add).then_inc(s_xl, 1)

        def front_norm_gpsimd(pool, i):
            pool.wait_ge(s_ms, 3 * i + 3)
            for h in range(2):
                pool.tensor_tensor(r2[:, h, :], ms[:, h, :], neg_half[:, :], ALU.pow).then_inc(s_r2, 1)

        def front_input_gpsimd(pool, i):
            for h in range(2):
                pool.wait_ge(s_sig, n(i, h))
                pool.tensor_tensor(bufB[h][:, :].rearrange("p (b s) -> p b s", b=SEQS),
                                   seqs(bufB[h]), xc[h][:, :, :], ALU.mult).then_inc(s_ix, 1)
            for h in range(2):
                pool.wait_ge(s_sq, n(i, h))
                pool.wait_ge(s_ix, n(i, h))
                pool.tensor_tensor(bufB[h][:, :], bufD[h][:, :], bufB[h][:, :], ALU.mult).then_inc(s_b, 1)

        def front_norm2_gpsimd(pool, i):
            for h in range(2):
                pool.wait_ge(s_ss, n(i, h))
                pool.tensor_tensor(ss[h][:, :], ss[h][:, :], rms_eps[:, :], ALU.add).then_inc(s_s2a, 1)
                pool.wait_ge(s_s2a, n(i, h))
                pool.tensor_tensor(r2[:, h, :], ss[h][:, :], neg_half[:, :], ALU.pow).then_inc(s_s2, 1)
            for h in range(2):
                pool.wait_ge(s_h1, n(i, h))
                pool.tensor_tensor(xg(i, h), xg(i, h), h1[h][:, :, :], ALU.add).then_inc(s_xh, 1)

        def front_in_tensor(pe, i):
            for h in range(2):
                pe.wait_ge(s_t, n(i, h))
                transposes(pe, pb(h, 0), tt[h], ident).then_inc(s_ttr, 1)
            for h in range(2):
                pe.wait_ge(s_tx, n(i, h))
                pe.matmul(pb(h, 1)[:, :], wx_n[:, 0, :], xt[h][:, :], start=True, stop=True).then_inc(s_xb, 1)
            for h in range(2):
                pe.matmul(pb(h, 0)[:, :], wx_n[:, 1, :], xt[h][:, :], start=True, stop=True).then_inc(s_y, 1)

        def front_gates_tensor(pe, i):
            for h in range(2):
                pe.wait_ge(s_conv, i * (2 * PAD) + (2 * (PAD - 1) + h + 1))
                pe.matmul(pb(h, 1)[:, :], w_sq[:, 3, :], xc[h][:, :, :], start=True, stop=True)
                pe.wait_ge(s_yb, n(i, h))
                pe.matmul(pb(h, 0)[:, :], w_sq[:, 2, :], xc[h][:, :, :], start=True, stop=True).then_inc(s_gates, 1)

        def front_mix_tensor(pe, i):
            for h in range(2):
                pe.wait_ge(s_hy, n(i, h))
                tile_mm(pe, pb(h, 1), bufE[h], w_sq[:, 4, :]).then_inc(s_mix, 1)

        def front_out_tensor(pe, i, q):
            for h in range(2):
                pe.wait_ge(s_u, n(i, h))
                if q is not None:
                    pe.wait_ge(s_xq, n(q, h))
                transposes(pe, pb(h, 0), tt[h], ident).then_inc(s_utr, 1)

        def ffn_up_tensor(pe, i, j):
            for h in range(2):
                if j:
                    pe.wait_ge(s_gelu, i * (2 * HJ) + (2 * (j - 1) + h + 1))
                    pe.wait_ge(s_hid, i * (2 * HJ) + (2 * (j - 1) + h + 1))
                else:
                    pe.wait_ge(s_ut, n(i, h))
                    pe.wait_ge(s_xl, n(i, h))
                pe.matmul(pb(h, 2)[:, :], wgu_n[:, 0, j * P:(j + 1) * P], ut[h], start=True, stop=True).then_inc(s_fg, 1)
                pe.matmul(pb(h, 3)[:, :], wgu_n[:, 1, j * P:(j + 1) * P], ut[h], start=True, stop=True).then_inc(s_fu, 1)

        def ffn_down_tensor(pe, i):
            for h in range(2):
                pe.wait_ge(s_hid, i * (2 * HJ) + (2 * (HJ - 1) + h + 1))
                for t in range(TILES):
                    for j in range(HJ):
                        m = pe.matmul(pb(h, 2)[:, t * P:(t + 1) * P], hid[h][:, j, t * P:(t + 1) * P],
                                      w_dn[:, j, :], start=(j == 0), stop=(j == HJ - 1))
                m.then_inc(s_ffn, 1)

        def front_in_scalar(act, i):
            for h in range(2):
                act.wait_ge(s_r2, n(i, h))
                act.wait_ge(s_xn[1], n(i, h))
                for t in range(TILES):
                    m = act.activation(tt[h][:, t, :], xn[h][:, t, 0:D], ACT.Copy, scale=r2[:, h, t:t + 1])
                m.then_inc(s_t, 1)
            for h in range(2):
                act.wait_ge(s_ttr, n(i, h))
                act.activation(xt[h][:, :], pb(h, 0)[:, :], ACT.Copy).then_inc(s_tx, 1)
            for h in range(2):
                act.wait_ge(s_xb, n(i, h))
                act.activation(xp[h][:, :, PAD:], seqs(pb(h, 1)), ACT.Copy)
                act.activation(xc[h][:, :, :], seqs(pb(h, 1)), ACT.Identity, scale=cols[:, CW0 + PAD:CW0 + PAD + 1],
                               bias=cols[:, CB:CB + 1]).then_inc(s_xp, 1)
            for h in range(2):
                act.wait_ge(s_y, n(i, h))
                act.activation(bufC[h][:, :], pb(h, 0)[:, :], ACT.Gelu_apprx_tanh).then_inc(s_yb, 1)

        def front_gates_scalar(act, i):
            for h in range(2):
                act.wait_ge(s_gates, n(i, h))
                act.activation(bufA[h][:, :], pb(h, 1)[:, :], ACT.Sigmoid)
                act.activation(bufB[h][:, :], pb(h, 0)[:, :], ACT.Sigmoid).then_inc(s_sig, 1)
            for h in range(2):
                act.wait_ge(s_sig, n(i, h))
                act.activation(bufA[h][:, :], bufA[h][:, :], ACT.Exp, scale=decay[:, 0:1]).then_inc(s_a, 1)
            for h in range(2):
                act.wait_ge(s_om, n(i, h))
                act.activation(bufD[h][:, :], bufD[h][:, :], ACT.Sqrt).then_inc(s_sq, 1)

        def front_norm2_scalar(act, i):
            for h in range(2):
                act.wait_ge(s_h1, n(i, h))
                for t in range(TILES):
                    m = act.activation(bufD[h][:, t * P:(t + 1) * P], h1[h][:, t, :], ACT.Square, scale=float(D) ** -0.5,
                                       accum_out=ss[h][:, t:t + 1])
                m.then_inc(s_ss, 1)
            for h in range(2):
                act.wait_ge(s_s2, n(i, h))
                for t in range(TILES):
                    m = act.activation(tt[h][:, t, :], h1[h][:, t, :], ACT.Copy, scale=r2[:, h, t:t + 1])
                m.then_inc(s_u, 1)
            for h in range(2):
                act.wait_ge(s_utr, n(i, h))
                act.activation(ut[h], pb(h, 0)[:, :], ACT.Copy).then_inc(s_ut, 1)

        def ffn_scalar(act, i, j):
            for h in range(2):
                act.wait_ge(s_fg, i * (2 * HJ) + (2 * j + h + 1))
                act.activation(gate[h][:, j, :], pb(h, 2)[:, :], ACT.Gelu_apprx_tanh).then_inc(s_gelu, 1)

        def when(i, step, *rest):
            if i is not None:
                step(*rest[:1], i, *rest[1:])

        def quant_l0_vector(dve, q, f, m):
            when(f, front_ln_vector, dve)
            when(m, ffn_hidden_vector, dve, 0)
            when(f, front_norm_vector, dve)
            when(m, ffn_hidden_vector, dve, 1)
            when(f, front_conv_vector, dve)
            when(m, ffn_hidden_vector, dve, 2)
            when(q, quant_ln_vector, dve, 0)
            when(q, quant_apply_vector, dve, 0)
            when(q, quant_max_vector, dve, 0)
            when(f, front_decay_vector, dve)
            when(q, quant_round_vector, dve, 0)
            when(f, front_scan_vector, dve)
            when(q, quant_clip_vector, dve, 0)
            when(f, front_gated_vector, dve)
            when(m, ffn_hidden_vector, dve, 3)
            when(f, front_mixed_vector, dve)
            when(q, quant_add_vector, dve, 0)
            when(m, ffn_add_vector, dve)

        def quant_l0_gpsimd(pool, q, f, m):
            when(f, ln_gpsimd, pool, 1, 0)
            when(f, front_norm_gpsimd, pool)
            when(q, ln_gpsimd, pool, 0, 0)
            when(f, front_input_gpsimd, pool)
            when(q, quant_gpsimd, pool, 0)
            when(f, front_norm2_gpsimd, pool)

        def quant_l0_tensor(pe, q, f, m):
            when(m, ffn_up_tensor, pe, 0)
            when(m, ffn_up_tensor, pe, 1)
            when(f, front_in_tensor, pe)
            when(m, ffn_up_tensor, pe, 2)
            when(f, front_gates_tensor, pe)
            when(m, ffn_up_tensor, pe, 3)
            if q is not None and f is not None:
                pe.wait_ge(s_sig, n(f, 1))
            when(q, quant_tensor, pe, 0)
            when(f, front_mix_tensor, pe)
            when(m, ffn_down_tensor, pe)
            when(f, front_out_tensor, pe, q)

        def quant_l0_scalar(act, q, f, m):
            when(m, ffn_scalar, act, 0)
            when(m, ffn_scalar, act, 1)
            when(f, front_in_scalar, act)
            when(m, ffn_scalar, act, 2)
            when(f, front_gates_scalar, act)
            when(m, ffn_scalar, act, 3)
            when(q, quant_scalar, act, 0)
            when(f, front_norm2_scalar, act)

        def ffn_quant_vector(dve, m, q):
            quant_ln_vector(dve, q, 1)
            ffn_hidden_vector(dve, m, 0)
            quant_apply_vector(dve, q, 1)
            ffn_hidden_vector(dve, m, 1)
            quant_max_vector(dve, q, 1)
            quant_round_vector(dve, q, 1)
            ffn_hidden_vector(dve, m, 2)
            quant_clip_vector(dve, q, 1)
            ffn_hidden_vector(dve, m, 3)
            quant_add_vector(dve, q, 1)
            ffn_add_vector(dve, m)

        def ffn_quant_gpsimd(pool, m, q):
            ln_gpsimd(pool, q, 0, 1)
            quant_gpsimd(pool, q, 1)

        def ffn_quant_tensor(pe, m, q):
            for j in range(HJ):
                ffn_up_tensor(pe, m, j)
            quant_tensor(pe, q, 1)
            ffn_down_tensor(pe, m)

        def ffn_quant_scalar(act, m, q):
            for j in range(HJ):
                ffn_scalar(act, m, j)
            quant_scalar(act, q, 1)

        def in_three_steps(eng, body_of):
            body_of(eng, 1, 0, None)
            with eng.Fori(0, PAIRS - 2) as i:
                body_of(eng, i + 2, i + 1, i)
            body_of(eng, None, PAIRS - 1, PAIRS - 2)

        def route_apply_vector(dve, i, p):
            if not (isinstance(i, int) and i == 0 and p == 0):
                for h in range(2):
                    dve.wait_ge(s_scat[h], SCAT * i + SCAT * PAIRS * p)
            ln_apply(dve, i, 1, 1 + p, xn)
            for h in range(2):
                ids = consts[:, K_TOKEN:K_AWAY].rearrange("p (a h t) -> p a h t", h=2, t=TILES)[:, i, h, :]
                dve.tensor_scalar(xn[h][:, :, D], ids, 0.0, None, ALU.add)
                dve.tensor_scalar(xn2[h][:, :, D], ids, float(TOKENS), None, ALU.add).then_inc(s_ids, 1)

        def route_bias_vector(dve, i, p):
            for h in range(2):
                dve.wait_ge(s_rl, n(i, h, p))
                dve.tensor_tensor(probs[h][:, :, :], rb(h, 1)[:, 0:TILES * E_ROUTED].rearrange("p (t e) -> p t e", t=TILES),
                                  rows[:, None, R_RB:R_RB + E_ROUTED].to_broadcast([P, TILES, E_ROUTED]),
                                  ALU.add).then_inc(s_rlb, 1)

        def route_rank_vector(dve, i, p):
            for h in range(2):
                dve.wait_ge(s_pr, n(i, h, p))
                pj = probs[h][:, :, None, :].to_broadcast([P, TILES, E_ROUTED, E_ROUTED])
                pe_ = probs[h][:, :, :, None].to_broadcast([P, TILES, E_ROUTED, E_ROUTED])
                dve.tensor_tensor(gt[h][:, :, :, :], pj, pe_, ALU.is_gt)
                dve.tensor_tensor(eq[h][:, :, :, :], pj, pe_, ALU.is_equal).then_inc(s_cmp, 1)
            for h in range(2):
                dve.wait_ge(s_cmp, n(i, h, p))
                dve.tensor_tensor(eq[h][:, :, :, :], eq[h][:, :, :, :],
                                  lower[:, None, :, :].to_broadcast([P, TILES, E_ROUTED, E_ROUTED]),
                                  ALU.mult).then_inc(s_cml, 1)
            for h in range(2):
                dve.wait_ge(s_cml, n(i, h, p))
                dve.tensor_tensor(gt[h][:, :, :, :], gt[h][:, :, :, :], eq[h][:, :, :, :], ALU.add).then_inc(s_cms, 1)
            for h in range(2):
                dve.wait_ge(s_cms, n(i, h, p))
                dve.tensor_reduce(rank[h][:, :, :], gt[h][:, :, :, :], AX.X, ALU.add).then_inc(s_rank, 1)
            for h in range(2):
                dve.wait_ge(s_rank, n(i, h, p))
                for r in range(TOP_K):
                    dve.tensor_scalar(first2[h][:, r, :, :], rank[h][:, :, :], float(r), None, ALU.is_equal)
                dve.tensor_scalar(chosen[h][:, :, :], rank[h][:, :, :], float(TOP_K), None, ALU.is_lt).then_inc(s_first2, 1)

        def route_rows_vector(dve, i, p):
            for h in range(2):
                dve.wait_ge(s_pref, n(i, h, p))
                dve.wait_ge(s_slot, 2 * i + (h + 1 + (GROUPS + 1) * p))
                pref = rb(h, 1)[:, 0:(TILES + 1) * E_ROUTED].rearrange("p (t e) -> p t e", e=E_ROUTED)
                dve.tensor_tensor(slot[h][:, :, :], pref[:, 0:TILES, :],
                                  carry[h][:, None, :].to_broadcast([P, TILES, E_ROUTED]), ALU.add)
                dve.tensor_tensor(carry[1 - h][:, :], carry[h][:, :], pref[:, TILES, :], ALU.add).then_inc(s_slot, 1)
            for h in range(2):
                dve.wait_ge(s_slot, 2 * i + (h + 2 + (GROUPS + 1) * p))
                bc = [P, TOP_K, TILES, E_ROUTED]
                dve.tensor_tensor(slotf[h][:, :, :, :], first2[h][:, :, :, :], slot[h][:, None, :, :].to_broadcast(bc), ALU.mult)
                for r in range(TOP_K):
                    m = dve.scalar_tensor_tensor(out=scoref[h][:, r, :, :], in0=first2[h][:, r, :, :], scalar=0.5,
                                                 in1=probs[h][:, :, :], op0=ALU.mult, op1=ALU.mult)
                m.then_inc(s_prod, 1)
            for h in range(2):
                dve.wait_ge(s_prod, n(i, h, p))
                dve.tensor_reduce(sidx[h][:, :], slotf[h][:, :, :, :].rearrange("p r t e -> p (r t) e"), AX.X, ALU.add)
                dve.tensor_reduce(score[:, i, h, :], scoref[h][:, :, :, :].rearrange("p r t e -> p (r t) e"),
                                  AX.X, ALU.add).then_inc(s_idx, 1)

        def shared_hidden_vector(dve, i, p, j):
            for h in range(2):
                dve.wait_ge(s_silu, 2 * IJ * i + (2 * j + h + 1 + GROUPS * IJ * p))
                dve.wait_ge(s_su, 2 * IJ * i + (2 * j + h + 1 + GROUPS * IJ * p))
                dve.tensor_tensor(hid[h][:, j, :], gate[h][:, j, :], rb(h, 1 - j)[:, :], ALU.mult).then_inc(s_sh, 1)

        def shared_add_vector(dve, i, p):
            for h in range(2):
                dve.wait_ge(s_sd, n(i, h, p))
                dve.scalar_tensor_tensor(out=x[:, i, h, :], in0=rb(h, 1)[:, :], scalar=0.5, in1=x[:, i, h, :],
                                         op0=ALU.mult, op1=ALU.add).then_inc(s_xsh, 1)

        def route_gpsimd(pool, i, p):
            for h in range(2):
                pool.wait_ge(s_idx, n(i, h, p))
                pool.wait_ge(s_xn2, n(i, h, p))
                pool.sem_inc(s_carry, 1)
                for r in range(TOP_K):
                    for t in range(TILES):
                        k = r * TILES + t
                        pool.indirect_dma_start(out=rows_by_expert, out_offset=bass.IndirectOffsetOnAxis(
                            ap=sidx[h][:, k:k + 1], axis=0), in_=(xn, xn2)[r][h][:, t, :], in_offset=None).then_inc(s_scat[h], 16)

        def route_logits_tensor(pe, i, p):
            xt_tensor(pe, i, 1, 1 + p, xn, p, lambda h: rb(h, 0))
            for h in range(2):
                pe.wait_ge(s_xt[1], n(i, h, p))
                tile_mm(pe, rb(h, 1), xt[h], w_r[:, :], E_ROUTED).then_inc(s_rl, 1)

        def shared_gate_tensor(pe, i, p, j, halves_of=(0, 1)):
            for h in halves_of:
                if j:
                    pe.wait_ge(s_silu, 2 * IJ * i + (2 * (j - 1) + h + 1 + GROUPS * IJ * p))
                pe.matmul(rb(h, 0)[:, :], e_gu[:, SHARED, 0, j * P:(j + 1) * P], xt[h][:, :],
                          start=True, stop=True).then_inc(s_sg, 1)

        def shared_up_tensor(pe, i, p, j, halves_of=(0, 1)):
            for h in halves_of:
                if j:
                    pe.wait_ge(s_silu, 2 * IJ * i + (2 * (IJ - 1) + h + 1 + GROUPS * IJ * p))
                else:
                    pe.wait_ge(s_slot, 2 * i + (h + 2 + (GROUPS + 1) * p))
                pe.matmul(rb(h, 1 - j)[:, :], e_gu[:, SHARED, 1, j * P:(j + 1) * P], xt[h][:, :],
                          start=True, stop=True).then_inc(s_su, 1)

        def route_counts_tensor(pe, i, p):
            for h in range(2):
                pe.wait_ge(s_first2, n(i, h, p))
                for t in range(TILES + 1):
                    dst = rb(h, 1)[:, t * E_ROUTED:(t + 1) * E_ROUTED]
                    for u in range(t):
                        m = pe.matmul(dst, ones_bf[:, :], chosen[h][:, u, :], start=(u == 0), stop=(u == t - 1 and t == TILES))
                    if t < TILES:
                        pe.matmul(dst, before_bf[:, :], chosen[h][:, t, :], start=(t == 0), stop=True)
                m.then_inc(s_pref, 1)

        def shared_down_tensor(pe, i, p, halves_of=(0, 1), tiles=range(TILES)):
            for h in halves_of:
                if tiles[0] == 0:
                    pe.wait_ge(s_sh, 2 * IJ * i + (2 * (IJ - 1) + h + 1 + GROUPS * IJ * p))
                for t in tiles:
                    for j in range(IJ):
                        m = pe.matmul(rb(h, 1)[:, t * P:(t + 1) * P], hid[h][:, j, t * P:(t + 1) * P],
                                      e_dn[:, SHARED, j, :], start=(j == 0), stop=(j == IJ - 1))
                if tiles[-1] == TILES - 1:
                    m.then_inc(s_sd, 1)

        def route_scalar(act, i, p):
            xt_scalar(act, i, 1, p, [xt[h][:, :] for h in range(2)], lambda h: rb(h, 0))
            for h in range(2):
                act.wait_ge(s_rlb, n(i, h, p))
                act.activation(probs[h][:, :, :], probs[h][:, :, :], ACT.Sigmoid).then_inc(s_pr, 1)
            for h in range(2):
                act.wait_ge(s_ids, n(i, h, p))
                act.activation(xn2[h][:, :, 0:D], xn[h][:, :, 0:D], ACT.Copy).then_inc(s_xn2, 1)

        def shared_scalar(act, i, p):
            for j in range(IJ):
                for h in range(2):
                    act.wait_ge(s_sg, 2 * IJ * i + (2 * j + h + 1 + GROUPS * IJ * p))
                    act.activation(gate[h][:, j, :], rb(h, 0)[:, :], ACT.Silu).then_inc(s_silu, 1)

        TAB = 9

        def tables_vector(dve, p):
            k = [TAB * p]

            def done(ins):
                k[0] += 1
                ins.then_inc(s_tab, 1)
                dve.wait_ge(s_tab, k[0])

            def over_e(a, w):
                return a[:, None, :].to_broadcast([P, w, E_ROUTED])

            dve.wait_ge(s_slot, (GROUPS + 1) * (p + 1))
            done(dve.tensor_tensor(cnt[:, :], carry[0][:, :], region, ALU.subtract))
            dve.tensor_tensor(padidx[:, :], cnt[:, :], consts[:, K_PAD:K_PAD + E_ROUTED], ALU.add)
            done(dve.tensor_scalar(tl[:, 0, :], cnt[:, :], 1.0 / P, (P / 2 - 0.5) / P, ALU.mult, ALU.add))
            done(dve.tensor_scalar(tl[:, 1, :], tl[:, 0, :], MAGIC, None, ALU.add))
            done(dve.tensor_scalar(tiles_e[:, :], tl[:, 1, :], -MAGIC, None, ALU.add))
            done(dve.tensor_tensor_scan(cum[:, :], ones8[:, :], tiles_e[:, :], 0.0, ALU.mult, ALU.add))
            done(dve.tensor_tensor(cmp[:, :, :], consts[:, K_J:K_J + NT, None].to_broadcast([P, NT, E_ROUTED]),
                                   over_e(cum, NT), ALU.is_ge))
            dve.tensor_tensor(cmpt[:, :, :], cmp[:, :, :], over_e(tiles_e, NT), ALU.mult)
            dve.tensor_reduce(etab[:, :, :].rearrange("p a b -> p (a b)"), cmp[:, :, :], AX.X, ALU.add)
            done(dve.tensor_reduce(etabf[:, :], cmp[:, :, :], AX.X, ALU.add))
            dve.tensor_reduce(stab[:, :], cmpt[:, :, :], AX.X, ALU.add)
            done(dve.scalar_tensor_tensor(out=rtabf[:, :], in0=etabf[:, :], scalar=float(REGION),
                                          in1=consts[:, K_J128:K_J128 + NT], op0=ALU.mult, op1=ALU.add))
            done(dve.scalar_tensor_tensor(out=rtab[:, :, :].rearrange("p a b -> p (a b)"), in0=stab[:, :], scalar=-float(P),
                                          in1=rtabf[:, :], op0=ALU.mult, op1=ALU.add))

        away = consts[:, K_AWAY:]

        def padding_rows(pool, n):
            if n == 1:
                pool.wait_ge(s_zfill, 16 * E_ROUTED)
            for e in range(E_ROUTED):
                pool.memset(tin[e][:, 0:D], 0.0)
            for e in range(E_ROUTED):
                k = (E_ROUTED if n == 0 else 0) + e
                m = pool.tensor_tensor(tin[e][:, D:ROW], away[:, k:k + 1], zero_col[:, :], ALU.add)
            m.then_inc(s_padding, 1)

        def pad_sync(sp_, p):
            sp_.wait_ge(s_tab, TAB * p + 2)
            sp_.wait_ge(s_padding, p + 2)
            for e in range(E_ROUTED):
                row = sp_.value_load(padidx[0:1, e:e + 1], min_val=0, max_val=E_ROUTED * REGION - P)
                sp_.dma_start(rows_by_expert[bass.ds(row, P), :], tin[e][:, :]).then_inc(s_pad, 16)

        LAG_ST = 4
        AHEAD = {"s_thid": 1, "s_thc": 2, "s_tht": 1, "s_tyc": LAG_ST, "s_tsil": 1, "s_tdn": 3}

        def lag(i, k, d):
            b, kk = (i, k - d) if k >= d else (i - 1, k - d + BLK)
            if isinstance(i, int) and not 0 <= b < NB:
                return None
            return b, kk

        def step_value(eng, i, k, c):
            v = i * BLK + (k + c)
            return v if isinstance(v, int) else eng.snap(v)

        def over_blocks(eng, block_of):
            block_of(0)
            with eng.Fori(1, NB) as i:
                block_of(i)
            block_of(NB)

        def stages(i, k, *lagged):
            for d, stage in lagged:
                where = lag(i, k, d)
                if where:
                    stage(*where)

        def experts_sync(sp_, p):
            pad_sync(sp_, p)
            sp_.wait_ge(s_scat[0], SCAT * PAIRS * (p + 1))
            sp_.wait_ge(s_scat[1], SCAT * PAIRS * (p + 1))
            sp_.wait_ge(s_pad, 16 * E_ROUTED * (p + 1))
            sp_.wait_ge(s_tab, TAB * (p + 1))

            def block_of(i):
                for k in range(BLK):
                    if isinstance(i, int) and i >= NB:
                        continue
                    row = sp_.value_load(rtab[0:1, i, k:k + 1], min_val=0, max_val=E_ROUTED * REGION + (E_ROUTED - 1) * P)
                    if not (isinstance(i, int) and i == 0 and p == 0):
                        sp_.wait_ge(s_tdst, i * BLK + (k + 1 - BLK + NT * p))
                    sp_.dma_start(tin[k][:, :], rows_by_expert[bass.ds(row, P), :]).then_inc(s_in[k], 16)

            over_blocks(sp_, block_of)

        def experts_tensor(pe, p):
            pe.wait_ge(s_tab, TAB * (p + 1))
            pe.wait_ge(s_xsh, GROUPS * (p + 1))

            def block_of(i):
                loaded = i * 16 + 16 * (1 + NB * p)
                loaded = loaded if isinstance(i, int) else pe.snap(loaded)
                experts = {}

                def expert(b, k):
                    if (b is i, k) not in experts:
                        experts[b is i, k] = pe.value_load(etab[0:1, b, k:k + 1], min_val=0, max_val=E_ROUTED)
                    return experts[b is i, k]

                for k in range(BLK):
                    v = step_value(pe, i, k, NT * p)

                    def transpose_in(b, kk):
                        pe.wait_ge(s_in[kk], loaded)
                        pe.transpose(bank[2 + kk % 2][:, 0:P], tin[kk][:, 0:D], ident).then_inc(s_tt, 1)

                    def up(b, kk):
                        e = expert(b, kk)
                        pe.wait_ge(s_ttc, v)
                        pe.matmul(bank[kk % 2][:, :], tint[kk % 2][:, :],
                                  e_gu[:, e, :, :].rearrange("p a n -> p (a n)"), start=True, stop=True).then_inc(s_tgu, 1)

                    def transpose_hidden(b, kk):
                        pe.wait_ge(s_thid, v)
                        for j in range(IJ):
                            m = pe.transpose(bank[4 + kk % 2][:, j * P:(j + 1) * P], thid[kk % 2][:, j * P:(j + 1) * P], ident)
                        m.then_inc(s_tht, 1)

                    def down(b, kk):
                        e = expert(b, kk)
                        pe.wait_ge(s_thc, v)
                        if isinstance(i, int) and i == NB:
                            pe.wait_ge(s_tyc, b * BLK + kk + NT * p - 1 + AHEAD["s_tyc"])
                        for j in range(IJ):
                            m = pe.matmul(bank[6 + kk % 2][:, 0:P], thidt[kk % 2][:, j, :], e_dn[:, e, j, :],
                                          start=(j == 0), stop=(j == IJ - 1))
                        m.then_inc(s_tdn, 1)

                    stages(i, k, (0, transpose_in), (1, up), (2, transpose_hidden), (3, down))

            over_blocks(pe, block_of)

        def experts_scalar(act, p):
            def block_of(i):
                for k in range(BLK):
                    v = step_value(act, i, k, NT * p)

                    def silu(b, kk):
                        act.wait_ge(s_tgu, v)
                        act.activation(tsil[kk % 2][:, :], bank[kk % 2][:, 0:INNER], ACT.Silu).then_inc(s_tsil, 1)

                    def copy_hidden(b, kk):
                        act.wait_ge(s_tht, v)
                        act.activation(thidt[kk % 2][:, :, :], bank[4 + kk % 2][:, 0:INNER].rearrange("p (j c) -> p j c", j=IJ),
                                       ACT.Copy).then_inc(s_thc, 1)

                    stages(i, k, (1, silu), (2, copy_hidden))

            over_blocks(act, block_of)

        def experts_gpsimd(pool, p):
            def block_of(i):
                for k in range(BLK):
                    v = step_value(pool, i, k, NT * p + 1)

                    def store(b, kk):
                        pool.wait_ge(s_tyc, v)
                        pool.sem_inc(s_carry, 1)
                        pool.indirect_dma_start(out=rows_done, out_offset=bass.IndirectOffsetOnAxis(
                            ap=tdst[kk][:, 0:1], axis=0), in_=tout[kk % OUT_RING][:, :], in_offset=None
                            ).then_inc(s_st[kk % OUT_RING], 16)

                    stages(i, k, (LAG_ST, store))

            over_blocks(pool, block_of)

        def experts_vector(dve, p):
            def block_of(i):
                for k in range(BLK):
                    v = step_value(dve, i, k, NT * p + 1)

                    def copy_in(b, kk):
                        dve.wait_ge(s_tt, v)
                        dve.tensor_copy(tdst[kk][:, :], tin[kk][:, D:ROW]).then_inc(s_tdst, 1)
                        dve.tensor_copy(tint[kk % 2][:, :], bank[2 + kk % 2][:, 0:P]).then_inc(s_ttc, 1)

                    def hidden(b, kk):
                        dve.wait_ge(s_tsil, v)
                        dve.tensor_tensor(thid[kk % 2][:, :], tsil[kk % 2][:, :], bank[kk % 2][:, INNER:2 * INNER],
                                          ALU.mult).then_inc(s_thid, 1)

                    def copy_out(b, kk):
                        dve.wait_ge(s_tdn, v)
                        turns = BLK // OUT_RING
                        if not (isinstance(b, int) and b == 0 and p == 0 and kk < OUT_RING):
                            dve.wait_ge(s_st[kk % OUT_RING], b * (16 * turns) + 16 * (kk // OUT_RING + turns * NB * p))
                        dve.tensor_copy(tout[kk % OUT_RING][:, :], bank[6 + kk % 2][:, 0:P]).then_inc(s_tyc, 1)

                    stages(i, k, (0, copy_in), (1, hidden), (3, copy_out))

            over_blocks(dve, block_of)

        def stored(eng, p):
            for k in range(OUT_RING):
                eng.wait_ge(s_st[k], 16 * (NT // OUT_RING) * (p + 1))

        def fetch_sync(sp_, i, p, after=None):
            for h in range(2):
                if after is not None:
                    sp_.wait_ge(s_add1, n(after, h, p))
                for r in range(TOP_K):
                    src = rows_done[r * TOKENS:(r + 1) * TOKENS, :].rearrange("(a h t p) d -> p a h t d", h=2, t=TILES, p=P)
                    sp_.dma_start(got[h][:, r * TILES:(r + 1) * TILES, :], src[:, i, h, :, :]).then_inc(s_got[h], 16)

        def combine_vector(dve, i, p):
            for h in range(2):
                for r in range(TOP_K):
                    if r == 0:
                        dve.wait_ge(s_got[h], 16 * TOP_K * (i + (1 + PAIRS * p)))
                    else:
                        dve.wait_ge(s_add0, n(i, h, p))
                    for t in range(TILES):
                        k = r * TILES + t
                        m = dve.scalar_tensor_tensor(out=xg(i, h)[:, t, :], in0=got[h][:, k, :], scalar=score[:, i, h, k:k + 1],
                                                     in1=xg(i, h)[:, t, :], op0=ALU.mult, op1=ALU.add)
                    m.then_inc(s_add1 if r else s_add0, 1)

        COPIES = LEVELS + 1

        def halves(buf, w):
            return buf[:, :].rearrange("p (b two r) -> p b two r", two=2, r=w)

        def gla_gates_vector(dve, i):
            for h in range(2):
                dve.wait_ge(s_v, n(i, h))
                dve.tensor_tensor(bufC[h][:, :].rearrange("p (t d) -> p t d", t=TILES),
                                  gb(h, 0)[:, :].rearrange("p (t d) -> p t d", t=TILES),
                                  rows[:, None, R_BV:R_BV + P].to_broadcast([P, TILES, P]), ALU.add).then_inc(s_vb, 1)
            for h in range(2):
                dve.wait_ge(s_qk, n(i, h))
                dve.tensor_tensor(bufA[h][:, :], bufD[h][:, :], tseg[h][:, :], ALU.mult).then_inc(s_q0, 1)

        def gla_level_vector(dve, i, lv):
            w = 1 << lv
            for h in range(2):
                dve.wait_ge(s_lvl, i * (2 * LEVELS) + (2 * lv + h + 1))
                if lv:
                    dve.wait_ge(s_upd, i * (2 * LEVELS) + (2 * (lv - 1) + h + 1))
                    dve.wait_ge(s_pred, i * (2 * COPIES) + (2 * (lv - 1) + h + 1))
                else:
                    dve.wait_ge(s_dg, n(i, h))
                cur, nxt = (tseg[h], tseg2[h]) if lv % 2 == 0 else (tseg2[h], tseg[h])
                seg = cur[:, 0:GROUP // w].rearrange("p (b two) -> p b two", two=2)
                nb = GROUP // (2 * w)
                dve.tensor_tensor(halves(bufA[h], w)[:, :, 1, :], halves(bufA[h], w)[:, :, 1, :],
                                  seg[:, :, 0:1].to_broadcast([P, nb, w]), ALU.mult)
                m = dve.tensor_tensor(halves(bufB[h], w)[:, :, 0, :], halves(bufB[h], w)[:, :, 0, :],
                                      seg[:, :, 1:2].to_broadcast([P, nb, w]), ALU.mult)
                if lv < LEVELS - 1:
                    m = dve.tensor_tensor(nxt[:, 0:nb], seg[:, :, 0], seg[:, :, 1], ALU.mult)
                m.then_inc(s_upd, 1)
                if lv == 0:
                    m = dve.copy_predicated(at[h][:, :], masks[:, (LEVELS - 1) * 256:], gb(h, 1)[:, :])
                else:
                    m = dve.copy_predicated(
                        halves(at[h], w // 2)[:, :, 1, :],
                        masks[:, (lv - 1) * 256:lv * 256].rearrange("p (b r) -> p b r", r=w // 2),
                        gb(h, (lv - 1) % 2)[:, 0:256].rearrange("p (b r) -> p b r", r=w // 2))
                m.then_inc(s_pred, 1)

        def gla_last_vector(dve, i):
            for h in range(2):
                dve.wait_ge(s_pred, i * (2 * COPIES) + (2 * (LEVELS - 1) + h + 1))
                dve.tensor_copy(halves(at[h], P // 2)[0:P // 2, :, 1, :],
                                gb(h, (LEVELS - 1) % 2)[0:P // 2, 0:256].rearrange("p (c r) -> p c r", c=TILES)
                                ).then_inc(s_pred, 1)

        def gla_add_vector(dve, i):
            for h in range(2):
                dve.wait_ge(s_op, n(i, h))
                dve.wait_ge(s_xbo, n(i, h))
                dve.tensor_tensor(x[:, i, h, :], x[:, i, h, :], gb(h, 1)[:, :], ALU.add).then_inc(s_x, 1)

        def gla_gpsimd(pool, i):
            for h in range(2):
                pool.wait_ge(s_xn[0], n(i, h, 2))
                pool.tensor_tensor(xg(i, h), xg(i, h), rows[:, None, R_BO:R_BO + P].to_broadcast([P, TILES, P]),
                                   ALU.add).then_inc(s_xbo, 1)

        def gla_in_tensor(pe, i):
            xt_tensor(pe, i, 0, 2, tt, 0, lambda h: gb(h, 0))
            for h in range(2):
                pe.wait_ge(s_xt[0], n(i, h))
                if not (isinstance(i, int) and i == 0):
                    pe.wait_ge(s_x, n(i, h) - 2)
                pe.matmul(gb(h, 1)[:, :], a_sq[:, 0, :], gxt[h], start=True, stop=True)
                pe.matmul(gb(h, 0)[:, :], a_sq[:, 1, :], gxt[h], start=True, stop=True).then_inc(s_qkp, 1)

        def gla_in2_tensor(pe, i):
            for h in range(2):
                pe.wait_ge(s_qkc, n(i, h))
                pe.matmul(gb(h, 1)[:, :], a_sq[:, 3, :], gxt[h], start=True, stop=True).then_inc(s_gp, 1)
                for t in range(TILES):
                    m = pe.matmul(gb(h, 0)[:, t * P:(t + 1) * P], gxt[h][:, t * P:(t + 1) * P], a_sq[:, 2, :],
                                  start=True, stop=True)
                m.then_inc(s_v, 1)

        def gla_diagonal_tensor(pe, i):
            for h in range(2):
                pe.wait_ge(s_qk, n(i, h))
                for c in range(TILES):
                    m = pe.matmul(gb(h, 1)[:, c * P:(c + 1) * P], bufB[h][:, c * P:(c + 1) * P],
                                  bufD[h][:, c * P:(c + 1) * P], start=True, stop=True)
                m.then_inc(s_dg, 1)

        def gla_level_tensor(pe, i, lv, halves_of=(0, 1)):
            w = 1 << lv
            for h in halves_of:
                if lv:
                    pe.wait_ge(s_upd, i * (2 * LEVELS) + (2 * (lv - 1) + h + 1))
                    pe.wait_ge(s_pred, i * (2 * COPIES) + (2 * (lv - 1) + h + 1))
                else:
                    pe.wait_ge(s_q0, n(i, h))
                qv = bufA[h][:, :].rearrange("p (c b two r) -> p c b two r", c=TILES, two=2, r=w)
                for c in range(TILES):
                    m = pe.matmul(gb(h, lv % 2)[:, c * 64:(c + 1) * 64], bufB[h][:, c * P:(c + 1) * P],
                                  qv[:, c, :, 1, :], start=True, stop=True)
                m.then_inc(s_lvl, 1)

        def gla_out_tensor(pe, i):
            for h in range(2):
                pe.wait_ge(s_upd, i * (2 * LEVELS) + (2 * (LEVELS - 1) + h + 1))
                pe.wait_ge(s_pred, i * (2 * COPIES) + (2 * (LEVELS - 1) + h + 1))
                for b in range(SEQS):
                    m = pe.matmul(gb(h, 1)[:, b * P:(b + 1) * P], bufB[h][:, 2 * b * P:(2 * b + 1) * P],
                                  bufA[h][:, (2 * b + 1) * P:(2 * b + 2) * P], start=True, stop=True)
                m.then_inc(s_cross, 1)
            for h in range(2):
                pe.wait_ge(s_cc, n(i, h))
                pe.wait_ge(s_pred, i * (2 * COPIES) + (2 * (COPIES - 1) + h + 1))
                v = bufC[h][:, :]
                for b in range(SEQS):
                    c0, c1 = 2 * b * P, (2 * b + 1) * P
                    pe.matmul(gb(h, 0)[:, c0:c0 + P], v[:, c0:c0 + P], at[h][:, c0:c0 + P], start=True, stop=True)
                    pe.matmul(gb(h, 0)[:, c1:c1 + P], v[:, c0:c0 + P], across[h][:, b, :], start=True, stop=False)
                    m = pe.matmul(gb(h, 0)[:, c1:c1 + P], v[:, c1:c1 + P], at[h][:, c1:c1 + P], start=False, stop=True)
                m.then_inc(s_o, 1)
            for h in range(2):
                pe.wait_ge(s_oc, n(i, h))
                tile_mm(pe, gb(h, 1), bufE[h], a_sq[:, 4, :]).then_inc(s_op, 1)

        def gla_in_scalar(act, i):
            xt_scalar(act, i, 0, 0, gxt, lambda h: gb(h, 0))
            for h in range(2):
                act.wait_ge(s_qkp, n(i, h))
                act.activation(bufD[h][:, :], gb(h, 1)[:, :], ACT.Identity, bias=cols[:, BQ:BQ + 1])
                act.activation(bufB[h][:, :], gb(h, 0)[:, :], ACT.Sigmoid, bias=cols[:, BK:BK + 1]).then_inc(s_qkc, 1)

        def gla_in2_scalar(act, i):
            for h in range(2):
                act.wait_ge(s_gp, n(i, h))
                act.activation(tseg[h][:, :], gb(h, 1)[:, :], ACT.Sigmoid, bias=cols[:, BG:BG + 1]).then_inc(s_qk, 1)

        def gla_out_scalar(act, i):
            for h in range(2):
                act.wait_ge(s_cross, n(i, h))
                act.activation(across[h][:, :, :], gb(h, 1)[:, 0:SEQS * P].rearrange("p (b c) -> p b c", b=SEQS),
                               ACT.Copy).then_inc(s_cc, 1)
            for h in range(2):
                act.wait_ge(s_o, n(i, h))
                act.activation(bufE[h][:, :], gb(h, 0)[:, :], ACT.Copy).then_inc(s_oc, 1)

        def quant_route_vector(dve, q, r):
            when(q, quant_ln_vector, dve, 1)
            if r is not None:
                dve.wait_ge(s_xq, n(r, 1, 1))
                dve.memset(scratch2[0][:, :], 0.0)
                ln_stats(dve, r, 1, 1)
            when(q, ln_root_vector, dve, 0, 1)
            when(q, quant_apply_vector, dve, 1)
            when(r, ln_root_vector, dve, 1, 1)
            when(r, route_apply_vector, dve, 0)
            when(q, quant_max_vector, dve, 1)
            when(q, quant_round_vector, dve, 1)
            when(q, quant_clip_vector, dve, 1)
            when(r, route_bias_vector, dve, 0)
            when(r, route_rank_vector, dve, 0)
            when(r, route_rows_vector, dve, 0)
            when(q, quant_add_vector, dve, 1)
            for j in range(IJ):
                when(r, shared_hidden_vector, dve, 0, j)
            when(r, shared_add_vector, dve, 0)

        def quant_route_gpsimd(pool, q, r):
            when(q, quant_gpsimd, pool, 1)
            when(r, route_gpsimd, pool, 0)

        def quant_route_tensor(pe, q, r):
            when(r, route_logits_tensor, pe, 0)
            when(r, shared_gate_tensor, pe, 0, 0)
            when(q, quant_tensor, pe, 1)
            when(r, route_counts_tensor, pe, 0)
            when(r, shared_gate_tensor, pe, 0, 1)
            for j in range(IJ):
                when(r, shared_up_tensor, pe, 0, j)
            when(r, shared_down_tensor, pe, 0)

        def quant_route_scalar(act, q, r):
            when(q, ln_root_scalar, act, 0, 1)
            when(r, ln_root_scalar, act, 1, 1)
            when(r, route_scalar, act, 0)
            when(q, quant_scalar, act, 1)
            when(r, shared_scalar, act, 0)

        def gla_route_vector(dve, g, r):
            if g is not None:
                combine_vector(dve, g, 0)
                dve.wait_ge(s_add1, n(g, 1))
                dve.memset(scratch2[1][:, :], 0.0)
                ln_stats(dve, g, 0, 2)
            if r is not None:
                gla_add_vector(dve, r)
                dve.wait_ge(s_x, n(r, 1))
                dve.memset(scratch2[0][:, :], 0.0)
                ln_stats(dve, r, 1, 2)
            if g is not None:
                ln_apply(dve, g, 0, 2, tt)
            if r is not None:
                route_apply_vector(dve, r, 1)
                route_bias_vector(dve, r, 1)
            if r is not None:
                route_rank_vector(dve, r, 1)
            if g is not None:
                gla_gates_vector(dve, g)
            if r is not None:
                route_rows_vector(dve, r, 1)
            for lv in range(LEVELS):
                if g is not None:
                    gla_level_vector(dve, g, lv)
                if r is not None and lv in (2, 3):
                    shared_hidden_vector(dve, r, 1, lv - 2)
                if r is not None and lv == 6:
                    shared_add_vector(dve, r, 1)
            if g is not None:
                gla_last_vector(dve, g)

        def gla_route_gpsimd(pool, g, r):
            if g is not None:
                ln_gpsimd(pool, g, 0, 2)
            if r is not None:
                ln_gpsimd(pool, r, 1, 2)
            if g is not None:
                gla_gpsimd(pool, g)
            if r is not None:
                route_gpsimd(pool, r, 1)

        def gla_route_tensor(pe, g, r):
            if r is not None:
                gla_out_tensor(pe, r)
            if g is not None:
                gla_in_tensor(pe, g)
            if r is not None:
                route_logits_tensor(pe, r, 1)
            if g is not None:
                gla_in2_tensor(pe, g)
            if r is not None:
                shared_gate_tensor(pe, r, 1, 0)
            if r is not None:
                route_counts_tensor(pe, r, 1)
            if g is not None:
                gla_diagonal_tensor(pe, g)
            first, last = range(TILES // 2), range(TILES // 2, TILES)
            for lv in range(LEVELS):
                for h in range(2):
                    if g is not None:
                        gla_level_tensor(pe, g, lv, (h,))
                    if r is None:
                        continue
                    if lv == 0:
                        shared_gate_tensor(pe, r, 1, 1, (h,))
                    elif lv in (1, 2):
                        shared_up_tensor(pe, r, 1, lv - 1, (h,))
                    elif lv in (4, 5):
                        shared_down_tensor(pe, r, 1, (lv - 4,), (first, last)[h])

        def gla_route_scalar(act, g, r):
            if r is not None:
                gla_out_scalar(act, r)
            if g is not None:
                gla_in_scalar(act, g)
            if r is not None:
                route_scalar(act, r, 1)
            if g is not None:
                gla_in2_scalar(act, g)
            if r is not None:
                shared_scalar(act, r, 1)

        def in_two_steps(eng, both, alone=0):
            for i in range(alone):
                both(eng, i + 1, i)
            with eng.Fori(alone, PAIRS - 1) as i:
                both(eng, i + 1, i)
            both(eng, None, PAIRS - 1)

        @block.sync
        def _(sp_):
            sp_.dma_start(x[:, 0, :, :], x_in[:, 0, :, :]).then_inc(s_first, 16)
            for dst, src in ((cols, cols_in), (rows, rows_in), (consts, consts_in)):
                sp_.dma_start(dst[:, :], src).then_inc(s_first, 16)
            sp_.dma_start(wq_int[:, :, :], wq64.bitcast(I32).rearrange("p (n w) -> p n w", w=2)).then_inc(s_first, 16)
            for g in range(1, PAIRS):
                sp_.dma_start(x[:, g, :, :], x_in[:, g, :, :]).then_inc(s_load, 16)
            sp_.dma_start(w_sq[:, :, :], l0_sq).then_inc(s_load, 16)
            sp_.dma_start(w_gu[:, :, :], l0_gu).then_inc(s_load, 16)
            sp_.dma_start(masks_wide, masks_in).then_inc(s_load, 16)
            sp_.dma_start(w_dn[:, :, :], l0_dn).then_inc(s_load, 16)
            sp_.dma_start(w_r[:, :], moe_r).then_inc(s_load, 16)
            sp_.dma_start(a_sq[:, :, :], l1_sq).then_inc(s_load2, 16)
            sp_.dma_start(e_gu[:, :, :, :], moe_gu).then_inc(s_load2, 16)
            sp_.dma_start(e_dn[:, :, :, :], moe_dn).then_inc(s_load2, 16)
            sp_.wait_ge(s_padding, 1)
            for e in range(E_ROUTED):
                first = E_ROUTED * REGION + e * P
                sp_.dma_start(rows_by_expert[first:first + P, :], tin[e][:, :]).then_inc(s_zfill, 16)
            sp_.wait_ge(s_zfill, 16 * E_ROUTED)
            for p in range(2):
                experts_sync(sp_, p)
                stored(sp_, p)
                fetch_sync(sp_, 0, p)
                with sp_.Fori(0, PAIRS - 1) as i:
                    fetch_sync(sp_, i + 1, p, after=i)
                    if p:
                        sp_.dma_start(out[:, i, :, :], x[:, i, :, :]).then_inc(s_out, 16)
            sp_.wait_ge(s_add1, GROUPS * 2)
            sp_.dma_start(out[:, PAIRS - 1, :, :], x[:, PAIRS - 1, :, :]).then_inc(s_out, 16)
            sp_.wait_ge(s_out, 16 * PAIRS)

        @block.vector
        def _(dve):
            dve.sem_inc(s_thid, AHEAD["s_thid"])
            dve.sem_inc(s_tyc, AHEAD["s_tyc"])
            dve.sem_inc(s_xl, XL_AHEAD)
            for h in range(2):
                dve.memset(at[h][:, :], 0.0)
                dve.memset(xp[h][:, :, 0:PAD], 0.0)
            dve.wait_ge(s_first, 16 * FIRST)
            dve.tensor_copy(wq[:, :], wq_int[:, :, 0])
            dve.tensor_copy(ident_bf[:, :], ident)
            for t in range(TILES):
                dve.tensor_scalar(half_ws[:, t, :], rows[:, R_WS:R_WS + P], 0.5, None, ALU.mult)
                dve.tensor_scalar(half_qb[:, t, :], rows[:, R_QB:R_QB + P], 0.5, None, ALU.mult)
            dve.tensor_copy(before_bf[:, :], consts[:, K_BEFORE:K_BEFORE + P]).then_inc(s_const, 1)
            dve.wait_ge(s_const, 1)
            quant_l0_vector(dve, 0, None, None)
            dve.wait_ge(s_load, 16 * LOADS)
            dve.tensor_scalar(wx_n[:, :, :], w_sq[:, 0:2, :], cols[:, N1W:N1W + 1], None, ALU.mult)
            dve.tensor_copy(masks[:, :], masks_wide)
            dve.tensor_scalar(wgu_n[:, :, :], w_gu[:, :, :], cols[:, N2W:N2W + 1], None, ALU.mult).then_inc(s_const, 1)
            dve.wait_ge(s_act_const, 1)
            dve.tensor_scalar(sp[:, 3:4], cols[:, LAM:LAM + 1], 0.0, sp[:, 2:3], ALU.max, ALU.add).then_inc(s_const, 1)
            dve.wait_ge(s_const, 3)
            dve.tensor_scalar(decay[:, :], sp[:, 3:4], -C_CONST, None, ALU.mult).then_inc(s_const, 1)
            in_three_steps(dve, quant_l0_vector)
            ffn_quant_vector(dve, PAIRS - 1, 0)
            dve.tensor_copy(carry[0][:, :], region).then_inc(s_slot, 1)
            in_two_steps(dve, quant_route_vector, alone=1)
            tables_vector(dve, 0)
            experts_vector(dve, 0)
            dve.wait_ge(s_tab, TAB)
            dve.tensor_copy(carry[0][:, :], region).then_inc(s_slot, 1)
            gla_route_vector(dve, 0, None)
            in_two_steps(dve, gla_route_vector)
            tables_vector(dve, 1)
            experts_vector(dve, 1)
            with dve.Fori(0, PAIRS) as i:
                combine_vector(dve, i, 1)

        @block.gpsimd
        def _(pool):
            pool.memset(zero_col[:, :], 0.0).then_inc(s_zero, 1)
            pool.memset(ones8[:, :], 1.0)
            pool.memset(ones_bf[:, :], 1.0)
            pool.memset(rms_eps[:, :], RMS_EPS)
            pool.memset(neg_half[:, :], -0.5).then_inc(s_pool_const, 1)
            pool.wait_ge(s_pool_const, 1)
            pool.wait_ge(s_const, 1)
            quant_l0_gpsimd(pool, 0, None, None)
            padding_rows(pool, 0)
            in_three_steps(pool, quant_l0_gpsimd)
            ffn_quant_gpsimd(pool, PAIRS - 1, 0)
            padding_rows(pool, 1)
            in_two_steps(pool, quant_route_gpsimd, alone=1)
            experts_gpsimd(pool, 0)
            padding_rows(pool, 2)
            gla_route_gpsimd(pool, 0, None)
            in_two_steps(pool, gla_route_gpsimd)
            experts_gpsimd(pool, 1)

        @block.tensor
        def _(pe):
            pe.sem_inc(s_tht, AHEAD["s_tht"])
            pe.sem_inc(s_tdn, AHEAD["s_tdn"])
            pe.wait_ge(s_const, 1)
            quant_l0_tensor(pe, 0, None, None)
            pe.wait_ge(s_const, 2)
            in_three_steps(pe, quant_l0_tensor)
            ffn_quant_tensor(pe, PAIRS - 1, 0)
            pe.wait_ge(s_load2, 48)
            in_two_steps(pe, quant_route_tensor, alone=1)
            experts_tensor(pe, 0)
            gla_route_tensor(pe, 0, None)
            in_two_steps(pe, gla_route_tensor)
            experts_tensor(pe, 1)

        @block.scalar
        def _(act):
            act.sem_inc(s_thc, AHEAD["s_thc"])
            act.sem_inc(s_tsil, AHEAD["s_tsil"])
            act.wait_ge(s_first, 16 * FIRST)
            act.activation(sp[:, 0:1], cols[:, LAM:LAM + 1], ACT.Abs).then_inc(s_act_sp, 1)
            act.wait_ge(s_act_sp, 1)
            act.activation(sp[:, 1:2], sp[:, 0:1], ACT.Exp, scale=-1.0).then_inc(s_act_sp, 1)
            act.wait_ge(s_act_sp, 2)
            act.activation(sp[:, 2:3], sp[:, 1:2], ACT.Ln, bias=1.0).then_inc(s_act_const, 1)
            quant_l0_scalar(act, 0, None, None)
            act.wait_ge(s_const, 4)
            in_three_steps(act, quant_l0_scalar)
            ffn_quant_scalar(act, PAIRS - 1, 0)
            in_two_steps(act, quant_route_scalar, alone=1)
            experts_scalar(act, 0)
            gla_route_scalar(act, 0, None)
            in_two_steps(act, gla_route_scalar)
            experts_scalar(act, 1)


def kernel(**inputs):
    import numpy as np
    import concourse.bacc as bacc
    from concourse.bass_utils import run_bass_kernel_spmd as run

    v = {k: np.asarray(a) for k, a in inputs.items()}
    c = np.ascontiguousarray

    def across(*vectors):
        return c(np.broadcast_to(np.concatenate(vectors)[None, :], (P, sum(len(a) for a in vectors))))

    def tokens(a):
        return a.reshape(PAIRS, 2, TILES, P, D).transpose(3, 0, 1, 2, 4).reshape(P, PAIRS, 2, GROUP)

    gate_up = np.stack([np.concatenate([v["L1_ffn_Wg"], v["L1_ffn_Wg_s"][None]]),
                        np.concatenate([v["L1_ffn_Wu"], v["L1_ffn_Wu_s"][None]])], axis=1)
    down = np.concatenate([v["L1_ffn_Wd"], v["L1_ffn_Wd_s"][None]])

    row = np.arange(P)[:, None]
    levels = []
    for lv in range(LEVELS - 1):
        w = 1 << lv
        col = np.arange(64)[None, :] // w
        levels.append(np.tile((row // w == 2 * col), (1, TILES)))
    levels.append(np.tile(row == np.arange(P)[None, :], (1, TILES)))
    masks = np.concatenate(levels, axis=1).astype(np.int32)
    ee = np.arange(E_ROUTED)
    region = np.tile(ee * REGION, (P, 1))
    consts = np.concatenate([np.eye(P), row < np.arange(P)[None, :],
                             np.tile((ee[None, :] < ee[:, None]).reshape(1, -1), (P, 1)),
                             region, region + row, np.tile(np.arange(NT), (P, 1)),
                             np.tile(np.arange(NT) * P, (P, 1)),
                             np.arange(TOKENS).reshape(TOKENS // P, P).T,
                             TOP_K * TOKENS + np.arange(2 * E_ROUTED) * P + row], axis=1).astype(np.float32)

    arrays = {
        "x_in": tokens(v["L0_attn_x"].reshape(TOKENS, D)),
        "wq64": v["L0_ffn_weight_q"].T.astype(np.int64),
        "cols_in": np.stack([v["L0_attn_norm1_w"], *v["L0_attn_conv_w"], v["L0_attn_conv_b"], v["L0_attn_lam"],
                             v["L0_attn_norm2_w"], v["L1_attn_bq"], v["L1_attn_bk"], v["L1_attn_bg"]], axis=1),
        "rows_in": across(v["L0_ffn_weight_scale"], v["L0_ffn_bias"], v["L1_attn_bv"], v["L1_attn_bo"], v["L1_ffn_rb"]),
        "l0_sq": np.stack([v["L0_attn_" + k] for k in ("Wx", "Wy", "Wi", "Wa", "Wo")], axis=1),
        "l0_gu": np.stack([v["L0_attn_Wg"], v["L0_attn_Wu"]], axis=1),
        "l0_dn": v["L0_attn_Wd"].reshape(HJ, P, D).transpose(1, 0, 2),
        "l1_sq": np.stack([v["L1_attn_" + k] for k in ("Wq", "Wk", "Wv", "Wg", "Wo")], axis=1),
        "moe_gu": gate_up.transpose(3, 0, 1, 2),
        "moe_dn": down.transpose(2, 0, 1).reshape(IJ, P, E_ALL, D).transpose(1, 2, 0, 3),
        "moe_r": v["L1_ffn_Wr"].T,
        "consts_in": consts,
        "masks_in": masks,
    }
    nc = bacc.Bacc("TRN2", target_bir_lowering=False, num_devices=1)
    args, feed = [], {}
    for name, a in arrays.items():
        feed[name] = c(a)
        args.append(nc.dram_tensor(name, a.shape, mybir.dt.from_np(a.dtype), kind="ExternalInput").ap())
    args.append(nc.dram_tensor("rows_by_expert", ((E_ROUTED + 1) * REGION, ROW), F32, kind="Internal").ap())
    args.append(nc.dram_tensor("rows_done", (TOP_K * TOKENS + 2 * E_ROUTED * P, D), F32, kind="Internal").ap())
    args.append(nc.dram_tensor("out", (P, PAIRS, 2, GROUP), F32, kind="ExternalOutput").ap())
    macaron_kernel(nc, *args)
    r = run(nc, [feed], core_ids=[0])
    got = r.results[0]["out"]
    return c(got.reshape(P, PAIRS, 2, TILES, D).transpose(1, 2, 3, 0, 4).reshape(B, S, D))
```

```python
from contextlib import ExitStack

import concourse.bass as bass
from concourse import mybir

ALU = mybir.AluOpType
ACT = mybir.ActivationFunctionType
AX = mybir.AxisListType
F32 = mybir.dt.float32
BF16 = mybir.dt.bfloat16
I32 = mybir.dt.int32
U8 = mybir.dt.uint8

P = 128
B, S, D = 16, 256, 128
TOKENS = B * S
GROUP = 512
TILES = GROUP // P
GROUPS = TOKENS // GROUP
PAIRS = GROUPS // 2
SEQS = GROUP // S
HID = 512
HJ = HID // P
TAPS = 4
PAD = TAPS - 1
E_ROUTED, E_ALL, INNER = 8, 9, 256
IJ = INNER // P
SHARED = E_ROUTED
TOP_K = 2
NT = TOP_K * TOKENS // P + E_ROUTED
REGION = TOKENS + P
BLK = 8
OUT_RING = 4
NB = NT // BLK
ROW = D + 1
LEVELS = 7
LN_EPS, RMS_EPS, Q_EPS = 1e-5, 1e-6, 1e-6
MAGIC = 1.5 * 2.0 ** 23
C_CONST = 8.0

N1W, CW0, CB, LAM, N2W, BQ, BK, BG = 0, 1, 5, 6, 7, 8, 9, 10
NCOLS = 11
R_WS, R_QB, R_BV, R_BO, R_RB = 0, P, 2 * P, 3 * P, 4 * P
NROWS = 4 * P + E_ROUTED
K_ID, K_BEFORE, K_LOWER, K_REGION, K_PAD, K_J, K_J128 = 0, P, 2 * P, 2 * P + 64, 2 * P + 72, 2 * P + 80, 2 * P + 80 + NT
K_TOKEN = K_J128 + NT
K_AWAY = K_TOKEN + TOP_K * TOKENS // P
NCONST = K_AWAY + 2 * E_ROUTED


def macaron_kernel(nc, x_in, wq64, cols_in, rows_in, l0_sq, l0_gu, l0_dn, l1_sq, moe_gu, moe_dn, moe_r,
                   consts_in, masks_in, rows_by_expert, rows_done, out):
    with ExitStack() as ctx:
        def sb(name, shape, dt=F32):
            return ctx.enter_context(nc.sbuf_tensor(name, shape, dt))

        def sem(name):
            return ctx.enter_context(nc.semaphore(name))

        ctx.enter_context(nc.allow_low_precision(reason="whole numbers below 2^24"))

        x = sb("x", [P, PAIRS, 2, GROUP])
        score = sb("score", [P, PAIRS, 2, TOP_K * TILES])
        carry = [sb(f"carry{h}", [P, E_ROUTED]) for h in range(2)]
        cnt = sb("cnt", [P, E_ROUTED])
        tl = sb("tl", [P, 4, E_ROUTED])
        tiles_e = sb("tiles_e", [P, E_ROUTED])
        cum = sb("cum", [P, E_ROUTED])
        padidx = sb("padidx", [P, E_ROUTED], I32)
        cmp = sb("cmp", [P, NT, E_ROUTED])
        cmpt = sb("cmpt", [P, NT, E_ROUTED])
        etabf = sb("etabf", [P, NT])
        stab = sb("stab", [P, NT])
        rtabf = sb("rtabf", [P, NT])
        etab = sb("etab", [P, NB, BLK], I32)
        rtab = sb("rtab", [P, NB, BLK], I32)
        zero_col = sb("zero_col", [P, 1])
        scratch2 = [sb(f"scratch2{h}", [P, 1]) for h in range(2)]
        ones8 = sb("ones8", [P, E_ROUTED])
        ones_bf = sb("ones_bf", [P, P], BF16)
        before_bf = sb("before_bf", [P, P], BF16)
        wq_int = sb("wq_int", [P, P, 2], I32)
        wq = sb("wq", [P, P], BF16)
        cols = sb("cols", [P, NCOLS])
        rows = sb("rows", [P, NROWS])
        w_sq = sb("w_sq", [P, 5, P])
        w_gu = sb("w_gu", [P, 2, HID])
        w_dn = sb("w_dn", [P, HJ, P])
        a_sq = sb("a_sq", [P, 5, P])
        e_gu = sb("e_gu", [P, E_ALL, 2, INNER])
        e_dn = sb("e_dn", [P, E_ALL, IJ, P])
        w_r = sb("w_r", [P, E_ROUTED])
        consts = sb("consts", [P, NCONST])
        ident = consts[:, K_ID:K_ID + P]
        ident_bf = sb("ident_bf", [P, P], BF16)
        masks = sb("masks", [P, (LEVELS - 1) * 256 + GROUP], U8)
        lower = consts[:, K_LOWER:K_LOWER + 64].rearrange("p (e j) -> p e j", e=E_ROUTED)
        region = consts[:, K_REGION:K_REGION + E_ROUTED]
        result_rows = consts[:, K_TOKEN:K_AWAY].rearrange("p (r a h t) -> p r a h t", r=TOP_K, a=PAIRS, h=2)
        neg_half = sb("neg_half", [P, TILES])
        rms_eps = sb("rms_eps", [P, TILES])
        wx_n = sb("wx_n", [P, 2, P])
        wgu_n = sb("wgu_n", [P, 2, HID])
        half_ws = sb("half_ws", [P, TILES, P])
        half_qb = sb("half_qb", [P, TILES, P])
        sp = sb("sp", [P, 4])
        decay = sb("decay", [P, 1])

        def two(name, shape, dt=F32):
            return [sb(f"{name}{h}", shape, dt) for h in range(2)]

        stats = two("stats", [P, 2, TILES, 6])
        msum = two("msum", [P, 2, TILES])
        mdif = two("mdif", [P, 2, TILES])
        m2 = two("m2", [P, 2, TILES])
        mean = two("mean", [P, 2, TILES])
        var = two("var", [P, 2, TILES])
        ve = two("ve", [P, 2, TILES])
        rstd = two("rstd", [P, 2, TILES])
        xn = two("xn", [P, TILES, ROW])
        xt = two("xt", [P, GROUP])
        amax = two("amax", [P, TILES])
        qs = two("qs", [P, TILES])
        qinv = two("qinv", [P, TILES])
        qt = two("qt", [P, TILES, P])
        qi = two("qi", [P, TILES, P], BF16)
        qit = two("qit", [P, GROUP], BF16)
        r2 = sb("r2", [P, 2, TILES])
        ms = sb("ms", [P, 2, TILES])
        tt = two("tt", [P, TILES, P])
        xp = two("xp", [P, SEQS, PAD + S])
        xc = two("xc", [P, SEQS, S])
        bufA = two("bufA", [P, GROUP])
        bufB = two("bufB", [P, GROUP])
        bufC = two("bufC", [P, GROUP])
        bufD = two("bufD", [P, GROUP])
        bufE = two("bufE", [P, GROUP])
        h1 = two("h1", [P, TILES, P])
        ss = two("ss", [P, TILES])
        gate = two("gate", [P, HJ, GROUP])
        hid = two("hid", [P, HJ, GROUP])
        masks_wide = hid[0][:, :, :].rearrange("p j c -> p (j c)").bitcast(I32)
        at = two("at", [P, GROUP])
        across = two("across", [P, SEQS, P])
        tseg = two("tseg", [P, GROUP])
        tseg2 = two("tseg2", [P, GROUP // 2])
        probs = two("probs", [P, TILES, E_ROUTED])
        gt = [h1[h][:, 0:2, :].rearrange("p a (b e j) -> p (a b) e j", b=2, e=E_ROUTED) for h in range(2)]
        eq = [h1[h][:, 2:4, :].rearrange("p a (b e j) -> p (a b) e j", b=2, e=E_ROUTED) for h in range(2)]
        gxt = [xc[h][:, :, :].rearrange("p b s -> p (b s)") for h in range(2)]
        rank = two("rank", [P, TILES, E_ROUTED])
        chosen = two("chosen", [P, TILES, E_ROUTED], BF16)
        slot = two("slot", [P, TILES, E_ROUTED])
        slotf = two("slotf", [P, TOP_K, TILES, E_ROUTED])
        scoref = two("scoref", [P, TOP_K, TILES, E_ROUTED])
        sidx = two("sidx", [P, TOP_K * TILES], I32)
        first2 = two("first2", [P, TOP_K, TILES, E_ROUTED])
        xn2 = two("xn2", [P, TILES, ROW])
        got = two("got", [P, TOP_K * TILES, P])
        twt = [gate[0][:, k, :] for k in range(2)]
        rn = [hid[h][:, HJ - 1, :].rearrange("p (t d) -> p t d", t=TILES) for h in range(2)]
        qxn = [got[h][:, 0:TILES, :] for h in range(2)]
        ut = [got[h][:, TILES:, :].rearrange("p t d -> p (t d)") for h in range(2)]
        tin = [sb(f"tin{k}", [P, ROW]) for k in range(BLK)]
        tdst = [sb(f"tdst{k}", [P, 1], I32) for k in range(BLK)]
        tout = [sb(f"tout{k}", [P, P]) for k in range(OUT_RING)]
        tint = two("tint", [P, P])
        tsil = two("tsil", [P, INNER])
        thidt = two("thidt", [P, IJ, P])

        bank = [ctx.enter_context(nc.psum_tensor(f"bank{i}", [P, GROUP], F32)) for i in range(8)]

        def pb(h, k):
            return bank[4 * h + k]

        def gb(h, k):
            return bank[4 * h + k]

        def rb(h, k):
            return bank[4 * h + 2 + k]

        s_first = sem("s_first")
        s_load = sem("s_load")
        s_load2 = sem("s_load2")
        s_act_sp = sem("s_act_sp")
        s_const = sem("s_const")
        s_pool_const = sem("s_pool_const")
        s_act_const = sem("s_act_const")
        s_stats = [sem(f"s_stats{u}") for u in range(2)]
        s_mom = [sem(f"s_mom{u}") for u in range(2)]; s_mean = [sem(f"s_mean{u}") for u in range(2)]
        s_mv = [sem(f"s_mv{u}") for u in range(2)]
        s_ve = [sem(f"s_ve{u}") for u in range(2)]
        s_rstd = [sem(f"s_rstd{u}") for u in range(2)]
        s_xn = [sem(f"s_xn{u}") for u in range(2)]
        s_xq = sem("s_xq"); s_xl = sem("s_xl"); s_x = sem("s_x")
        s_xtr = [sem(f"s_xtr{u}") for u in range(2)]
        s_xt = [sem(f"s_xt{u}") for u in range(2)]
        s_root = [sem(f"s_root{u}") for u in range(2)]
        s_amax = sem("s_amax"); s_qs = sem("s_qs"); s_qinv = sem("s_qinv"); s_qmul = sem("s_qmul")
        s_qclip = sem("s_qclip"); s_qi = sem("s_qi"); s_qtr = sem("s_qtr"); s_qit = sem("s_qit")
        s_qy = sem("s_qy"); s_qz = sem("s_qz"); s_qxb = sem("s_qxb")
        s_xb = sem("s_xb"); s_xp = sem("s_xp"); s_ms = sem("s_ms"); s_r2 = sem("s_r2")
        s_t = sem("s_t"); s_ttr = sem("s_ttr"); s_tx = sem("s_tx")
        s_conv = sem("s_conv"); s_y = sem("s_y"); s_gates = sem("s_gates"); s_sig = sem("s_sig")
        s_a = sem("s_a"); s_a2 = sem("s_a2"); s_om = sem("s_om"); s_sq = sem("s_sq"); s_ix = sem("s_ix")
        s_b = sem("s_b"); s_scan = sem("s_scan"); s_yb = sem("s_yb"); s_hy = sem("s_hy")
        s_mix = sem("s_mix"); s_h1 = sem("s_h1"); s_ss = sem("s_ss"); s_s2a = sem("s_s2a"); s_s2 = sem("s_s2")
        s_u = sem("s_u"); s_utr = sem("s_utr"); s_ut = sem("s_ut"); s_fg = sem("s_fg"); s_fu = sem("s_fu")
        s_gelu = sem("s_gelu"); s_hid = sem("s_hid"); s_ffn = sem("s_ffn"); s_xh = sem("s_xh")
        s_qkp = sem("s_qkp"); s_qkc = sem("s_qkc"); s_gp = sem("s_gp"); s_v = sem("s_v"); s_qk = sem("s_qk"); s_vb = sem("s_vb")
        s_q0 = sem("s_q0"); s_lvl = sem("s_lvl"); s_upd = sem("s_upd")
        s_pred = sem("s_pred"); s_cross = sem("s_cross"); s_cc = sem("s_cc"); s_o = sem("s_o")
        s_oc = sem("s_oc"); s_op = sem("s_op"); s_xbo = sem("s_xbo"); s_dg = sem("s_dg")
        s_rl = sem("s_rl"); s_rlb = sem("s_rlb"); s_pr = sem("s_pr"); s_cmp = sem("s_cmp")
        s_cml = sem("s_cml"); s_cms = sem("s_cms"); s_rank = sem("s_rank"); s_first2 = sem("s_first2")
        s_pref = sem("s_pref"); s_slot = sem("s_slot"); s_prod = sem("s_prod"); s_idx = sem("s_idx")
        s_xn2 = sem("s_xn2"); s_carry = sem("s_carry")
        s_scat = [sem(f"s_scat{h}") for h in range(2)]
        s_tab = sem("s_tab")
        s_zero = sem("s_zero"); s_padding = sem("s_padding"); s_zfill = sem("s_zfill"); s_pad = sem("s_pad")
        s_sg = sem("s_sg"); s_su = sem("s_su"); s_silu = sem("s_silu"); s_sh = sem("s_sh"); s_sd = sem("s_sd")
        s_xsh = sem("s_xsh")
        s_add0 = sem("s_add0"); s_add1 = sem("s_add1")
        s_got = [sem(f"s_got{h}") for h in range(2)]
        s_in = [sem(f"s_in{k}") for k in range(BLK)]
        s_st = [sem(f"s_st{k}") for k in range(OUT_RING)]
        s_tt = sem("s_tt"); s_ttc = sem("s_ttc"); s_tgu = sem("s_tgu"); s_tsil = sem("s_tsil")
        s_thid = sem("s_thid"); s_twt = sem("s_twt"); s_tdn = sem("s_tdn")
        s_tyc = sem("s_tyc"); s_tdst = sem("s_tdst")
        s_out = sem("s_out")

        FIRST, LOADS = 5, 8
        SCAT = 16 * TOP_K * TILES
        XL_AHEAD = 2

        def xg(i, h):
            return x[:, i, h, :].rearrange("p (t d) -> p t d", t=TILES)

        def seqs(buf):
            return buf[:, :].rearrange("p (b s) -> p b s", b=SEQS)

        def n(i, h, ph=0):
            return 2 * i + (h + 1 + GROUPS * ph)

        def body(i, ph=0):
            return i + (1 + PAIRS * ph)

        def tile_mm(pe, ps, lhs, rhs, w=P):
            for t in range(TILES):
                m = pe.matmul(ps[:, t * w:(t + 1) * w], lhs[:, t * P:(t + 1) * P], rhs, start=True, stop=True)
            return m

        def transposes(pe, ps, src, idn):
            for t in range(TILES):
                m = pe.transpose(ps[:, t * P:(t + 1) * P], src[:, t, 0:P], idn)
            return m

        def ln_stats(dve, i, u, ph):
            for h in range(2):
                for t in range(TILES):
                    m = dve.bn_stats(stats[u][:, h, t, :], xg(i, h)[:, t, :])
            m.then_inc(s_stats[u], 1)
            dve.wait_ge(s_stats[u], body(i, ph))
            dve.tensor_tensor(msum[u][:, :, :], stats[u][:, :, :, 1], stats[u][:, :, :, 4], ALU.add)
            dve.tensor_tensor(mdif[u][:, :, :], stats[u][:, :, :, 1], stats[u][:, :, :, 4], ALU.subtract)
            dve.tensor_tensor(m2[u][:, :, :], stats[u][:, :, :, 2], stats[u][:, :, :, 5], ALU.add).then_inc(s_mom[u], 1)
            dve.wait_ge(s_mom[u], body(i, ph))
            dve.tensor_scalar(mean[u][:, :, :], msum[u][:, :, :], 0.5, None, ALU.mult)
            dve.scalar_tensor_tensor(out=mdif[u][:, :, :], in0=mdif[u][:, :, :], scalar=0.25, in1=mdif[u][:, :, :],
                                     op0=ALU.mult, op1=ALU.mult).then_inc(s_mean[u], 1)
            dve.wait_ge(s_mean[u], body(i, ph))
            dve.scalar_tensor_tensor(out=var[u][:, :, :], in0=m2[u][:, :, :], scalar=1.0 / D, in1=mdif[u][:, :, :],
                                     op0=ALU.mult, op1=ALU.add).then_inc(s_mv[u], 1)
            dve.wait_ge(s_mv[u], body(i, ph))
            dve.tensor_scalar(ve[u][:, :, :], var[u][:, :, :], LN_EPS, None, ALU.add).then_inc(s_ve[u], 1)

        def ln_gpsimd(pool, i, u, ph):
            pool.wait_ge(s_ve[u], body(i, ph))
            for h in range(2):
                pool.tensor_tensor(rstd[u][:, h, :], ve[u][:, h, :], neg_half[:, :], ALU.pow).then_inc(s_rstd[u], 1)

        def ln_root_scalar(act, i, u, ph):
            act.wait_ge(s_ve[u], body(i, ph))
            act.activation(ve[u][:, :, :], ve[u][:, :, :], ACT.Sqrt).then_inc(s_root[u], 1)

        def ln_root_vector(dve, i, u, before):
            dve.wait_ge(s_root[u], i + before)
            for h in range(2):
                dve.reciprocal(rstd[u][:, h, :], ve[u][:, h, :]).then_inc(s_rstd[u], 1)

        def ln_apply(dve, i, u, ph, dst):
            for h in range(2):
                dve.wait_ge(s_rstd[u], n(i, h, ph))
                for t in range(TILES):
                    m = dve.tensor_scalar(dst[h][:, t, 0:D], xg(i, h)[:, t, :], mean[u][:, h, t:t + 1],
                                          rstd[u][:, h, t:t + 1], ALU.subtract, ALU.mult)
                m.then_inc(s_xn[u], 1)

        def xt_tensor(pe, i, u, ph, src, k, banks):
            for h in range(2):
                pe.wait_ge(s_xn[u], n(i, h, ph))
                transposes(pe, banks(h), src[h], ident).then_inc(s_xtr[u], 1)

        def xt_scalar(act, i, u, k, dst, banks):
            for h in range(2):
                act.wait_ge(s_xtr[u], n(i, h, k))
                act.activation(dst[h], banks(h)[:, :], ACT.Copy).then_inc(s_xt[u], 1)

        block = ctx.enter_context(nc.Block())

        def quant_ln_vector(dve, i, p):
            if p:
                dve.wait_ge(s_xl, (2 if isinstance(i, int) and i == 0 else GROUPS) + XL_AHEAD)
            ln_stats(dve, i, 0, p)

        def quant_apply_vector(dve, i, p):
            ln_apply(dve, i, 0, p, qxn)

        def quant_max_vector(dve, i, p):
            for h in range(2):
                dve.wait_ge(s_xn[0], n(i, h, p))
                dve.tensor_reduce(amax[h][:, :], qxn[h], AX.X, ALU.max, apply_absolute_value=True).then_inc(s_amax, 1)

        def quant_round_vector(dve, i, p):
            for h in range(2):
                dve.wait_ge(s_amax, n(i, h, p))
                dve.tensor_scalar(qs[h][:, :], amax[h][:, :], Q_EPS, 1.0 / 127.0, ALU.max, ALU.mult).then_inc(s_qs, 1)
            for h in range(2):
                dve.wait_ge(s_qs, n(i, h, p))
                dve.reciprocal(qinv[h][:, :], qs[h][:, :]).then_inc(s_qinv, 1)
            for h in range(2):
                dve.wait_ge(s_qinv, n(i, h, p))
                for t in range(TILES):
                    m = dve.tensor_scalar(qt[h][:, t, :], qxn[h][:, t, :], qinv[h][:, t:t + 1], MAGIC,
                                          ALU.mult, ALU.add)
                m.then_inc(s_qmul, 1)

        def quant_clip_vector(dve, i, p):
            for h in range(2):
                dve.wait_ge(s_qmul, n(i, h, p))
                dve.tensor_scalar(qt[h][:, :, :], qt[h][:, :, :], MAGIC - 128.0, MAGIC + 127.0,
                                  ALU.max, ALU.min).then_inc(s_qclip, 1)
            for h in range(2):
                dve.wait_ge(s_qclip, n(i, h, p))
                dve.tensor_scalar(qi[h][:, :, :], qt[h][:, :, :], -MAGIC, None, ALU.add).then_inc(s_qi, 1)

        def quant_add_vector(dve, i, p):
            for h in range(2):
                dve.wait_ge(s_qy, n(i, h, p))
                dve.wait_ge(s_qxb, n(i, h, p))
                for t in range(TILES):
                    m = dve.scalar_tensor_tensor(out=qt[h][:, t, :], in0=pb(h, 0)[:, t * P:(t + 1) * P],
                                                 scalar=qs[h][:, t:t + 1], in1=half_ws[:, t, :],
                                                 op0=ALU.mult, op1=ALU.mult)
                m.then_inc(s_qz, 1)
            for h in range(2):
                dve.wait_ge(s_qz, n(i, h, p))
                dve.tensor_tensor(xg(i, h), xg(i, h), qt[h][:, :, :], ALU.add).then_inc(s_xq, 1)

        def quant_gpsimd(pool, i, p):
            for h in range(2):
                pool.wait_ge(s_xn[0], n(i, h, p))
                pool.tensor_tensor(xg(i, h), xg(i, h), half_qb[:, :, :], ALU.add).then_inc(s_qxb, 1)

        def quant_tensor(pe, i, p):
            for h in range(2):
                pe.wait_ge(s_qi, n(i, h, p))
                transposes(pe, pb(h, 0)[:, 0:GROUP // 2].bitcast(BF16), qi[h], ident_bf[:, :]).then_inc(s_qtr, 1)
            for h in range(2):
                pe.wait_ge(s_qit, n(i, h, p))
                tile_mm(pe, pb(h, 0), qit[h], wq[:, :]).then_inc(s_qy, 1)

        def quant_scalar(act, i, p):
            for h in range(2):
                act.wait_ge(s_qtr, n(i, h, p))
                act.activation(qit[h][:, :], pb(h, 0)[:, 0:GROUP // 2].bitcast(BF16), ACT.Copy).then_inc(s_qit, 1)

        def front_ln_vector(dve, i):
            dve.wait_ge(s_xq, n(i, 1))
            dve.memset(scratch2[0][:, :], 0.0)
            ln_stats(dve, i, 1, 0)

        def front_norm_vector(dve, i):
            dve.wait_ge(s_rstd[1], n(i, 1))
            dve.tensor_tensor(ms[:, :, :], rstd[1][:, :, :], rstd[1][:, :, :], ALU.mult).then_inc(s_ms, 1)
            dve.wait_ge(s_ms, 3 * i + 1)
            dve.tensor_tensor(ms[:, :, :], ms[:, :, :], var[1][:, :, :], ALU.mult).then_inc(s_ms, 1)
            dve.wait_ge(s_ms, 3 * i + 2)
            dve.tensor_scalar(ms[:, :, :], ms[:, :, :], RMS_EPS, None, ALU.add).then_inc(s_ms, 1)
            ln_apply(dve, i, 1, 0, xn)

        def front_conv_vector(dve, i):
            for k in range(PAD):
                for h in range(2):
                    dve.wait_ge(s_xp, n(i, h))
                    if k:
                        dve.wait_ge(s_conv, i * (2 * PAD) + (2 * (k - 1) + h + 1))
                    dve.scalar_tensor_tensor(out=xc[h][:, :, :], in0=xp[h][:, :, k:k + S],
                                             scalar=cols[:, CW0 + k:CW0 + k + 1], in1=xc[h][:, :, :],
                                             op0=ALU.mult, op1=ALU.add).then_inc(s_conv, 1)

        def front_decay_vector(dve, i):
            for h in range(2):
                dve.wait_ge(s_a, n(i, h))
                dve.scalar_tensor_tensor(out=bufD[h][:, :], in0=bufA[h][:, :], scalar=-1.0, in1=bufA[h][:, :],
                                         op0=ALU.mult, op1=ALU.mult).then_inc(s_a2, 1)
            for h in range(2):
                dve.wait_ge(s_a2, n(i, h))
                dve.tensor_scalar(bufD[h][:, :], bufD[h][:, :], 1.0, 1e-12, ALU.add, ALU.max).then_inc(s_om, 1)

        def front_scan_vector(dve, i):
            for h in range(2):
                dve.wait_ge(s_b, n(i, h))
                for b in range(SEQS):
                    m = dve.tensor_tensor_scan(bufE[h][:, b * S:(b + 1) * S], bufA[h][:, b * S:(b + 1) * S],
                                               bufB[h][:, b * S:(b + 1) * S], 0.0, ALU.mult, ALU.add)
                m.then_inc(s_scan, 1)

        def front_gated_vector(dve, i):
            for h in range(2):
                dve.wait_ge(s_scan, n(i, h))
                dve.wait_ge(s_yb, n(i, h))
                dve.tensor_tensor(bufE[h][:, :], bufE[h][:, :], bufC[h][:, :], ALU.mult).then_inc(s_hy, 1)

        def front_mixed_vector(dve, i):
            for h in range(2):
                dve.wait_ge(s_mix, n(i, h))
                dve.tensor_tensor(h1[h][:, :, :], xn[h][:, :, 0:D],
                                  pb(h, 1)[:, :].rearrange("p (t d) -> p t d", t=TILES), ALU.add).then_inc(s_h1, 1)

        def ffn_hidden_vector(dve, i, j):
            for h in range(2):
                dve.wait_ge(s_gelu, i * (2 * HJ) + (2 * j + h + 1))
                dve.wait_ge(s_fu, i * (2 * HJ) + (2 * j + h + 1))
                dve.tensor_tensor(hid[h][:, j, :], gate[h][:, j, :], pb(h, 3)[:, :], ALU.mult).then_inc(s_hid, 1)

        def ffn_add_vector(dve, i):
            for h in range(2):
                dve.wait_ge(s_ffn, n(i, h))
                dve.wait_ge(s_xh, n(i, h))
                dve.tensor_tensor(x[:, i, h, :], x[:, i, h, :], pb(h, 2)[:, :], ALU.add).then_inc(s_xl, 1)

        def front_norm_gpsimd(pool, i):
            pool.wait_ge(s_ms, 3 * i + 3)
            for h in range(2):
                pool.tensor_tensor(r2[:, h, :], ms[:, h, :], neg_half[:, :], ALU.pow).then_inc(s_r2, 1)

        def front_input_gpsimd(pool, i):
            for h in range(2):
                pool.wait_ge(s_sig, n(i, h))
                pool.tensor_tensor(bufB[h][:, :].rearrange("p (b s) -> p b s", b=SEQS),
                                   seqs(bufB[h]), xc[h][:, :, :], ALU.mult).then_inc(s_ix, 1)
            for h in range(2):
                pool.wait_ge(s_sq, n(i, h))
                pool.wait_ge(s_ix, n(i, h))
                pool.tensor_tensor(bufB[h][:, :], bufD[h][:, :], bufB[h][:, :], ALU.mult).then_inc(s_b, 1)

        def front_norm2_gpsimd(pool, i):
            for h in range(2):
                pool.wait_ge(s_ss, n(i, h))
                pool.tensor_tensor(ss[h][:, :], ss[h][:, :], rms_eps[:, :], ALU.add).then_inc(s_s2a, 1)
                pool.wait_ge(s_s2a, n(i, h))
                pool.tensor_tensor(r2[:, h, :], ss[h][:, :], neg_half[:, :], ALU.pow).then_inc(s_s2, 1)
            for h in range(2):
                pool.wait_ge(s_h1, n(i, h))
                pool.tensor_tensor(xg(i, h), xg(i, h), h1[h][:, :, :], ALU.add).then_inc(s_xh, 1)

        def front_in_tensor(pe, i):
            for h in range(2):
                pe.wait_ge(s_t, n(i, h))
                transposes(pe, pb(h, 0), tt[h], ident).then_inc(s_ttr, 1)
            for h in range(2):
                pe.wait_ge(s_tx, n(i, h))
                pe.matmul(pb(h, 1)[:, :], wx_n[:, 0, :], xt[h][:, :], start=True, stop=True).then_inc(s_xb, 1)
            for h in range(2):
                pe.matmul(pb(h, 0)[:, :], wx_n[:, 1, :], xt[h][:, :], start=True, stop=True).then_inc(s_y, 1)

        def front_gates_tensor(pe, i):
            for h in range(2):
                pe.wait_ge(s_conv, i * (2 * PAD) + (2 * (PAD - 1) + h + 1))
                pe.matmul(pb(h, 1)[:, :], w_sq[:, 3, :], xc[h][:, :, :], start=True, stop=True)
                pe.wait_ge(s_yb, n(i, h))
                pe.matmul(pb(h, 0)[:, :], w_sq[:, 2, :], xc[h][:, :, :], start=True, stop=True).then_inc(s_gates, 1)

        def front_mix_tensor(pe, i):
            for h in range(2):
                pe.wait_ge(s_hy, n(i, h))
                tile_mm(pe, pb(h, 1), bufE[h], w_sq[:, 4, :]).then_inc(s_mix, 1)

        def front_out_tensor(pe, i, q):
            for h in range(2):
                pe.wait_ge(s_u, n(i, h))
                if q is not None:
                    pe.wait_ge(s_xq, n(q, h))
                transposes(pe, pb(h, 0), tt[h], ident).then_inc(s_utr, 1)

        def ffn_up_tensor(pe, i, j):
            for h in range(2):
                if j:
                    pe.wait_ge(s_gelu, i * (2 * HJ) + (2 * (j - 1) + h + 1))
                    pe.wait_ge(s_hid, i * (2 * HJ) + (2 * (j - 1) + h + 1))
                else:
                    pe.wait_ge(s_ut, n(i, h))
                    pe.wait_ge(s_xl, n(i, h))
                pe.matmul(pb(h, 2)[:, :], wgu_n[:, 0, j * P:(j + 1) * P], ut[h], start=True, stop=True).then_inc(s_fg, 1)
                pe.matmul(pb(h, 3)[:, :], wgu_n[:, 1, j * P:(j + 1) * P], ut[h], start=True, stop=True).then_inc(s_fu, 1)

        def ffn_down_tensor(pe, i):
            for h in range(2):
                pe.wait_ge(s_hid, i * (2 * HJ) + (2 * (HJ - 1) + h + 1))
                for t in range(TILES):
                    for j in range(HJ):
                        m = pe.matmul(pb(h, 2)[:, t * P:(t + 1) * P], hid[h][:, j, t * P:(t + 1) * P],
                                      w_dn[:, j, :], start=(j == 0), stop=(j == HJ - 1))
                m.then_inc(s_ffn, 1)

        def front_norm_scalar(act, i):
            for h in range(2):
                act.wait_ge(s_r2, n(i, h))
                act.wait_ge(s_xn[1], n(i, h))
                for t in range(TILES):
                    m = act.activation(tt[h][:, t, :], xn[h][:, t, 0:D], ACT.Copy, scale=r2[:, h, t:t + 1])
                m.then_inc(s_t, 1)

        def front_in_scalar(act, i):
            for h in range(2):
                act.wait_ge(s_ttr, n(i, h))
                act.activation(xt[h][:, :], pb(h, 0)[:, :], ACT.Copy).then_inc(s_tx, 1)
            for h in range(2):
                act.wait_ge(s_xb, n(i, h))
                act.activation(xp[h][:, :, PAD:], seqs(pb(h, 1)), ACT.Copy)
                act.activation(xc[h][:, :, :], seqs(pb(h, 1)), ACT.Identity, scale=cols[:, CW0 + PAD:CW0 + PAD + 1],
                               bias=cols[:, CB:CB + 1]).then_inc(s_xp, 1)
            for h in range(2):
                act.wait_ge(s_y, n(i, h))
                act.activation(bufC[h][:, :], pb(h, 0)[:, :], ACT.Gelu_apprx_tanh).then_inc(s_yb, 1)

        def front_gates_scalar(act, i):
            for h in range(2):
                act.wait_ge(s_gates, n(i, h))
                act.activation(bufA[h][:, :], pb(h, 1)[:, :], ACT.Sigmoid)
                act.activation(bufB[h][:, :], pb(h, 0)[:, :], ACT.Sigmoid).then_inc(s_sig, 1)
            for h in range(2):
                act.wait_ge(s_sig, n(i, h))
                act.activation(bufA[h][:, :], bufA[h][:, :], ACT.Exp, scale=decay[:, 0:1]).then_inc(s_a, 1)
            for h in range(2):
                act.wait_ge(s_om, n(i, h))
                act.activation(bufD[h][:, :], bufD[h][:, :], ACT.Sqrt).then_inc(s_sq, 1)

        def front_norm2_scalar(act, i):
            for h in range(2):
                act.wait_ge(s_h1, n(i, h))
                for t in range(TILES):
                    m = act.activation(bufD[h][:, t * P:(t + 1) * P], h1[h][:, t, :], ACT.Square, scale=float(D) ** -0.5,
                                       accum_out=ss[h][:, t:t + 1])
                m.then_inc(s_ss, 1)
            for h in range(2):
                act.wait_ge(s_s2, n(i, h))
                for t in range(TILES):
                    m = act.activation(tt[h][:, t, :], h1[h][:, t, :], ACT.Copy, scale=r2[:, h, t:t + 1])
                m.then_inc(s_u, 1)
            for h in range(2):
                act.wait_ge(s_utr, n(i, h))
                act.activation(ut[h], pb(h, 0)[:, :], ACT.Copy).then_inc(s_ut, 1)

        def ffn_scalar(act, i, j):
            for h in range(2):
                act.wait_ge(s_fg, i * (2 * HJ) + (2 * j + h + 1))
                act.activation(gate[h][:, j, :], pb(h, 2)[:, :], ACT.Gelu_apprx_tanh).then_inc(s_gelu, 1)

        def when(i, step, *rest):
            if i is not None:
                step(*rest[:1], i, *rest[1:])

        def quant_l0_vector(dve, q, f, m):
            when(f, front_ln_vector, dve)
            when(m, ffn_hidden_vector, dve, 0)
            when(f, front_norm_vector, dve)
            when(m, ffn_hidden_vector, dve, 1)
            when(m, ffn_hidden_vector, dve, 2)
            when(f, front_conv_vector, dve)
            when(m, ffn_hidden_vector, dve, 3)
            when(q, quant_ln_vector, dve, 0)
            when(q, quant_apply_vector, dve, 0)
            when(q, quant_max_vector, dve, 0)
            when(f, front_decay_vector, dve)
            when(q, quant_round_vector, dve, 0)
            when(f, front_scan_vector, dve)
            when(q, quant_clip_vector, dve, 0)
            when(f, front_gated_vector, dve)
            when(m, ffn_add_vector, dve)
            when(f, front_mixed_vector, dve)
            when(q, quant_add_vector, dve, 0)

        def quant_l0_gpsimd(pool, q, f, m):
            when(f, ln_gpsimd, pool, 1, 0)
            when(f, front_norm_gpsimd, pool)
            when(q, ln_gpsimd, pool, 0, 0)
            when(f, front_input_gpsimd, pool)
            when(q, quant_gpsimd, pool, 0)
            when(f, front_norm2_gpsimd, pool)

        def quant_l0_tensor(pe, q, f, m):
            for j in range(HJ - 1):
                when(m, ffn_up_tensor, pe, j)
            when(f, front_in_tensor, pe)
            when(m, ffn_up_tensor, pe, HJ - 1)
            when(f, front_gates_tensor, pe)
            when(m, ffn_down_tensor, pe)
            if q is not None and f is not None:
                pe.wait_ge(s_sig, n(f, 1))
            when(q, quant_tensor, pe, 0)
            when(f, front_mix_tensor, pe)
            when(f, front_out_tensor, pe, q)

        def quant_l0_scalar(act, q, f, m):
            for j in range(HJ - 2):
                when(m, ffn_scalar, act, j)
            when(f, front_norm_scalar, act)
            when(m, ffn_scalar, act, HJ - 2)
            when(f, front_in_scalar, act)
            when(m, ffn_scalar, act, HJ - 1)
            when(f, front_gates_scalar, act)
            when(q, quant_scalar, act, 0)
            when(f, front_norm2_scalar, act)

        def ffn_quant_vector(dve, m, q):
            quant_ln_vector(dve, q, 1)
            ffn_hidden_vector(dve, m, 0)
            quant_apply_vector(dve, q, 1)
            ffn_hidden_vector(dve, m, 1)
            quant_max_vector(dve, q, 1)
            quant_round_vector(dve, q, 1)
            ffn_hidden_vector(dve, m, 2)
            quant_clip_vector(dve, q, 1)
            ffn_hidden_vector(dve, m, 3)
            quant_add_vector(dve, q, 1)
            ffn_add_vector(dve, m)

        def ffn_quant_gpsimd(pool, m, q):
            ln_gpsimd(pool, q, 0, 1)
            quant_gpsimd(pool, q, 1)

        def ffn_quant_tensor(pe, m, q):
            for j in range(HJ):
                ffn_up_tensor(pe, m, j)
            quant_tensor(pe, q, 1)
            ffn_down_tensor(pe, m)

        def ffn_quant_scalar(act, m, q):
            for j in range(HJ):
                ffn_scalar(act, m, j)
            quant_scalar(act, q, 1)

        def in_three_steps(eng, body_of):
            body_of(eng, 1, 0, None)
            with eng.Fori(0, PAIRS - 2) as i:
                body_of(eng, i + 2, i + 1, i)
            body_of(eng, None, PAIRS - 1, PAIRS - 2)

        def route_apply_vector(dve, i, p):
            ln_apply(dve, i, 1, 1 + p, rn)

        def route_bias_vector(dve, i, p):
            for h in range(2):
                dve.wait_ge(s_rl, n(i, h, p))
                dve.tensor_tensor(probs[h][:, :, :], rb(h, 1)[:, 0:TILES * E_ROUTED].rearrange("p (t e) -> p t e", t=TILES),
                                  rows[:, None, R_RB:R_RB + E_ROUTED].to_broadcast([P, TILES, E_ROUTED]),
                                  ALU.add).then_inc(s_rlb, 1)

        def route_rank_vector(dve, i, p):
            for h in range(2):
                dve.wait_ge(s_pr, n(i, h, p))
                pj = probs[h][:, :, None, :].to_broadcast([P, TILES, E_ROUTED, E_ROUTED])
                pe_ = probs[h][:, :, :, None].to_broadcast([P, TILES, E_ROUTED, E_ROUTED])
                dve.tensor_tensor(gt[h][:, :, :, :], pj, pe_, ALU.is_gt)
                dve.tensor_tensor(eq[h][:, :, :, :], pj, pe_, ALU.is_equal).then_inc(s_cmp, 1)
            for h in range(2):
                dve.wait_ge(s_cmp, n(i, h, p))
                dve.tensor_tensor(eq[h][:, :, :, :], eq[h][:, :, :, :],
                                  lower[:, None, :, :].to_broadcast([P, TILES, E_ROUTED, E_ROUTED]),
                                  ALU.mult).then_inc(s_cml, 1)
            for h in range(2):
                dve.wait_ge(s_cml, n(i, h, p))
                dve.tensor_tensor(gt[h][:, :, :, :], gt[h][:, :, :, :], eq[h][:, :, :, :], ALU.add).then_inc(s_cms, 1)
            for h in range(2):
                dve.wait_ge(s_cms, n(i, h, p))
                dve.tensor_reduce(rank[h][:, :, :], gt[h][:, :, :, :], AX.X, ALU.add).then_inc(s_rank, 1)
            for h in range(2):
                dve.wait_ge(s_rank, n(i, h, p))
                for r in range(TOP_K):
                    dve.tensor_scalar(first2[h][:, r, :, :], rank[h][:, :, :], float(r), None, ALU.is_equal)
                dve.tensor_scalar(chosen[h][:, :, :], rank[h][:, :, :], float(TOP_K), None, ALU.is_lt).then_inc(s_first2, 1)

        def route_rows_vector(dve, i, p):
            for h in range(2):
                dve.wait_ge(s_pref, n(i, h, p))
                dve.wait_ge(s_slot, 2 * i + (h + 1 + (GROUPS + 1) * p))
                pref = rb(h, 1)[:, 0:(TILES + 1) * E_ROUTED].rearrange("p (t e) -> p t e", e=E_ROUTED)
                dve.tensor_tensor(slot[h][:, :, :], pref[:, 0:TILES, :],
                                  carry[h][:, None, :].to_broadcast([P, TILES, E_ROUTED]), ALU.add)
                dve.tensor_tensor(carry[1 - h][:, :], carry[h][:, :], pref[:, TILES, :], ALU.add).then_inc(s_slot, 1)
            for h in range(2):
                dve.wait_ge(s_slot, 2 * i + (h + 2 + (GROUPS + 1) * p))
                bc = [P, TOP_K, TILES, E_ROUTED]
                dve.tensor_tensor(slotf[h][:, :, :, :], first2[h][:, :, :, :], slot[h][:, None, :, :].to_broadcast(bc), ALU.mult)
                for r in range(TOP_K):
                    m = dve.scalar_tensor_tensor(out=scoref[h][:, r, :, :], in0=first2[h][:, r, :, :], scalar=0.5,
                                                 in1=probs[h][:, :, :], op0=ALU.mult, op1=ALU.mult)
                m.then_inc(s_prod, 1)
            for h in range(2):
                dve.wait_ge(s_prod, n(i, h, p))
                dve.wait_ge(s_xn2, n(i, h, p))
                dve.tensor_reduce(sidx[h][:, :], slotf[h][:, :, :, :].rearrange("p r t e -> p (r t) e"), AX.X, ALU.add)
                dve.tensor_reduce(score[:, i, h, :], scoref[h][:, :, :, :].rearrange("p r t e -> p (r t) e"),
                                  AX.X, ALU.add).then_inc(s_idx, 1)

        def shared_hidden_vector(dve, i, p, j):
            for h in range(2):
                dve.wait_ge(s_silu, 2 * IJ * i + (2 * j + h + 1 + GROUPS * IJ * p))
                dve.wait_ge(s_su, 2 * IJ * i + (2 * j + h + 1 + GROUPS * IJ * p))
                dve.tensor_tensor(hid[h][:, j, :], gate[h][:, j, :], rb(h, 1 - j)[:, :], ALU.mult).then_inc(s_sh, 1)

        def shared_add_vector(dve, i, p):
            for h in range(2):
                dve.wait_ge(s_sd, n(i, h, p))
                dve.scalar_tensor_tensor(out=x[:, i, h, :], in0=rb(h, 1)[:, :], scalar=0.5, in1=x[:, i, h, :],
                                         op0=ALU.mult, op1=ALU.add).then_inc(s_xsh, 1)

        def route_gpsimd(pool, i, p):
            for h in range(2):
                pool.wait_ge(s_idx, n(i, h, p))
                pool.wait_ge(s_xn2, n(i, h, p))
                pool.sem_inc(s_carry, 1)
                for r in range(TOP_K):
                    for t in range(TILES):
                        k = r * TILES + t
                        pool.indirect_dma_start(out=rows_by_expert, out_offset=bass.IndirectOffsetOnAxis(
                            ap=sidx[h][:, k:k + 1], axis=0), in_=(xn, xn2)[r][h][:, t, :], in_offset=None).then_inc(s_scat[h], 16)

        def route_logits_tensor(pe, i, p):
            xt_tensor(pe, i, 1, 1 + p, rn, p, lambda h: rb(h, 0))
            for h in range(2):
                pe.wait_ge(s_xt[1], n(i, h, p))
                tile_mm(pe, rb(h, 1), xt[h], w_r[:, :], E_ROUTED).then_inc(s_rl, 1)

        def shared_gate_tensor(pe, i, p, j, halves_of=(0, 1)):
            for h in halves_of:
                if j:
                    pe.wait_ge(s_silu, 2 * IJ * i + (2 * (j - 1) + h + 1 + GROUPS * IJ * p))
                pe.matmul(rb(h, 0)[:, :], e_gu[:, SHARED, 0, j * P:(j + 1) * P], xt[h][:, :],
                          start=True, stop=True).then_inc(s_sg, 1)

        def shared_up_tensor(pe, i, p, j, halves_of=(0, 1)):
            for h in halves_of:
                if j:
                    pe.wait_ge(s_silu, 2 * IJ * i + (2 * (IJ - 1) + h + 1 + GROUPS * IJ * p))
                else:
                    pe.wait_ge(s_slot, 2 * i + (h + 2 + (GROUPS + 1) * p))
                pe.matmul(rb(h, 1 - j)[:, :], e_gu[:, SHARED, 1, j * P:(j + 1) * P], xt[h][:, :],
                          start=True, stop=True).then_inc(s_su, 1)

        def route_counts_tensor(pe, i, p):
            for h in range(2):
                pe.wait_ge(s_first2, n(i, h, p))
                for t in range(TILES + 1):
                    dst = rb(h, 1)[:, t * E_ROUTED:(t + 1) * E_ROUTED]
                    for u in range(t):
                        m = pe.matmul(dst, ones_bf[:, :], chosen[h][:, u, :], start=(u == 0), stop=(u == t - 1 and t == TILES))
                    if t < TILES:
                        pe.matmul(dst, before_bf[:, :], chosen[h][:, t, :], start=(t == 0), stop=True)
                m.then_inc(s_pref, 1)

        def shared_down_tensor(pe, i, p, halves_of=(0, 1), tiles=range(TILES)):
            for h in halves_of:
                if tiles[0] == 0:
                    pe.wait_ge(s_sh, 2 * IJ * i + (2 * (IJ - 1) + h + 1 + GROUPS * IJ * p))
                for t in tiles:
                    for j in range(IJ):
                        m = pe.matmul(rb(h, 1)[:, t * P:(t + 1) * P], hid[h][:, j, t * P:(t + 1) * P],
                                      e_dn[:, SHARED, j, :], start=(j == 0), stop=(j == IJ - 1))
                if tiles[-1] == TILES - 1:
                    m.then_inc(s_sd, 1)

        def route_scalar(act, i, p):
            xt_scalar(act, i, 1, p, [xt[h][:, :] for h in range(2)], lambda h: rb(h, 0))
            for h in range(2):
                act.wait_ge(s_rlb, n(i, h, p))
                act.activation(probs[h][:, :, :], probs[h][:, :, :], ACT.Sigmoid).then_inc(s_pr, 1)

        def route_rows_scalar(act, i, p):
            for h in range(2):
                act.wait_ge(s_xn[1], n(i, h, 1 + p))
                if not (isinstance(i, int) and i == 0 and p == 0):
                    act.wait_ge(s_scat[h], SCAT * i + SCAT * PAIRS * p)
                for r, rows_of in enumerate((xn, xn2)):
                    act.activation(rows_of[h][:, :, 0:D], rn[h], ACT.Copy)
                    m = act.activation(rows_of[h][:, :, D], result_rows[:, r, i, h, :], ACT.Copy)
                m.then_inc(s_xn2, 1)

        def shared_scalar(act, i, p, j):
            for h in range(2):
                act.wait_ge(s_sg, 2 * IJ * i + (2 * j + h + 1 + GROUPS * IJ * p))
                act.activation(gate[h][:, j, :], rb(h, 0)[:, :], ACT.Silu).then_inc(s_silu, 1)

        TAB = 9

        def tables_vector(dve, p):
            k = [TAB * p]

            def done(ins):
                k[0] += 1
                ins.then_inc(s_tab, 1)
                dve.wait_ge(s_tab, k[0])

            def over_e(a, w):
                return a[:, None, :].to_broadcast([P, w, E_ROUTED])

            dve.wait_ge(s_slot, (GROUPS + 1) * (p + 1))
            done(dve.tensor_tensor(cnt[:, :], carry[0][:, :], region, ALU.subtract))
            dve.tensor_tensor(padidx[:, :], cnt[:, :], consts[:, K_PAD:K_PAD + E_ROUTED], ALU.add)
            done(dve.tensor_scalar(tl[:, 0, :], cnt[:, :], 1.0 / P, (P / 2 - 0.5) / P, ALU.mult, ALU.add))
            done(dve.tensor_scalar(tl[:, 1, :], tl[:, 0, :], MAGIC, None, ALU.add))
            done(dve.tensor_scalar(tiles_e[:, :], tl[:, 1, :], -MAGIC, None, ALU.add))
            done(dve.tensor_tensor_scan(cum[:, :], ones8[:, :], tiles_e[:, :], 0.0, ALU.mult, ALU.add))
            done(dve.tensor_tensor(cmp[:, :, :], consts[:, K_J:K_J + NT, None].to_broadcast([P, NT, E_ROUTED]),
                                   over_e(cum, NT), ALU.is_ge))
            dve.tensor_tensor(cmpt[:, :, :], cmp[:, :, :], over_e(tiles_e, NT), ALU.mult)
            dve.tensor_reduce(etab[:, :, :].rearrange("p a b -> p (a b)"), cmp[:, :, :], AX.X, ALU.add)
            done(dve.tensor_reduce(etabf[:, :], cmp[:, :, :], AX.X, ALU.add))
            dve.tensor_reduce(stab[:, :], cmpt[:, :, :], AX.X, ALU.add)
            done(dve.scalar_tensor_tensor(out=rtabf[:, :], in0=etabf[:, :], scalar=float(REGION),
                                          in1=consts[:, K_J128:K_J128 + NT], op0=ALU.mult, op1=ALU.add))
            done(dve.scalar_tensor_tensor(out=rtab[:, :, :].rearrange("p a b -> p (a b)"), in0=stab[:, :], scalar=-float(P),
                                          in1=rtabf[:, :], op0=ALU.mult, op1=ALU.add))

        away = consts[:, K_AWAY:]

        def padding_rows(pool, n):
            if n == 1:
                pool.wait_ge(s_zfill, 16 * E_ROUTED)
            for e in range(E_ROUTED):
                pool.memset(tin[e][:, 0:D], 0.0)
            for e in range(E_ROUTED):
                k = (E_ROUTED if n == 0 else 0) + e
                m = pool.tensor_tensor(tin[e][:, D:ROW], away[:, k:k + 1], zero_col[:, :], ALU.add)
            m.then_inc(s_padding, 1)

        def pad_sync(sp_, p):
            sp_.wait_ge(s_tab, TAB * p + 2)
            sp_.wait_ge(s_padding, p + 2)
            for e in range(E_ROUTED):
                row = sp_.value_load(padidx[0:1, e:e + 1], min_val=0, max_val=E_ROUTED * REGION - P)
                sp_.dma_start(rows_by_expert[bass.ds(row, P), :], tin[e][:, :]).then_inc(s_pad, 16)

        LAG_ST = 3
        AHEAD = {"s_thid": 1, "s_tyc": LAG_ST, "s_tsil": 1, "s_tdn": 2}

        def lag(i, k, d):
            b, kk = (i, k - d) if k >= d else (i - 1, k - d + BLK)
            if isinstance(i, int) and not 0 <= b < NB:
                return None
            return b, kk

        def step_value(eng, i, k, c):
            v = i * BLK + (k + c)
            return v if isinstance(v, int) else eng.snap(v)

        def over_blocks(eng, block_of):
            block_of(0)
            with eng.Fori(1, NB) as i:
                block_of(i)
            block_of(NB)

        def stages(i, k, *lagged):
            for d, stage in lagged:
                where = lag(i, k, d)
                if where:
                    stage(*where)

        def experts_sync(sp_, p):
            pad_sync(sp_, p)
            sp_.wait_ge(s_scat[0], SCAT * PAIRS * (p + 1))
            sp_.wait_ge(s_scat[1], SCAT * PAIRS * (p + 1))
            sp_.wait_ge(s_pad, 16 * E_ROUTED * (p + 1))
            sp_.wait_ge(s_tab, TAB * (p + 1))

            def block_of(i):
                for k in range(BLK):
                    if isinstance(i, int) and i >= NB:
                        continue
                    row = sp_.value_load(rtab[0:1, i, k:k + 1], min_val=0, max_val=E_ROUTED * REGION + (E_ROUTED - 1) * P)
                    if not (isinstance(i, int) and i == 0 and p == 0):
                        sp_.wait_ge(s_tdst, i * BLK + (k + 1 - BLK + NT * p))
                    sp_.dma_start(tin[k][:, :], rows_by_expert[bass.ds(row, P), :]).then_inc(s_in[k], 16)

            over_blocks(sp_, block_of)

        def experts_tensor(pe, p):
            pe.wait_ge(s_tab, TAB * (p + 1))
            pe.wait_ge(s_xsh, GROUPS * (p + 1))

            def block_of(i):
                loaded = i * 16 + 16 * (1 + NB * p)
                loaded = loaded if isinstance(i, int) else pe.snap(loaded)
                experts = {}

                def expert(b, k):
                    if (b is i, k) not in experts:
                        experts[b is i, k] = pe.value_load(etab[0:1, b, k:k + 1], min_val=0, max_val=E_ROUTED)
                    return experts[b is i, k]

                for k in range(BLK):
                    v = step_value(pe, i, k, NT * p)

                    def transpose_in(b, kk):
                        pe.wait_ge(s_in[kk], loaded)
                        pe.transpose(bank[2 + kk % 2][:, 0:P], tin[kk][:, 0:D], ident).then_inc(s_tt, 1)

                    def up(b, kk):
                        pe.wait_ge(s_twt, v)
                        pe.wait_ge(s_ttc, v)
                        for c in range(2 * IJ):
                            m = pe.matmul(bank[kk % 2][:, c * P:(c + 1) * P], twt[kk % 2][:, c * P:(c + 1) * P],
                                          tint[kk % 2][:, :], start=True, stop=True)
                        m.then_inc(s_tgu, 1)

                    def down(b, kk):
                        e = expert(b, kk)
                        pe.wait_ge(s_thid, v)
                        if isinstance(i, int) and i == NB:
                            pe.wait_ge(s_tyc, b * BLK + kk + NT * p - 1 + AHEAD["s_tyc"])
                        for j in range(IJ):
                            m = pe.matmul(bank[6 + kk % 2][:, 0:P], thidt[kk % 2][:, j, :], e_dn[:, e, j, :],
                                          start=(j == 0), stop=(j == IJ - 1))
                        m.then_inc(s_tdn, 1)

                    stages(i, k, (0, transpose_in), (1, up), (2, down))

            over_blocks(pe, block_of)

        def experts_scalar(act, p):
            act.wait_ge(s_tab, TAB * (p + 1))
            act.wait_ge(s_load2, 48)
            act.wait_ge(s_sh, GROUPS * IJ * (p + 1))

            def block_of(i):
                for k in range(BLK):
                    v = step_value(act, i, k, NT * p)

                    def weights(b, kk):
                        e = act.value_load(etab[0:1, b, kk:kk + 1], min_val=0, max_val=E_ROUTED)
                        act.activation(twt[kk % 2], e_gu[:, e, :, :].rearrange("p a n -> p (a n)"),
                                       ACT.Copy).then_inc(s_twt, 1)

                    def silu(b, kk):
                        act.wait_ge(s_tgu, v)
                        act.activation(tsil[kk % 2][:, :], bank[kk % 2][:, 0:INNER], ACT.Silu).then_inc(s_tsil, 1)

                    stages(i, k, (0, weights), (1, silu))

            over_blocks(act, block_of)

        def experts_gpsimd(pool, p):
            def block_of(i):
                for k in range(BLK):
                    v = step_value(pool, i, k, NT * p + 1)

                    def store(b, kk):
                        pool.wait_ge(s_tyc, v)
                        pool.sem_inc(s_carry, 1)
                        pool.indirect_dma_start(out=rows_done, out_offset=bass.IndirectOffsetOnAxis(
                            ap=tdst[kk][:, 0:1], axis=0), in_=tout[kk % OUT_RING][:, :], in_offset=None
                            ).then_inc(s_st[kk % OUT_RING], 16)

                    stages(i, k, (LAG_ST, store))

            over_blocks(pool, block_of)

        def experts_vector(dve, p):
            def block_of(i):
                for k in range(BLK):
                    v = step_value(dve, i, k, NT * p + 1)

                    def copy_in(b, kk):
                        dve.wait_ge(s_tt, v)
                        dve.tensor_copy(tdst[kk][:, :], tin[kk][:, D:ROW]).then_inc(s_tdst, 1)
                        dve.tensor_copy(tint[kk % 2][:, :], bank[2 + kk % 2][:, 0:P]).then_inc(s_ttc, 1)

                    def hidden(b, kk):
                        dve.wait_ge(s_tsil, v)
                        dve.tensor_tensor(thidt[kk % 2][:, :, :].rearrange("p j c -> p (j c)"), tsil[kk % 2][:, :],
                                          bank[kk % 2][:, INNER:2 * INNER], ALU.mult).then_inc(s_thid, 1)

                    def copy_out(b, kk):
                        dve.wait_ge(s_tdn, v)
                        turns = BLK // OUT_RING
                        if not (isinstance(b, int) and b == 0 and p == 0 and kk < OUT_RING):
                            dve.wait_ge(s_st[kk % OUT_RING], b * (16 * turns) + 16 * (kk // OUT_RING + turns * NB * p))
                        dve.tensor_copy(tout[kk % OUT_RING][:, :], bank[6 + kk % 2][:, 0:P]).then_inc(s_tyc, 1)

                    stages(i, k, (0, copy_in), (1, hidden), (2, copy_out))

            over_blocks(dve, block_of)

        def stored(eng, p):
            for k in range(OUT_RING):
                eng.wait_ge(s_st[k], 16 * (NT // OUT_RING) * (p + 1))

        def fetch_sync(sp_, i, p, after=None):
            for h in range(2):
                if after is not None:
                    sp_.wait_ge(s_add1, n(after, h, p))
                for r in range(TOP_K):
                    src = rows_done[r * TOKENS:(r + 1) * TOKENS, :].rearrange("(a h t p) d -> p a h t d", h=2, t=TILES, p=P)
                    sp_.dma_start(got[h][:, r * TILES:(r + 1) * TILES, :], src[:, i, h, :, :]).then_inc(s_got[h], 16)

        def combine_vector(dve, i, p):
            for h in range(2):
                for r in range(TOP_K):
                    if r == 0:
                        dve.wait_ge(s_got[h], 16 * TOP_K * (i + (1 + PAIRS * p)))
                    else:
                        dve.wait_ge(s_add0, n(i, h, p))
                    for t in range(TILES):
                        k = r * TILES + t
                        m = dve.scalar_tensor_tensor(out=xg(i, h)[:, t, :], in0=got[h][:, k, :], scalar=score[:, i, h, k:k + 1],
                                                     in1=xg(i, h)[:, t, :], op0=ALU.mult, op1=ALU.add)
                    m.then_inc(s_add1 if r else s_add0, 1)

        COPIES = LEVELS + 1

        def halves(buf, w):
            return buf[:, :].rearrange("p (b two r) -> p b two r", two=2, r=w)

        def gla_gates_vector(dve, i):
            for h in range(2):
                dve.wait_ge(s_v, n(i, h))
                dve.tensor_tensor(bufC[h][:, :].rearrange("p (t d) -> p t d", t=TILES),
                                  gb(h, 0)[:, :].rearrange("p (t d) -> p t d", t=TILES),
                                  rows[:, None, R_BV:R_BV + P].to_broadcast([P, TILES, P]), ALU.add).then_inc(s_vb, 1)
            for h in range(2):
                dve.wait_ge(s_qk, n(i, h))
                dve.tensor_tensor(bufA[h][:, :], bufD[h][:, :], tseg[h][:, :], ALU.mult).then_inc(s_q0, 1)

        def gla_level_vector(dve, i, lv):
            w = 1 << lv
            for h in range(2):
                dve.wait_ge(s_lvl, i * (2 * LEVELS) + (2 * lv + h + 1))
                if lv:
                    dve.wait_ge(s_upd, i * (2 * LEVELS) + (2 * (lv - 1) + h + 1))
                    dve.wait_ge(s_pred, i * (2 * COPIES) + (2 * (lv - 1) + h + 1))
                else:
                    dve.wait_ge(s_dg, n(i, h))
                cur, nxt = (tseg[h], tseg2[h]) if lv % 2 == 0 else (tseg2[h], tseg[h])
                seg = cur[:, 0:GROUP // w].rearrange("p (b two) -> p b two", two=2)
                nb = GROUP // (2 * w)
                dve.tensor_tensor(halves(bufA[h], w)[:, :, 1, :], halves(bufA[h], w)[:, :, 1, :],
                                  seg[:, :, 0:1].to_broadcast([P, nb, w]), ALU.mult)
                m = dve.tensor_tensor(halves(bufB[h], w)[:, :, 0, :], halves(bufB[h], w)[:, :, 0, :],
                                      seg[:, :, 1:2].to_broadcast([P, nb, w]), ALU.mult)
                if lv < LEVELS - 1:
                    m = dve.tensor_tensor(nxt[:, 0:nb], seg[:, :, 0], seg[:, :, 1], ALU.mult)
                m.then_inc(s_upd, 1)
                if lv == 0:
                    m = dve.copy_predicated(at[h][:, :], masks[:, (LEVELS - 1) * 256:], gb(h, 1)[:, :])
                else:
                    m = dve.copy_predicated(
                        halves(at[h], w // 2)[:, :, 1, :],
                        masks[:, (lv - 1) * 256:lv * 256].rearrange("p (b r) -> p b r", r=w // 2),
                        gb(h, (lv - 1) % 2)[:, 0:256].rearrange("p (b r) -> p b r", r=w // 2))
                m.then_inc(s_pred, 1)

        def gla_last_vector(dve, i):
            for h in range(2):
                dve.wait_ge(s_pred, i * (2 * COPIES) + (2 * (LEVELS - 1) + h + 1))
                dve.tensor_copy(halves(at[h], P // 2)[0:P // 2, :, 1, :],
                                gb(h, (LEVELS - 1) % 2)[0:P // 2, 0:256].rearrange("p (c r) -> p c r", c=TILES)
                                ).then_inc(s_pred, 1)

        def gla_add_vector(dve, i):
            for h in range(2):
                dve.wait_ge(s_op, n(i, h))
                dve.wait_ge(s_xbo, n(i, h))
                dve.tensor_tensor(x[:, i, h, :], x[:, i, h, :], gb(h, 1)[:, :], ALU.add).then_inc(s_x, 1)

        def gla_gpsimd(pool, i):
            for h in range(2):
                pool.wait_ge(s_xn[0], n(i, h, 2))
                pool.tensor_tensor(xg(i, h), xg(i, h), rows[:, None, R_BO:R_BO + P].to_broadcast([P, TILES, P]),
                                   ALU.add).then_inc(s_xbo, 1)

        def gla_in_tensor(pe, i):
            xt_tensor(pe, i, 0, 2, tt, 0, lambda h: gb(h, 0))
            for h in range(2):
                pe.wait_ge(s_xt[0], n(i, h))
                if not (isinstance(i, int) and i == 0):
                    pe.wait_ge(s_x, n(i, h) - 2)
                pe.matmul(gb(h, 1)[:, :], a_sq[:, 0, :], gxt[h], start=True, stop=True)
                pe.matmul(gb(h, 0)[:, :], a_sq[:, 1, :], gxt[h], start=True, stop=True).then_inc(s_qkp, 1)

        def gla_in2_tensor(pe, i):
            for h in range(2):
                pe.wait_ge(s_qkc, n(i, h))
                pe.matmul(gb(h, 1)[:, :], a_sq[:, 3, :], gxt[h], start=True, stop=True).then_inc(s_gp, 1)
                for t in range(TILES):
                    m = pe.matmul(gb(h, 0)[:, t * P:(t + 1) * P], gxt[h][:, t * P:(t + 1) * P], a_sq[:, 2, :],
                                  start=True, stop=True)
                m.then_inc(s_v, 1)

        def gla_diagonal_tensor(pe, i):
            for h in range(2):
                pe.wait_ge(s_qk, n(i, h))
                for c in range(TILES):
                    m = pe.matmul(gb(h, 1)[:, c * P:(c + 1) * P], bufB[h][:, c * P:(c + 1) * P],
                                  bufD[h][:, c * P:(c + 1) * P], start=True, stop=True)
                m.then_inc(s_dg, 1)

        def gla_level_tensor(pe, i, lv, halves_of=(0, 1)):
            w = 1 << lv
            for h in halves_of:
                if lv:
                    pe.wait_ge(s_upd, i * (2 * LEVELS) + (2 * (lv - 1) + h + 1))
                    pe.wait_ge(s_pred, i * (2 * COPIES) + (2 * (lv - 1) + h + 1))
                else:
                    pe.wait_ge(s_q0, n(i, h))
                qv = bufA[h][:, :].rearrange("p (c b two r) -> p c b two r", c=TILES, two=2, r=w)
                for c in range(TILES):
                    m = pe.matmul(gb(h, lv % 2)[:, c * 64:(c + 1) * 64], bufB[h][:, c * P:(c + 1) * P],
                                  qv[:, c, :, 1, :], start=True, stop=True)
                m.then_inc(s_lvl, 1)

        def gla_out_tensor(pe, i):
            for h in range(2):
                pe.wait_ge(s_upd, i * (2 * LEVELS) + (2 * (LEVELS - 1) + h + 1))
                pe.wait_ge(s_pred, i * (2 * COPIES) + (2 * (LEVELS - 1) + h + 1))
                for b in range(SEQS):
                    m = pe.matmul(gb(h, 1)[:, b * P:(b + 1) * P], bufB[h][:, 2 * b * P:(2 * b + 1) * P],
                                  bufA[h][:, (2 * b + 1) * P:(2 * b + 2) * P], start=True, stop=True)
                m.then_inc(s_cross, 1)
            for h in range(2):
                pe.wait_ge(s_cc, n(i, h))
                pe.wait_ge(s_pred, i * (2 * COPIES) + (2 * (COPIES - 1) + h + 1))
                v = bufC[h][:, :]
                for b in range(SEQS):
                    c0, c1 = 2 * b * P, (2 * b + 1) * P
                    pe.matmul(gb(h, 0)[:, c0:c0 + P], v[:, c0:c0 + P], at[h][:, c0:c0 + P], start=True, stop=True)
                    pe.matmul(gb(h, 0)[:, c1:c1 + P], v[:, c0:c0 + P], across[h][:, b, :], start=True, stop=False)
                    m = pe.matmul(gb(h, 0)[:, c1:c1 + P], v[:, c1:c1 + P], at[h][:, c1:c1 + P], start=False, stop=True)
                m.then_inc(s_o, 1)
            for h in range(2):
                pe.wait_ge(s_oc, n(i, h))
                tile_mm(pe, gb(h, 1), bufE[h], a_sq[:, 4, :]).then_inc(s_op, 1)

        def gla_in_scalar(act, i):
            xt_scalar(act, i, 0, 0, gxt, lambda h: gb(h, 0))
            for h in range(2):
                act.wait_ge(s_qkp, n(i, h))
                act.activation(bufD[h][:, :], gb(h, 1)[:, :], ACT.Identity, bias=cols[:, BQ:BQ + 1])
                act.activation(bufB[h][:, :], gb(h, 0)[:, :], ACT.Sigmoid, bias=cols[:, BK:BK + 1]).then_inc(s_qkc, 1)

        def gla_in2_scalar(act, i):
            for h in range(2):
                act.wait_ge(s_gp, n(i, h))
                act.activation(tseg[h][:, :], gb(h, 1)[:, :], ACT.Sigmoid, bias=cols[:, BG:BG + 1]).then_inc(s_qk, 1)

        def gla_out_scalar(act, i):
            for h in range(2):
                act.wait_ge(s_cross, n(i, h))
                act.activation(across[h][:, :, :], gb(h, 1)[:, 0:SEQS * P].rearrange("p (b c) -> p b c", b=SEQS),
                               ACT.Copy).then_inc(s_cc, 1)
            for h in range(2):
                act.wait_ge(s_o, n(i, h))
                act.activation(bufE[h][:, :], gb(h, 0)[:, :], ACT.Copy).then_inc(s_oc, 1)

        def quant_route_vector(dve, q, r, e):
            when(q, quant_ln_vector, dve, 1)
            when(e, shared_hidden_vector, dve, 0, 0)
            if r is not None:
                dve.wait_ge(s_xq, n(r, 1, 1))
                dve.memset(scratch2[0][:, :], 0.0)
                ln_stats(dve, r, 1, 1)
            when(e, shared_hidden_vector, dve, 0, 1)
            when(q, ln_root_vector, dve, 0, 0)
            when(q, quant_apply_vector, dve, 1)
            when(r, ln_root_vector, dve, 1, 1)
            when(e, shared_add_vector, dve, 0)
            when(r, route_apply_vector, dve, 0)
            when(q, quant_max_vector, dve, 1)
            when(q, quant_round_vector, dve, 1)
            when(q, quant_clip_vector, dve, 1)
            when(r, route_bias_vector, dve, 0)
            when(r, route_rank_vector, dve, 0)
            when(r, route_rows_vector, dve, 0)
            when(q, quant_add_vector, dve, 1)

        def quant_route_gpsimd(pool, q, r, e):
            when(q, quant_gpsimd, pool, 1)
            when(r, route_gpsimd, pool, 0)

        def quant_route_tensor(pe, q, r, e):
            for j in range(IJ):
                when(e, shared_up_tensor, pe, 0, j)
            when(e, shared_down_tensor, pe, 0)
            when(r, route_logits_tensor, pe, 0)
            when(r, shared_gate_tensor, pe, 0, 0)
            when(q, quant_tensor, pe, 1)
            when(r, route_counts_tensor, pe, 0)
            when(r, shared_gate_tensor, pe, 0, 1)

        def quant_route_scalar(act, q, r, e):
            when(q, ln_root_scalar, act, 0, 1)
            when(r, ln_root_scalar, act, 1, 1)
            when(r, route_scalar, act, 0)
            when(q, quant_scalar, act, 1)
            when(r, route_rows_scalar, act, 0)
            for j in range(IJ):
                when(r, shared_scalar, act, 0, j)

        def over_quant_route(eng, body_of):
            body_of(eng, 1, 0, None)
            with eng.Fori(1, PAIRS - 1) as i:
                body_of(eng, i + 1, i, i - 1)
            body_of(eng, None, PAIRS - 1, PAIRS - 2)

        def gla_start_vector(dve, i):
            combine_vector(dve, i, 0)
            gla_ln_vector(dve, i)
            ln_apply(dve, i, 0, 2, tt)

        def gla_ln_vector(dve, i):
            dve.wait_ge(s_add1, n(i, 1))
            dve.memset(scratch2[1][:, :], 0.0)
            ln_stats(dve, i, 0, 2)

        def gla_apply_vector(dve, i):
            ln_root_vector(dve, i, 0, PAIRS - 1)
            ln_apply(dve, i, 0, 2, tt)

        def routed_ln_vector(dve, i):
            gla_add_vector(dve, i)
            dve.wait_ge(s_x, n(i, 1))
            dve.memset(scratch2[0][:, :], 0.0)
            ln_stats(dve, i, 1, 2)

        def gla_route_vector(dve, g, r, c):
            when(c, combine_vector, dve, 0)
            when(r, routed_ln_vector, dve)
            when(c, gla_ln_vector, dve)
            when(r, route_apply_vector, dve, 1)
            when(g, gla_gates_vector, dve)
            when(r, route_bias_vector, dve, 1)
            when(g, gla_level_vector, dve, 0)
            when(r, route_rank_vector, dve, 1)
            when(g, gla_level_vector, dve, 1)
            when(r, route_rows_vector, dve, 1)
            for lv in range(2, LEVELS):
                when(g, gla_level_vector, dve, lv)
                if lv == 3:
                    when(c, gla_apply_vector, dve)
                if lv == 4:
                    for j in range(IJ):
                        when(r, shared_hidden_vector, dve, 1, j)
            when(g, gla_last_vector, dve)
            when(r, shared_add_vector, dve, 1)

        def gla_route_gpsimd(pool, g, r, c):
            when(r, ln_gpsimd, pool, 1, 2)
            when(g, gla_gpsimd, pool)
            when(r, route_gpsimd, pool, 1)

        def gla_route_tensor(pe, g, r, c):
            when(r, gla_out_tensor, pe)
            when(g, gla_in_tensor, pe)
            when(g, gla_in2_tensor, pe)
            when(g, gla_diagonal_tensor, pe)
            when(r, route_logits_tensor, pe, 1)
            first, last = range(TILES // 2), range(TILES // 2, TILES)
            for lv in range(LEVELS):
                for h in range(2):
                    when(g, gla_level_tensor, pe, lv, (h,))
                    if lv == 0:
                        when(r, shared_gate_tensor, pe, 1, 0, (h,))
                    elif lv == 2:
                        when(r, shared_gate_tensor, pe, 1, 1, (h,))
                    elif lv in (3, 4):
                        when(r, shared_up_tensor, pe, 1, lv - 3, (h,))
                    elif (lv, h) == (5, 1):
                        when(r, shared_down_tensor, pe, 1, (0,), first)
                    elif (lv, h) == (6, 0):
                        when(r, shared_down_tensor, pe, 1, (0,), last)
                    elif (lv, h) == (6, 1):
                        when(r, shared_down_tensor, pe, 1, (1,))
                if lv == 1:
                    when(r, route_counts_tensor, pe, 1)

        def gla_route_scalar(act, g, r, c):
            when(r, gla_out_scalar, act)
            when(g, gla_in_scalar, act)
            when(g, gla_in2_scalar, act)
            when(r, route_scalar, act, 1)
            when(r, shared_scalar, act, 1, 0)
            when(r, route_rows_scalar, act, 1)
            for j in range(1, IJ):
                when(r, shared_scalar, act, 1, j)
            when(c, ln_root_scalar, act, 0, 2)

        def over_gla_route(eng, body_of):
            body_of(eng, 0, None, 1)
            with eng.Fori(0, PAIRS - 2) as i:
                body_of(eng, i + 1, i, i + 2)
            body_of(eng, PAIRS - 1, PAIRS - 2, None)
            body_of(eng, None, PAIRS - 1, None)

        @block.sync
        def _(sp_):
            sp_.dma_start(x[:, 0, :, :], x_in[:, 0, :, :]).then_inc(s_first, 16)
            for dst, src in ((cols, cols_in), (rows, rows_in), (consts, consts_in)):
                sp_.dma_start(dst[:, :], src).then_inc(s_first, 16)
            sp_.dma_start(wq_int[:, :, :], wq64.bitcast(I32).rearrange("p (n w) -> p n w", w=2)).then_inc(s_first, 16)
            for g in range(1, PAIRS):
                sp_.dma_start(x[:, g, :, :], x_in[:, g, :, :]).then_inc(s_load, 16)
            sp_.dma_start(w_sq[:, :, :], l0_sq).then_inc(s_load, 16)
            sp_.dma_start(w_gu[:, :, :], l0_gu).then_inc(s_load, 16)
            sp_.dma_start(masks_wide, masks_in).then_inc(s_load, 16)
            sp_.dma_start(w_dn[:, :, :], l0_dn).then_inc(s_load, 16)
            sp_.dma_start(w_r[:, :], moe_r).then_inc(s_load, 16)
            sp_.dma_start(a_sq[:, :, :], l1_sq).then_inc(s_load2, 16)
            sp_.dma_start(e_gu[:, :, :, :], moe_gu).then_inc(s_load2, 16)
            sp_.dma_start(e_dn[:, :, :, :], moe_dn).then_inc(s_load2, 16)
            sp_.wait_ge(s_padding, 1)
            for e in range(E_ROUTED):
                first = E_ROUTED * REGION + e * P
                sp_.dma_start(rows_by_expert[first:first + P, :], tin[e][:, :]).then_inc(s_zfill, 16)
            sp_.wait_ge(s_zfill, 16 * E_ROUTED)
            for p in range(2):
                experts_sync(sp_, p)
                stored(sp_, p)
                fetch_sync(sp_, 0, p)
                with sp_.Fori(0, PAIRS - 1) as i:
                    fetch_sync(sp_, i + 1, p, after=i)
                    if p:
                        sp_.dma_start(out[:, i, :, :], x[:, i, :, :]).then_inc(s_out, 16)
            sp_.wait_ge(s_add1, GROUPS * 2)
            sp_.dma_start(out[:, PAIRS - 1, :, :], x[:, PAIRS - 1, :, :]).then_inc(s_out, 16)
            sp_.wait_ge(s_out, 16 * PAIRS)

        @block.vector
        def _(dve):
            dve.sem_inc(s_thid, AHEAD["s_thid"])
            dve.sem_inc(s_tyc, AHEAD["s_tyc"])
            dve.sem_inc(s_xl, XL_AHEAD)
            for h in range(2):
                dve.memset(at[h][:, :], 0.0)
                dve.memset(xp[h][:, :, 0:PAD], 0.0)
            dve.wait_ge(s_first, 16 * FIRST)
            dve.tensor_copy(wq[:, :], wq_int[:, :, 0])
            dve.tensor_copy(ident_bf[:, :], ident)
            for t in range(TILES):
                dve.tensor_scalar(half_ws[:, t, :], rows[:, R_WS:R_WS + P], 0.5, None, ALU.mult)
                dve.tensor_scalar(half_qb[:, t, :], rows[:, R_QB:R_QB + P], 0.5, None, ALU.mult)
            dve.tensor_copy(before_bf[:, :], consts[:, K_BEFORE:K_BEFORE + P]).then_inc(s_const, 1)
            dve.wait_ge(s_const, 1)
            quant_l0_vector(dve, 0, None, None)
            dve.wait_ge(s_load, 16 * LOADS)
            dve.tensor_scalar(wx_n[:, :, :], w_sq[:, 0:2, :], cols[:, N1W:N1W + 1], None, ALU.mult)
            dve.tensor_copy(masks[:, :], masks_wide)
            dve.tensor_scalar(wgu_n[:, :, :], w_gu[:, :, :], cols[:, N2W:N2W + 1], None, ALU.mult).then_inc(s_const, 1)
            dve.wait_ge(s_act_const, 1)
            dve.tensor_scalar(sp[:, 3:4], cols[:, LAM:LAM + 1], 0.0, sp[:, 2:3], ALU.max, ALU.add).then_inc(s_const, 1)
            dve.wait_ge(s_const, 3)
            dve.tensor_scalar(decay[:, :], sp[:, 3:4], -C_CONST, None, ALU.mult).then_inc(s_const, 1)
            in_three_steps(dve, quant_l0_vector)
            ffn_quant_vector(dve, PAIRS - 1, 0)
            dve.tensor_copy(carry[0][:, :], region).then_inc(s_slot, 1)
            over_quant_route(dve, quant_route_vector)
            tables_vector(dve, 0)
            quant_route_vector(dve, None, None, PAIRS - 1)
            experts_vector(dve, 0)
            dve.wait_ge(s_tab, TAB)
            dve.tensor_copy(carry[0][:, :], region).then_inc(s_slot, 1)
            gla_start_vector(dve, 0)
            over_gla_route(dve, gla_route_vector)
            tables_vector(dve, 1)
            experts_vector(dve, 1)
            with dve.Fori(0, PAIRS) as i:
                combine_vector(dve, i, 1)

        @block.gpsimd
        def _(pool):
            pool.memset(zero_col[:, :], 0.0).then_inc(s_zero, 1)
            pool.memset(ones8[:, :], 1.0)
            pool.memset(ones_bf[:, :], 1.0)
            pool.memset(rms_eps[:, :], RMS_EPS)
            pool.memset(neg_half[:, :], -0.5).then_inc(s_pool_const, 1)
            pool.wait_ge(s_pool_const, 1)
            pool.wait_ge(s_const, 1)
            quant_l0_gpsimd(pool, 0, None, None)
            padding_rows(pool, 0)
            in_three_steps(pool, quant_l0_gpsimd)
            ffn_quant_gpsimd(pool, PAIRS - 1, 0)
            padding_rows(pool, 1)
            over_quant_route(pool, quant_route_gpsimd)
            experts_gpsimd(pool, 0)
            padding_rows(pool, 2)
            ln_gpsimd(pool, 0, 0, 2)
            over_gla_route(pool, gla_route_gpsimd)
            experts_gpsimd(pool, 1)

        @block.tensor
        def _(pe):
            pe.sem_inc(s_tdn, AHEAD["s_tdn"])
            pe.wait_ge(s_const, 1)
            quant_l0_tensor(pe, 0, None, None)
            pe.wait_ge(s_const, 2)
            in_three_steps(pe, quant_l0_tensor)
            ffn_quant_tensor(pe, PAIRS - 1, 0)
            pe.wait_ge(s_load2, 48)
            over_quant_route(pe, quant_route_tensor)
            quant_route_tensor(pe, None, None, PAIRS - 1)
            experts_tensor(pe, 0)
            over_gla_route(pe, gla_route_tensor)
            experts_tensor(pe, 1)

        @block.scalar
        def _(act):
            act.sem_inc(s_tsil, AHEAD["s_tsil"])
            act.wait_ge(s_first, 16 * FIRST)
            act.activation(sp[:, 0:1], cols[:, LAM:LAM + 1], ACT.Abs).then_inc(s_act_sp, 1)
            act.wait_ge(s_act_sp, 1)
            act.activation(sp[:, 1:2], sp[:, 0:1], ACT.Exp, scale=-1.0).then_inc(s_act_sp, 1)
            act.wait_ge(s_act_sp, 2)
            act.activation(sp[:, 2:3], sp[:, 1:2], ACT.Ln, bias=1.0).then_inc(s_act_const, 1)
            quant_l0_scalar(act, 0, None, None)
            act.wait_ge(s_const, 4)
            in_three_steps(act, quant_l0_scalar)
            ffn_quant_scalar(act, PAIRS - 1, 0)
            over_quant_route(act, quant_route_scalar)
            experts_scalar(act, 0)
            over_gla_route(act, gla_route_scalar)
            experts_scalar(act, 1)


def kernel(**inputs):
    import numpy as np
    import concourse.bacc as bacc
    from concourse.bass_utils import run_bass_kernel_spmd as run

    v = {k: np.asarray(a) for k, a in inputs.items()}
    c = np.ascontiguousarray

    def across(*vectors):
        return c(np.broadcast_to(np.concatenate(vectors)[None, :], (P, sum(len(a) for a in vectors))))

    def tokens(a):
        return a.reshape(PAIRS, 2, TILES, P, D).transpose(3, 0, 1, 2, 4).reshape(P, PAIRS, 2, GROUP)

    gate_up = np.stack([np.concatenate([v["L1_ffn_Wg"], v["L1_ffn_Wg_s"][None]]),
                        np.concatenate([v["L1_ffn_Wu"], v["L1_ffn_Wu_s"][None]])], axis=1)
    down = np.concatenate([v["L1_ffn_Wd"], v["L1_ffn_Wd_s"][None]])

    row = np.arange(P)[:, None]
    levels = []
    for lv in range(LEVELS - 1):
        w = 1 << lv
        col = np.arange(64)[None, :] // w
        levels.append(np.tile((row // w == 2 * col), (1, TILES)))
    levels.append(np.tile(row == np.arange(P)[None, :], (1, TILES)))
    masks = np.concatenate(levels, axis=1).astype(np.int32)
    ee = np.arange(E_ROUTED)
    region = np.tile(ee * REGION, (P, 1))
    consts = np.concatenate([np.eye(P), row < np.arange(P)[None, :],
                             np.tile((ee[None, :] < ee[:, None]).reshape(1, -1), (P, 1)),
                             region, region + row, np.tile(np.arange(NT), (P, 1)),
                             np.tile(np.arange(NT) * P, (P, 1)),
                             np.arange(TOP_K * TOKENS).reshape(TOP_K * TOKENS // P, P).T,
                             TOP_K * TOKENS + np.arange(2 * E_ROUTED) * P + row], axis=1).astype(np.float32)

    arrays = {
        "x_in": tokens(v["L0_attn_x"].reshape(TOKENS, D)),
        "wq64": v["L0_ffn_weight_q"].T.astype(np.int64),
        "cols_in": np.stack([v["L0_attn_norm1_w"], *v["L0_attn_conv_w"], v["L0_attn_conv_b"], v["L0_attn_lam"],
                             v["L0_attn_norm2_w"], v["L1_attn_bq"], v["L1_attn_bk"], v["L1_attn_bg"]], axis=1),
        "rows_in": across(v["L0_ffn_weight_scale"], v["L0_ffn_bias"], v["L1_attn_bv"], v["L1_attn_bo"], v["L1_ffn_rb"]),
        "l0_sq": np.stack([v["L0_attn_" + k] for k in ("Wx", "Wy", "Wi", "Wa", "Wo")], axis=1),
        "l0_gu": np.stack([v["L0_attn_Wg"], v["L0_attn_Wu"]], axis=1),
        "l0_dn": v["L0_attn_Wd"].reshape(HJ, P, D).transpose(1, 0, 2),
        "l1_sq": np.stack([v["L1_attn_" + k] for k in ("Wq", "Wk", "Wv", "Wg", "Wo")], axis=1),
        "moe_gu": gate_up.transpose(3, 0, 1, 2),
        "moe_dn": down.transpose(2, 0, 1).reshape(IJ, P, E_ALL, D).transpose(1, 2, 0, 3),
        "moe_r": v["L1_ffn_Wr"].T,
        "consts_in": consts,
        "masks_in": masks,
    }
    nc = bacc.Bacc("TRN2", target_bir_lowering=False, num_devices=1)
    args, feed = [], {}
    for name, a in arrays.items():
        feed[name] = c(a)
        args.append(nc.dram_tensor(name, a.shape, mybir.dt.from_np(a.dtype), kind="ExternalInput").ap())
    args.append(nc.dram_tensor("rows_by_expert", ((E_ROUTED + 1) * REGION, ROW), F32, kind="Internal").ap())
    args.append(nc.dram_tensor("rows_done", (TOP_K * TOKENS + 2 * E_ROUTED * P, D), F32, kind="Internal").ap())
    args.append(nc.dram_tensor("out", (P, PAIRS, 2, GROUP), F32, kind="ExternalOutput").ap())
    macaron_kernel(nc, *args)
    r = run(nc, [feed], core_ids=[0])
    got = r.results[0]["out"]
    return c(got.reshape(P, PAIRS, 2, TILES, D).transpose(1, 2, 3, 0, 4).reshape(B, S, D))
```
